# Optimizing a Trainium2 kernel written in Bass

```python
import numpy as np
import jax
import jax.numpy as jnp

def _softmax(x, axis=-1):
    return jax.nn.softmax(x, axis=axis)

def _gelu(x):
    return jax.nn.gelu(x, approximate=True)

def _silu(x):
    return jax.nn.silu(x)

def _sigmoid(x):
    return jax.nn.sigmoid(x)

def _layernorm(x, axis=-1, eps=1e-05):
    m = jnp.mean(x, axis=axis, keepdims=True)
    v = jnp.var(x, axis=axis, keepdims=True)
    return (x - m) / jnp.sqrt(v + eps)

def _scatter_add(tgt, idx, src, axis=0):
    return tgt.at[idx].add(src)

def _segment_sum(src, seg, n):
    return jax.ops.segment_sum(src, seg, n)
kernel_name = 'mk_audio_tower_d1_tok_audfeat512_r4_fbafb2'

def setup_inputs(seed: int=0):
    np.random.seed(seed)
    _w = jnp.asarray

    def _rec_inputs():
        import jax
        import jax.numpy as jnp
        _rk = jax.random.key(seed)
        x = 7.22013e-05 + 1.00017 * jax.random.normal(jax.random.fold_in(_rk, 1), (32, 256, 64), jnp.float32)
        return x
    x = _rec_inputs()

    def _L0_tok_setup():
        import jax, jax.numpy as jnp
        import numpy as np
        B, W, CIN = (32, 1024, 64)
        K, DOUT = (3, 128)
        key = jax.random.key(seed)
        k1, k2, k3 = jax.random.split(key, 3)
        x = jax.random.normal(k1, (B, W, CIN), dtype=jnp.float32)
        kernel = jax.random.normal(k2, (K, CIN, DOUT), dtype=jnp.float32)
        bias = jax.random.uniform(k3, (DOUT,), dtype=jnp.float32, minval=0.0, maxval=2.0 * np.pi)
        kernel_scale = jnp.full((1,), np.sqrt(CIN * K ** 2 / 2.0), dtype=jnp.float32)
        return {'x': x, 'kernel': kernel, 'bias': bias, 'kernel_scale': kernel_scale}
    _L0_tok_all = _L0_tok_setup()
    _L0_tok_in = {k: v for k, v in _L0_tok_all.items() if k in ('kernel', 'bias', 'kernel_scale')}
    del _L0_tok_all

    def _L0_attn_setup():
        import jax, jax.numpy as jnp
        import numpy as np
        N_HEAD = 8
        D_MODEL = 128
        D_HEAD = D_MODEL // N_HEAD
        QLEN = 512
        BSZ = 4
        LN_EPS = 1e-05

        def _layer_norm(x, gamma, beta):
            mu = jnp.mean(x, axis=-1, keepdims=True)
            var = jnp.mean(jnp.square(x - mu), axis=-1, keepdims=True)
            return (x - mu) * jax.lax.rsqrt(var + LN_EPS) * gamma + beta

        def _pos_emb(qlen, d_model, dtype):
            pos_seq = jnp.arange(qlen - 1, -1, -1, dtype=dtype)
            inv_freq = 1.0 / 10000.0 ** (jnp.arange(0, d_model, 2, dtype=dtype) / d_model)
            sinusoid = pos_seq[:, None] * inv_freq[None, :]
            return jnp.concatenate([jnp.sin(sinusoid), jnp.cos(sinusoid)], axis=-1)

        def _rel_shift(x):
            q, r, b, n = x.shape
            x_padded = jnp.pad(x, ((0, 0), (1, 0), (0, 0), (0, 0)))
            x_padded = x_padded.reshape(r + 1, q, b, n)
            return x_padded[1:].reshape(q, r, b, n)
        key = jax.random.key(seed)
        ks = jax.random.split(key, 6)
        s = 0.02
        return {'w': jax.random.normal(ks[0], (QLEN, BSZ, D_MODEL), dtype=jnp.float32), 'Wqkv': jax.random.normal(ks[1], (3 * D_MODEL, D_MODEL), dtype=jnp.float32) * s, 'Wr': jax.random.normal(ks[2], (D_MODEL, D_MODEL), dtype=jnp.float32) * s, 'Wo': jax.random.normal(ks[3], (D_MODEL, D_MODEL), dtype=jnp.float32) * s, 'ln_gamma': jnp.ones((D_MODEL,), dtype=jnp.float32), 'ln_beta': jnp.zeros((D_MODEL,), dtype=jnp.float32), 'r_w_bias': jax.random.normal(ks[4], (N_HEAD, D_HEAD), dtype=jnp.float32) * s, 'r_r_bias': jax.random.normal(ks[5], (N_HEAD, D_HEAD), dtype=jnp.float32) * s}
    _L0_attn_all = _L0_attn_setup()
    _L0_attn_in = {k: v for k, v in _L0_attn_all.items() if k in ('Wqkv', 'Wr', 'Wo', 'ln_gamma', 'ln_beta', 'r_w_bias', 'r_r_bias')}
    del _L0_attn_all

    def _L0_ffn_setup():
        import jax, jax.numpy as jnp
        import numpy as np
        B, S, D = (4, 512, 128)
        I = 96
        E = 16
        K = 2

        def _inv_softplus(v):
            return float(np.log(np.expm1(v)))

        def swiglu5(h, alpha, gate_scale, up_shift, gate_clamp_raw, up_clamp_raw):
            gate_clamp = jax.nn.softplus(gate_clamp_raw)
            up_clamp = jax.nn.softplus(up_clamp_raw)
            g = jnp.clip(h[..., ::2], -gate_clamp, gate_clamp)
            u = jnp.clip(h[..., 1::2], -up_clamp, up_clamp)
            return g * jax.nn.sigmoid(g * alpha) * gate_scale * (u + up_shift)
        key = jax.random.key(seed)
        ks = jax.random.split(key, 10)
        std = 0.02
        raw = _inv_softplus(7.0)
        act = jnp.array([1.702, 1.0, 1.0, raw, raw], dtype=jnp.float32)
        return {'x': jax.random.normal(ks[0], (B, S, D), dtype=jnp.float32), 'gate_w': jax.random.normal(ks[1], (D, E), dtype=jnp.float32) * 0.01, 'gate_b': jnp.zeros((E,), dtype=jnp.float32), 'shared_w1': jax.random.normal(ks[2], (D, 2 * I), dtype=jnp.float32) * std, 'shared_b1': jnp.zeros((2 * I,), dtype=jnp.float32), 'shared_w2': jax.random.normal(ks[3], (I, D), dtype=jnp.float32) * std, 'shared_b2': jnp.zeros((D,), dtype=jnp.float32), 'shared_act': act, 'expert_w1': jax.random.normal(ks[4], (E, D, 2 * I), dtype=jnp.float32) * std, 'expert_b1': jnp.zeros((E, 2 * I), dtype=jnp.float32), 'expert_w2': jax.random.normal(ks[5], (E, I, D), dtype=jnp.float32) * std, 'expert_b2': jnp.zeros((E, D), dtype=jnp.float32), 'expert_act': jnp.tile(act[None, :], (E, 1))}
    _L0_ffn_all = _L0_ffn_setup()
    _L0_ffn_in = {k: v for k, v in _L0_ffn_all.items() if k in ('gate_w', 'gate_b', 'shared_w1', 'shared_b1', 'shared_w2', 'shared_b2', 'shared_act', 'expert_w1', 'expert_b1', 'expert_w2', 'expert_b2', 'expert_act')}
    del _L0_ffn_all
    return {'x': x, 'L0_tok_kernel': _L0_tok_in['kernel'], 'L0_tok_bias': _L0_tok_in['bias'], 'L0_tok_kernel_scale': _L0_tok_in['kernel_scale'], 'L0_attn_Wqkv': _L0_attn_in['Wqkv'], 'L0_attn_Wr': _L0_attn_in['Wr'], 'L0_attn_Wo': _L0_attn_in['Wo'], 'L0_attn_ln_gamma': _L0_attn_in['ln_gamma'], 'L0_attn_ln_beta': _L0_attn_in['ln_beta'], 'L0_attn_r_w_bias': _L0_attn_in['r_w_bias'], 'L0_attn_r_r_bias': _L0_attn_in['r_r_bias'], 'L0_ffn_gate_w': _L0_ffn_in['gate_w'], 'L0_ffn_gate_b': _L0_ffn_in['gate_b'], 'L0_ffn_shared_w1': _L0_ffn_in['shared_w1'], 'L0_ffn_shared_b1': _L0_ffn_in['shared_b1'], 'L0_ffn_shared_w2': _L0_ffn_in['shared_w2'], 'L0_ffn_shared_b2': _L0_ffn_in['shared_b2'], 'L0_ffn_shared_act': _L0_ffn_in['shared_act'], 'L0_ffn_expert_w1': _L0_ffn_in['expert_w1'], 'L0_ffn_expert_b1': _L0_ffn_in['expert_b1'], 'L0_ffn_expert_w2': _L0_ffn_in['expert_w2'], 'L0_ffn_expert_b2': _L0_ffn_in['expert_b2'], 'L0_ffn_expert_act': _L0_ffn_in['expert_act']}

def reference(x, L0_tok_kernel, L0_tok_bias, L0_tok_kernel_scale, L0_attn_Wqkv, L0_attn_Wr, L0_attn_Wo, L0_attn_ln_gamma, L0_attn_ln_beta, L0_attn_r_w_bias, L0_attn_r_r_bias, L0_ffn_gate_w, L0_ffn_gate_b, L0_ffn_shared_w1, L0_ffn_shared_b1, L0_ffn_shared_w2, L0_ffn_shared_b2, L0_ffn_shared_act, L0_ffn_expert_w1, L0_ffn_expert_b1, L0_ffn_expert_w2, L0_ffn_expert_b2, L0_ffn_expert_act):
    import jax
    import jax.numpy as jnp

    def _L0_tok_ref(x, kernel, bias, kernel_scale):
        import jax, jax.numpy as jnp
        import numpy as np
        B, W, CIN = (32, 1024, 64)
        K, DOUT = (3, 128)
        scaled_kernel = kernel / kernel_scale
        out = jax.lax.conv_general_dilated(x, scaled_kernel, window_strides=(1,), padding='VALID', dimension_numbers=('NWC', 'WIO', 'NWC'))
        out = out + bias
        norm = jnp.sqrt(jnp.float32(2.0 / DOUT))
        return norm * jnp.cos(out)

    def _L0_attn_ref(w, Wqkv, Wr, Wo, ln_gamma, ln_beta, r_w_bias, r_r_bias):
        import jax, jax.numpy as jnp
        import numpy as np
        N_HEAD = 8
        D_MODEL = 128
        D_HEAD = D_MODEL // N_HEAD
        QLEN = 512
        BSZ = 4
        LN_EPS = 1e-05

        def _layer_norm(x, gamma, beta):
            mu = jnp.mean(x, axis=-1, keepdims=True)
            var = jnp.mean(jnp.square(x - mu), axis=-1, keepdims=True)
            return (x - mu) * jax.lax.rsqrt(var + LN_EPS) * gamma + beta

        def _pos_emb(qlen, d_model, dtype):
            pos_seq = jnp.arange(qlen - 1, -1, -1, dtype=dtype)
            inv_freq = 1.0 / 10000.0 ** (jnp.arange(0, d_model, 2, dtype=dtype) / d_model)
            sinusoid = pos_seq[:, None] * inv_freq[None, :]
            return jnp.concatenate([jnp.sin(sinusoid), jnp.cos(sinusoid)], axis=-1)

        def _rel_shift(x):
            q, r, b, n = x.shape
            x_padded = jnp.pad(x, ((0, 0), (1, 0), (0, 0), (0, 0)))
            x_padded = x_padded.reshape(r + 1, q, b, n)
            return x_padded[1:].reshape(q, r, b, n)
        qlen, bsz, d_model = w.shape
        scale = 1.0 / D_HEAD ** 0.5
        r = _pos_emb(qlen, d_model, w.dtype)
        wn = _layer_norm(w, ln_gamma, ln_beta)
        heads = jnp.einsum('ibd,ed->ibe', wn, Wqkv)
        q_h, k_h, v_h = jnp.split(heads, 3, axis=-1)
        q_h = q_h.reshape(qlen, bsz, N_HEAD, D_HEAD)
        k_h = k_h.reshape(qlen, bsz, N_HEAD, D_HEAD)
        v_h = v_h.reshape(qlen, bsz, N_HEAD, D_HEAD)
        r_k = jnp.einsum('rd,ed->re', r, Wr).reshape(qlen, N_HEAD, D_HEAD)
        AC = jnp.einsum('ibnd,jbnd->ijbn', q_h + r_w_bias, k_h)
        BD = _rel_shift(jnp.einsum('ibnd,jnd->ijbn', q_h + r_r_bias, r_k))
        attn_score = (AC + BD) * scale
        attn_prob = jax.nn.softmax(attn_score, axis=1)
        attn_vec = jnp.einsum('ijbn,jbnd->ibnd', attn_prob, v_h)
        attn_vec = attn_vec.reshape(qlen, bsz, N_HEAD * D_HEAD)
        attn_out = jnp.einsum('ibe,de->ibd', attn_vec, Wo)
        return w + attn_out

    def _L0_ffn_ref(x, gate_w, gate_b, shared_w1, shared_b1, shared_w2, shared_b2, shared_act, expert_w1, expert_b1, expert_w2, expert_b2, expert_act):
        import jax, jax.numpy as jnp
        import numpy as np
        B, S, D = (4, 512, 128)
        I = 96
        E = 16
        K = 2

        def _inv_softplus(v):
            return float(np.log(np.expm1(v)))

        def swiglu5(h, alpha, gate_scale, up_shift, gate_clamp_raw, up_clamp_raw):
            gate_clamp = jax.nn.softplus(gate_clamp_raw)
            up_clamp = jax.nn.softplus(up_clamp_raw)
            g = jnp.clip(h[..., ::2], -gate_clamp, gate_clamp)
            u = jnp.clip(h[..., 1::2], -up_clamp, up_clamp)
            return g * jax.nn.sigmoid(g * alpha) * gate_scale * (u + up_shift)
        shape = x.shape
        xf = x.reshape(-1, shape[-1])
        h = xf @ shared_w1 + shared_b1
        t = swiglu5(h, shared_act[0], shared_act[1], shared_act[2], shared_act[3], shared_act[4])
        z = t @ shared_w2 + shared_b2
        gate_logits = xf @ gate_w + gate_b
        gate_probs = jax.nn.softmax(gate_logits, -1)
        w, idx = jax.lax.top_k(gate_probs, K)
        w = w / jnp.sum(w, axis=-1, keepdims=True)
        cw = jnp.sum(jax.nn.one_hot(idx, E, dtype=xf.dtype) * w[..., None], axis=1)
        he = jnp.einsum('nd,edh->enh', xf, expert_w1) + expert_b1[:, None, :]
        a = expert_act
        te = swiglu5(he, a[:, 0, None, None], a[:, 1, None, None], a[:, 2, None, None], a[:, 3, None, None], a[:, 4, None, None])
        oe = jnp.einsum('enh,ehd->end', te, expert_w2) + expert_b2[:, None, :]
        y = jnp.einsum('ne,end->nd', cw, oe)
        return (y + z).reshape(shape)
    h = _L0_tok_ref(x, L0_tok_kernel, L0_tok_bias, L0_tok_kernel_scale)
    h = h + _L0_attn_ref(_layernorm(h, axis=-1), L0_attn_Wqkv, L0_attn_Wr, L0_attn_Wo, L0_attn_ln_gamma, L0_attn_ln_beta, L0_attn_r_w_bias, L0_attn_r_r_bias)
    h = h + _L0_ffn_ref(_layernorm(h, axis=-1), L0_ffn_gate_w, L0_ffn_gate_b, L0_ffn_shared_w1, L0_ffn_shared_b1, L0_ffn_shared_w2, L0_ffn_shared_b2, L0_ffn_shared_act, L0_ffn_expert_w1, L0_ffn_expert_b1, L0_ffn_expert_w2, L0_ffn_expert_b2, L0_ffn_expert_act)
    return h

_drawn_inputs = setup_inputs


def setup_inputs(seed=0):
    import zlib

    import numpy as np

    out = dict(_drawn_inputs(seed))
    spreads = {'L0_attn_ln_gamma': (1.0, 0.6),
     'L0_attn_ln_beta': (0.0, 0.8),
     'L0_ffn_gate_b': (0.0, 0.1),
     'L0_ffn_shared_b1': (0.0, 0.746),
     'L0_ffn_shared_b2': (0.0, 0.1),
     'L0_ffn_expert_b1': (0.0, 0.8),
     'L0_ffn_expert_b2': (0.0, 0.1)}
    factors = {'L0_attn_Wr': 22.008,
     'L0_attn_r_w_bias': 48.638,
     'L0_attn_r_r_bias': 39.876,
     'L0_ffn_shared_w1': 2.707,
     'L0_ffn_expert_w1': 3.775,
     'L0_ffn_expert_w2': 3.345}
    for name, (base, spread) in spreads.items():
        noise = np.random.default_rng([zlib.crc32(name.encode()), seed]).standard_normal(out[name].shape)
        drawn = base * np.exp(spread * noise) if base else spread * noise
        out[name] = jnp.asarray(drawn.astype(out[name].dtype))
    for name, factor in factors.items():
        out[name] = (out[name] * factor).astype(out[name].dtype)
    return out
```

```python
from contextlib import ExitStack

import numpy as np

import concourse.bass as bass
from concourse import mybir

F32 = mybir.dt.float32
BF16 = mybir.dt.bfloat16
I32 = mybir.dt.int32
U32 = mybir.dt.uint32
ALU = mybir.AluOpType
ACT = mybir.ActivationFunctionType
AX = mybir.AxisListType.X

SEG, WIDTH, CIN, TAPS, D = 32, 256, 64, 3, 128
POS = WIDTH - TAPS + 1
HALF = POS // 2
POSP = 256
HEADS, DH = 8, 16
GROUPS, QUADS = 2, 4
E, IH = 16, 96
CB = 16
CHUNKS = POSP // CB
CC = CB * SEG
TILES = CC // 128
TOKT = SEG * POSP // 128
BIG = 64
REGION = SEG * POSP + 128
DUMMY = E * REGION
ETILES = 2 * TOKT + E
NB1 = (E + 1) * 2 * IH
WIN = 2 * SEG - 1
MAGIC = float(1.5 * 2 ** 23)
TWO_PI_HI = float(np.float32(6.28125))
TWO_PI_LO = float(np.float32(2 * np.pi - 6.28125))
INV_TWO_PI = float(np.float32(1 / (2 * np.pi)))
EPS = 1e-5
COS_NORM = float(np.sqrt(np.float32(2.0 / D)))
SCALE = 1.0 / DH ** 0.5

W_COLS = dict(conv01=D, conv2=D, conv12=D, conv0=D, ident=128, wq=D, wk=D, wv=D, wo=D, wr=D, wvp=D, post=SEG,
              rwb=1, rrb=1, gamma=1, beta=1, gate=E, ws1=2 * IH, ws2=D, iota=ETILES, qmask=QUADS,
              pmask=QUADS, tri16=E, stri16=E, pmask3=3)
W_AT = {}
_at = 0
for _k, _n in W_COLS.items():
    W_AT[_k] = (_at, _at + _n)
    _at += _n
W_ALL = _at
W_EARLY = W_AT['wq'][0]
R_COLS = dict(cbias=D, kscale=1, gateb=E, act=5 * (E + 1), iota16=E, ebase=E)
R_AT = {}
_at = 0
for _k, _n in R_COLS.items():
    R_AT[_k] = (_at, _at + _n)
    _at += _n
R_ALL = _at


def staged(eng, total, stages, unroll=4):
    lag = max(l for _, l in stages)
    first = lag + unroll
    loops = (total - first) // unroll
    last = first + loops * unroll

    def step(j):
        for fn, l in stages:
            if 0 <= j - l < total:
                fn(j - l, (j - l) % unroll)

    for j in range(first):
        step(j)
    if loops > 1:
        with eng.Fori(first, last - unroll + 1, unroll) as at:
            for u in range(unroll):
                for fn, l in stages:
                    n = at + (u - l) if u != l else at
                    fn(n, (first + u - l) % unroll)
    else:
        last = first
    for j in range(last, total + lag):
        step(j)


def after(eng, sem, value):
    if not isinstance(value, int) or value > 0:
        eng.wait_ge(sem, value)


def alone(eng, sem, value):
    if not isinstance(value, int):
        value = eng.snap(eng.to_reg(value))
        eng.wait_ge(sem, 1)
    after(eng, sem, value)


def landed(n, s, ring):
    return (n - s % ring) * (16 // ring) + 16


def build(nc, x, weights, rows, w1, w2, b1, out):
    with ExitStack() as ctx:
        def sb(name, cols, dt=F32):
            return ctx.enter_context(nc.sbuf_tensor(name, [128, cols], dt))[:, :]

        def sem(name):
            return ctx.enter_context(nc.semaphore(name))

        def sems(name, n):
            return [sem(f"{name}{i}") for i in range(n)]

        res_d = nc.dram_tensor("res_d", [POSP, SEG, D], F32, kind="Internal").ap()
        b1s_d = nc.dram_tensor("b1s_d", [3, NB1], BF16, kind="Internal").ap()
        xs_d = nc.dram_tensor("xs_d", [DUMMY + 128, D], F32, kind="Internal").ap()
        ys_d = nc.dram_tensor("ys_d", [ETILES * 128, D], F32, kind="Internal").ap()

        wnT = sb("wnT", POSP * SEG)
        qr = sb("qr", POSP * SEG)
        bdt = sb("bdt", GROUPS * POSP * SEG)
        W = sb("W", W_ALL)
        R = sb("R", R_ALL)
        yrow = sb("yrow", CHUNKS * 2 * TILES, I32)
        onesb = sb("onesb", 128, BF16)
        trib = sb("trib", 128, BF16)
        b1sh = sb("b1sh", 2 * IH, BF16)

        def w(key, a=0, b=None):
            lo, hi = W_AT[key]
            return W[:, lo + a:(hi if b is None else lo + b)]

        def r(key, a=0, b=None):
            lo, hi = R_AT[key]
            return R[:, lo + a:(hi if b is None else lo + b)]

        slots = w("wvp")
        chosen = w("wr")
        wts = w("wq")

        QV = sb("QV", 3 * CB * 128)
        Qb = [QV[:, u * CB * 128:(u + 1) * CB * 128] for u in range(2)]
        Vb = QV[:, 2 * CB * 128:]
        S = [sb(f"S{u}", GROUPS * CC) for u in range(2)]
        Kt = [sb(f"Kt{u}", CC) for u in range(2)]
        Vt = [sb(f"Vt{u}", CC) for u in range(2)]
        PP = sb("PP", 2 * GROUPS * CC)
        PT = [PP[:, u * GROUPS * CC:(u + 1) * GROUPS * CC] for u in range(2)]
        at = w("conv01", 0, CC)
        res = [sb(f"res{u}", CC) for u in range(2)]
        xf = [sb(f"xf{u}", CC) for u in range(2)]
        xfT = sb("xfT", CC)
        tT = sb("tT", CC)
        gc = sb("gc", TILES * IH)
        eg = sb("eg", TILES * IH)
        uc = sb("uc", TILES * IH)
        small = sb("small", 1300)
        used = [0]

        def tiny(cols):
            used[0] += cols
            return small[:, used[0] - cols:used[0]]

        neg_half = tiny(8)
        half_pi = tiny(1)
        recip_ks = tiny(1)
        conv_scaled = w("conv01", 0, 4 * D)
        bq, bk, bv = tiny(1), tiny(1), tiny(1)
        qbias = tiny(1)
        wrdiff = tiny(1)
        qmb = tiny(QUADS)
        win = bdt[:, 12288:12288 + 2 * QUADS * WIN]
        win1, win2 = win[:, 0:QUADS * WIN], win[:, QUADS * WIN:]
        par = r("act").rearrange("p (e f) -> p e f", f=5)
        absraw, expraw, clamp, nclamp, maxraw = (tiny(2 * (E + 1)) for _ in range(5))
        nalpha = tiny(E + 1)

        mx = [tiny(GROUPS * CB) for _ in range(2)]
        sm = tiny(GROUPS * CB)
        rc = [tiny(GROUPS * CB) for _ in range(2)]
        st2 = tiny(TILES * 6)
        mv2 = [tiny(TILES * 2) for _ in range(2)]
        vp2 = tiny(TILES)
        rstd_t = [tiny(TILES) for _ in range(2)]
        sl32 = [tiny(2 * TILES) for _ in range(2)]
        alpha, shift_p = tiny(E + 1), tiny(E + 1)
        rt2 = sem("slot_steps")
        b1_tmp = sem("b1_rests")
        lg = tiny(TILES * E)
        m8 = tiny(TILES * 8)
        ix8 = tiny(TILES * 8)
        ixf = tiny(2 * TILES)
        oh = tiny(2 * TILES * E)
        rb = tiny(TILES * E)
        ohr = tiny(2 * TILES * E)
        slf = tiny(2 * TILES)
        dd = tiny(TILES)
        ed = tiny(2 * TILES)
        both = [tiny(TILES * E // 2) for _ in range(2)]
        both = [b.bitcast(BF16) for b in both]
        seen = [tiny(E // 2).bitcast(BF16) for _ in range(2)]
        tsum = tiny(E)

        assert used[0] <= 1300
        def window(k, t0):
            if k == 0:
                return QV[:, t0 * 128:(t0 + 1) * 128]
            return QV[:, (SEG + t0) * 128:(SEG + t0 + 1) * 128] if t0 < 16 else PP[:, (t0 - 16) * 128:(t0 - 15) * 128]

        def slide(v, first, count):
            return bass.AP(tensor=v.tensor, offset=v.offset + first, ap=[v.ap[0], [1, count], [1, SEG]])

        ps = ctx.enter_context(nc.psum_tensor("ps", [128, 8 * 512], F32))[:, :]

        def bank(n, k=1):
            return ps[:, n * 512:(n + k) * 512]

        taken = [0]

        def in_bdt(cols):
            taken[0] += cols
            return bdt[:, taken[0] - cols:taken[0]]

        xin = [in_bdt(128) for _ in range(4)]
        XT = [in_bdt(128) for _ in range(2)]
        va = [in_bdt(2 * D) for _ in range(2)]
        ka = [in_bdt(2 * D) for _ in range(2)]
        ra = [in_bdt(2 * D) for _ in range(2)]
        ca = [in_bdt(2 * D) for _ in range(4)]
        st = in_bdt(12)
        mv = [in_bdt(4) for _ in range(4)]
        pw = [in_bdt(4) for _ in range(2)]
        rr = [in_bdt(4) for _ in range(4)]
        rs = [in_bdt(4) for _ in range(2)]
        wn = [in_bdt(2 * D) for _ in range(2)]
        ha = [in_bdt(2 * D) for _ in range(4)]
        zpad = in_bdt(D)
        b1f = in_bdt(NB1)[0:3]
        b1h = in_bdt(NB1 // 2)[0:3].bitcast(BF16)
        b1t = in_bdt(NB1 // 2)[0:3].bitcast(BF16)
        taken[0] = 0
        w1s = in_bdt(E * 2 * IH)
        w2s = in_bdt(E * D)
        b1e = in_bdt(NB1 // 2).bitcast(BF16)
        xe = [in_bdt(D) for _ in range(4)]
        xeT = [in_bdt(128) for _ in range(2)]
        ge, ee, ue, te = ([in_bdt(IH) for _ in range(2)] for _ in range(4))
        teT = [in_bdt(128) for _ in range(2)]
        ye = [in_bdt(D) for _ in range(4)]
        cnt = in_bdt(8)
        cmp = in_bdt(ETILES)
        ones1 = in_bdt(128)
        rowi, rowe = in_bdt(ETILES), in_bdt(ETILES)
        scaled16, delta = in_bdt(E), in_bdt(E)
        look = in_bdt(2 * TOKT * E)
        rowf = in_bdt(4 * ETILES)
        cnt1 = in_bdt(2 * E)
        g0 = [in_bdt(D) for _ in range(4)]
        g1 = [in_bdt(D) for _ in range(4)]
        of = [in_bdt(D) for _ in range(4)]
        zeros = in_bdt(D)
        idx = [in_bdt(2).bitcast(I32) for _ in range(4)]

        ident = w("ident")
        weights_in, weights2_in, rows_in, b1_in = sem("weights_in"), sem("weights2_in"), sem("rows_in"), sem("b1_in")
        consts = sem("consts")
        conv_ready = sem("conv_ready")
        setup_mm, rk_ready, wqkv_ready = sem("setup_mm"), sem("rk_ready"), sem("wqkv_ready")
        qbias_ready, win_ready, dve_setup = sem("qbias_ready"), sem("win_ready"), sem("dve_setup")
        params_abs, params_log, params_ready = sem("params_abs"), sem("params_log"), sem("params_ready")
        b1_parts, b1_stored, b1sh_in = sem("b1_parts"), sem("b1_stored"), sem("b1sh_in")
        pads = sem("pads")
        x_in = sems("x_in", 4)
        xt_ps, xt_sb, conv_ps = sem("xt_ps"), sem("xt_sb"), sem("conv_ps")
        biased, rounded, multiple, reduced_hi, reduced = (sem(n) for n in (
            "biased", "rounded", "multiple", "reduced_hi", "reduced"))
        absolute, cosine = sem("absolute"), sem("cosine")
        stats_a, mv_a, pw_a, rr_a, rs_a, wn_a = (sem(n) for n in ("stats_a", "mv_a", "pw_a", "rr_a", "rs_a", "wn_a"))
        ha_ready, ha_stored, wt_ps, wnT_ready = sem("ha_ready"), sems("ha_stored", 4), sem("wt_ps"), sem("wnT_ready")
        q_ps, qr_ready, bd_ps, bdt_ready = sem("q_ps"), sem("qr_ready"), sem("bd_ps"), sem("bdt_ready")
        k_ps, k_sb, v_ps, vt_ready, vb_ready = (sem(n) for n in ("k_ps", "k_sb", "v_ps", "vt_ready", "vb_ready"))
        qb_dve, qb_act, ac_ps, scores = sem("qb_dve"), sem("qb_act"), sem("ac_ps"), sem("scores")
        max_ready, shifted, exped, sums, rc_ready, probs, pt_ready = (sem(n) for n in (
            "max_ready", "shifted", "exped", "sums", "rc_ready", "probs", "pt_ready"))
        pv_ps, at_ready, wo_ps = sem("pv_ps"), sem("at_ready"), sem("wo_ps")
        res_in, h1_ready = sems("res_in", 2), sem("h1_ready")
        stats_d, mv_d, vp_d, rstd_d, xf_ready = (sem(n) for n in ("stats_d", "mv_d", "vp_d", "rstd_d", "xf_ready"))
        xft_ps, xft_sb, logit_ps, hs_ps = (sem(n) for n in ("xft_ps", "xft_sb", "logit_ps", "hs_ps"))
        gc_ready, eg_act, eg_dve, uc_ready, ts_ready = (sem(n) for n in (
            "gc_ready", "eg_act", "eg_dve", "uc_ready", "ts_ready"))
        tt_ps, tt_sb, z_ps, z_added = (sem(n) for n in ("tt_ps", "tt_sb", "z_ps", "z_added"))
        win_src, tri_scaled, delta_ps, looked = sem("win_src"), sem("tri_scaled"), sem("delta_ps"), sem("looked")
        rt, ed_plus = sem("router_steps"), sem("ed_plus")
        both_ready, seen_ready, rank_ps, slot_ready, dd_ready, ed_ready, wts_ready = (sem(n) for n in (
            "both_ready", "seen_ready", "rank_ps", "slot_ready", "dd_ready", "ed_ready", "wts_ready"))
        sent = sems("sent", 2)
        w1_in, w2_in, b1e_in, w2_scaled = sem("w1_in"), sem("w2_in"), sem("b1e_in"), sem("w2_scaled")
        zeros_ready, counts_ps, prep, prep_mm, map_ready, tails = (sem(n) for n in (
            "zeros_ready", "counts_ps", "prep", "prep_mm", "map_ready", "tails"))
        xe_in, ye_out = sems("xe_in", 4), sems("ye_out", 4)
        xet_ps, xet_sb, he_ps, ge_ready, ee_ready, m_ready, ue_ready, te_ready = (sem(n) for n in (
            "xet_ps", "xet_sb", "he_ps", "ge_ready", "ee_ready", "m_ready", "ue_ready", "te_ready"))
        tet_ps, tet_sb, ye_ps, ye_ready = (sem(n) for n in ("tet_ps", "tet_sb", "ye_ps", "ye_ready"))
        idx_ready, g_in, f_half, f_ready, stored = sem("idx_ready"), sems("g_in", 4), sem("f_half"), sem("f_ready"), sems("stored", 4)

        def cols(t, n, width=CC):
            return t[:, n * width:(n + 1) * width] if isinstance(n, int) else t[:, bass.ds(n * width, width)]

        def bchunk(n):
            v = bdt.rearrange("p (g c) -> p g c", g=GROUPS)
            return (v[:, :, n * CC:(n + 1) * CC] if isinstance(n, int) else v[:, :, bass.ds(n * CC, CC)])

        def scores4(s):
            return S[s % 2].rearrange("p (g b j) -> p g b j", g=GROUPS, j=SEG)

        def tiled(t, k=TILES):
            return t.rearrange("p (t d) -> p t d", t=k)

        def tile_expert(n):
            i = rowe.bitcast(I32)
            return i[0:1, n:n + 1] if isinstance(n, int) else i[0:1, bass.ds(n, 1)]

        block = ctx.enter_context(nc.Block())

        @block.sync
        def _(sp):
            sp.dma_start(W[:, 0:W_EARLY], weights[:, 0:W_EARLY]).then_inc(weights_in, 16)
            sp.dma_start(R, rows[0:1, :].to_broadcast([128, R_ALL])).then_inc(rows_in, 16)
            sp.dma_start(W[:, W_EARLY:], weights[:, W_EARLY:]).then_inc(weights2_in, 16)
            sp.dma_start(b1f, b1[0:1, :].to_broadcast([3, NB1])).then_inc(b1_in, 16)

            def load_x(n, s):
                after(sp, xt_ps, n - 3)
                sp.dma_start(xin[s % 4], x[n] if isinstance(n, int) else
                             x[bass.ds(n, 1)].rearrange("o p c -> (o p) c")).then_inc(x_in[s % 4], 16)

            def store_res(n, s):
                sp.wait_ge(ha_ready, n + 1)
                dst = res_d.rearrange("(p s) i d -> p i s d", s=2)
                src = ha[s % 4].rearrange("p (s d) -> p s d", s=2)
                for a, b in ((0, 112), (112, HALF)):
                    v = dst[a:b, n] if isinstance(n, int) else \
                        dst[a:b, bass.ds(n, 1)].rearrange("p o s d -> p (o s) d")
                    sp.dma_start(v, src[a:b]).then_inc(ha_stored[s % 4], 16)

            staged(sp, SEG, [(load_x, 0), (store_res, 3)])
            sp.wait_ge(pads, 1)
            sp.dma_start(res_d[POS:POSP].rearrange("b i d -> (b i) d"), zpad[0:64, :]).then_inc(pads, 16)
            sp.wait_ge(b1_parts, 5)
            sp.dma_start(b1s_d, b1h).then_inc(b1_stored, 16)
            sp.wait_ge(b1_stored, 16)
            sp.dma_start(b1sh[0:3, :], b1s_d[:, E * 2 * IH:]).then_inc(b1sh_in, 16)
            for q in ha_stored:
                sp.wait_ge(q, 2 * 16 * SEG // 4)
            sp.wait_ge(pads, 17)

            def load_res(n, s):
                after(sp, h1_ready, n - 1)
                v = res_d.rearrange("(t b) i d -> (b i) t d", b=128 // SEG)
                v = v[:, n * TILES:(n + 1) * TILES] if isinstance(n, int) else v[:, bass.ds(n * TILES, TILES)]
                sp.dma_start(tiled(res[s % 2]), v).then_inc(res_in[s % 2], 16)

            staged(sp, CHUNKS, [(load_res, 0)], 2)

            sp.wait_ge(pt_ready, CHUNKS)
            sp.dma_start(w1s.rearrange("p (e h) -> p e h", e=E), w1).then_inc(w1_in, 16)
            sp.dma_start(w2s[0:IH + 1, :].rearrange("p (e h) -> p e h", e=E), w2).then_inc(w2_in, 16)
            sp.dma_start(b1e[0:3, :], b1s_d).then_inc(b1e_in, 16)
            sp.wait_ge(zeros_ready, 1)
            sp.wait_ge(map_ready, 1)
            sp.dma_start(xs_d[DUMMY:DUMMY + 128, :], zeros).then_inc(tails, 16)
            with sp.Fori(0, E) as e:
                c = sp.value_load(cnt1.bitcast(I32)[0:1, bass.ds(e, 1)], min_val=0, max_val=E * REGION)
                sp.dma_start(xs_d[bass.ds(c, 128), :], zeros).then_inc(tails, 16)
            sp.wait_ge(tails, 16 * (E + 1))
            for q in sent:
                sp.wait_ge(q, 16 * TOKT)

            def tile_row(n):
                i = rowi.bitcast(I32)
                i = i[0:1, n:n + 1] if isinstance(n, int) else i[0:1, bass.ds(n, 1)]
                return sp.value_load(i, min_val=0, max_val=DUMMY)

            def load_xe(n, s):
                after(sp, xet_ps, n - 3)
                sp.dma_start(xe[s % 4], xs_d[bass.ds(tile_row(n), 128), :]).then_inc(xe_in[s % 4], 16)

            def store_ye(n, s):
                sp.wait_ge(ye_ready, n + 1)
                v = ys_d.rearrange("(t r) d -> t r d", r=128)
                v = v[n] if isinstance(n, int) else v[bass.ds(n, 1)].rearrange("o r d -> (o r) d")
                sp.dma_start(v, ye[s % 4]).then_inc(ye_out[s % 4], 16)

            staged(sp, ETILES, [(load_xe, 0), (store_ye, 3)])

            def store_out(n, s):
                sp.wait_ge(f_ready, n + 1)
                v = out.rearrange("(t b) i d -> t (b i) d", b=128 // SEG)
                v = v[n] if isinstance(n, int) else v[bass.ds(n, 1)].rearrange("o r d -> (o r) d")
                sp.dma_start(v, of[s % 4]).then_inc(stored[s % 4], 16)

            staged(sp, TOKT, [(store_out, 0)])
            for q in stored:
                sp.wait_ge(q, 16 * TOKT // 4)

        @block.gpsimd
        def _(pool):
            pool.memset(neg_half, -0.5)
            pool.memset(half_pi, float(np.pi / 2))
            pool.memset(onesb, 1.0)
            pool.memset(zpad, 0.0).then_inc(pads, 1)
            pool.memset(win, 0.0)
            pool.memset(seen[0], 0.0)
            pool.memset(trib, 1.0)
            pool.memset(wnT[:, POS * SEG:], 0.0).then_inc(consts, 1)
            pool.wait_ge(consts, 1)
            pool.affine_select(out=trib, in_=trib, compare_op=ALU.is_gt, fill=0.0, base=0,
                               pattern=[[1, 128]], channel_multiplier=-1).then_inc(consts, 1)

            def split_b1():
                pool.wait_ge(b1_in, 16)
                pool.wait_ge(weights2_in, 16)
                pool.tensor_copy(b1h, b1f).then_inc(b1_parts, 1)
                t = b1t
                for k in (1, 2):
                    pool.wait_ge(b1_parts, 2 * k - 1)
                    pool.tensor_scalar(t, b1h, w("pmask3", k, k + 1)[0:3, :], None, ALU.mult).then_inc(b1_tmp, 1)
                    pool.wait_ge(b1_tmp, 2 * k - 1)
                    pool.tensor_tensor(b1f, b1f, t, ALU.subtract).then_inc(b1_tmp, 1)
                    pool.wait_ge(b1_tmp, 2 * k)
                    pool.tensor_copy(b1h, b1f).then_inc(b1_parts, 2)

            def rstd_a(n, s):
                alone(pool, pw_a, n + 1)
                alone(pool, wn_a, n - 3)
                pool.tensor_tensor(rr[s % 4][0:HALF, :], pw[s % 2][0:HALF, :], neg_half[0:HALF, 0:4], ALU.pow).then_inc(rr_a, 1)

            def residual_a(n, s):
                alone(pool, rs_a, n + 1)
                if not isinstance(n, int) or n >= 4:
                    alone(pool, ha_stored[s % 4], (n - s % 4) * 8)
                for k in range(2):
                    c = ca[s % 4][0:HALF, k * D:(k + 1) * D]
                    o = pool.tensor_scalar(ha[s % 4][0:HALF, k * D:(k + 1) * D], c, rs[s % 2][0:HALF, k:k + 1],
                                           rs[s % 2][0:HALF, 2 + k:3 + k], ALU.mult, ALU.add)
                o.then_inc(ha_ready, 1)

            staged(pool, SEG, [(rstd_a, 0), (residual_a, 1)])
            split_b1()

            def shift(n, s):
                alone(pool, max_ready, n + 1)
                m = mx[s % 2].rearrange("p (g b) -> p g b", g=GROUPS).unsqueeze(3).to_broadcast([128, GROUPS, CB, SEG])
                v = scores4(s)
                for g in range(GROUPS):
                    o = pool.tensor_tensor(v[:, g], v[:, g], m[:, g], ALU.subtract)
                o.then_inc(shifted, 1)

            def normalise(n, s):
                alone(pool, rc_ready, n + 1)
                m = rc[s % 2].rearrange("p (g b) -> p g b", g=GROUPS).unsqueeze(3).to_broadcast([128, GROUPS, CB, SEG])
                v = scores4(s)
                for g in range(GROUPS):
                    o = pool.tensor_tensor(v[:, g], v[:, g], m[:, g], ALU.mult)
                o.then_inc(probs, 1)

            def rstd(n, s):
                alone(pool, mv_d, n + 1)
                alone(pool, rstd_d, n)
                pool.tensor_scalar(vp2, tiled(mv2[s % 2])[:, :, 1], EPS, None, ALU.add).then_inc(vp_d, 1)
                alone(pool, vp_d, n + 1)
                pool.tensor_tensor(rstd_t[s % 2], vp2, neg_half[:, 0:TILES], ALU.pow).then_inc(rstd_d, 1)

            def dispatch(n, s):
                alone(pool, slot_ready, n + 1)
                for k in range(2):
                    for t in range(TILES):
                        pool.indirect_dma_start(
                            out=xs_d, out_offset=bass.IndirectOffsetOnAxis(
                                ap=sl32[s % 2].bitcast(I32)[:, k * TILES + t:k * TILES + t + 1], axis=0),
                            in_=xf[s % 2][:, t * D:(t + 1) * D], in_offset=None).then_inc(sent[s % 2], 16)

            staged(pool, CHUNKS, [(shift, 0), (normalise, 1), (rstd, 2), (dispatch, 3)], 2)
            pool.wait_ge(pt_ready, CHUNKS)
            pool.memset(zeros, 0.0).then_inc(zeros_ready, 1)
            for q in ye_out:
                pool.wait_ge(q, 16 * ETILES // 4)

            def gather(n, s):
                alone(pool, idx_ready, n + 1)
                for k, g in ((0, g0), (1, g1)):
                    pool.indirect_dma_start(
                        out=g[s % 4], out_offset=None, in_=ys_d,
                        in_offset=bass.IndirectOffsetOnAxis(ap=idx[s % 4][:, k:k + 1], axis=0)).then_inc(g_in[s % 4], 16)

            staged(pool, TOKT, [(gather, 0)])

        @block.scalar
        def _(act):
            act.wait_ge(params_abs, 2)
            act.activation(expraw, absraw, ACT.Exp, scale=-1.0).then_inc(params_log, 1)
            act.wait_ge(params_log, 1)
            act.activation(absraw, expraw, ACT.Ln, bias=1.0).then_inc(params_log, 1)

            def xt_copy(n, s):
                act.wait_ge(xt_ps, n + 1)
                after(act, conv_ps, n - 1)
                act.activation(XT[s % 2], bank(s % 2)[:, 0:128], ACT.Copy).then_inc(xt_sb, 1)

            def cosines(n, s):
                act.wait_ge(reduced, n + 1)
                act.activation(ra[s % 2][0:HALF], ra[s % 2][0:HALF], ACT.Abs).then_inc(absolute, 1)
                act.wait_ge(absolute, n + 1)
                after(act, ha_ready, n - 3)
                after(act, wn_a, n - 3)
                act.activation(ca[s % 4][0:HALF], ra[s % 2][0:HALF], ACT.Sin, bias=half_pi[0:HALF, :], scale=-1.0).then_inc(cosine, 1)

            def wt_copy(n, s):
                act.wait_ge(wt_ps, n + 1)
                v = wnT.rearrange("d (p s i) -> d i s p", s=2, i=SEG)
                v = v[:, n, :, 0:HALF] if isinstance(n, int) else v[:, bass.ds(n, 1), :, 0:HALF].rearrange("d o s p -> d (o s) p")
                act.activation(v, bank(4 + s % 2)[:, 0:2 * HALF].rearrange("d (s p) -> d s p", s=2), ACT.Copy).then_inc(wnT_ready, 1)

            act.wait_ge(consts, 1)
            staged(act, SEG, [(xt_copy, 0), (cosines, 1), (wt_copy, 3)])

            def q_copy(n, s):
                act.wait_ge(q_ps, n + 1)
                if isinstance(n, int) and n == 0:
                    act.wait_ge(qbias_ready, 1)
                act.activation(cols(qr, n), bank(s % 4), ACT.Identity, bias=qbias).then_inc(qr_ready, 1)

            staged(act, CHUNKS, [(q_copy, 0)])

            def k_copy(n, s):
                act.wait_ge(k_ps, n + 1)
                after(act, ac_ps, n - 1)
                act.activation(Kt[s % 2], bank(0), ACT.Identity, bias=bk).then_inc(k_sb, 1)

            def q_expand(n, s):
                after(act, ac_ps, n - 1)
                if isinstance(n, int) and n == 0:
                    act.wait_ge(bd_ps, 2 * POSP // BIG)
                o = Qb[s % 2].rearrange("p (b q i) -> p q b i", q=QUADS, i=SEG)
                q = cols(qr, n).rearrange("p (b i) -> p b i", i=SEG)
                for k in (2, 3):
                    i = act.activation(o[:, k], q, ACT.Identity, scale=w("qmask", k, k + 1), bias=qmb[:, k:k + 1])
                i.then_inc(qb_act, 1)

            def exps(n, s):
                act.wait_ge(shifted, n + 1)
                act.activation(S[s % 2], S[s % 2], ACT.Exp, scale=SCALE).then_inc(exped, 1)

            def v_expand(n, s):
                act.wait_ge(vt_ready, n + 1)
                after(act, pv_ps, n)
                o = Vb.rearrange("p (g b q d) -> p q g b d", g=GROUPS, b=CB, q=QUADS)
                v = Vt[s % 2].rearrange("p (b g d) -> p g b d", g=GROUPS, d=DH)
                for k in range(QUADS):
                    i = act.activation(o[:, k], v, ACT.Copy, scale=w("pmask", k, k + 1))
                i.then_inc(vb_ready, 1)

            def at_copy(n, s):
                act.wait_ge(pv_ps, n + 1)
                after(act, wo_ps, n)
                act.activation(at, bank(3), ACT.Identity, bias=bv).then_inc(at_ready, 1)

            def xft_copy(n, s):
                act.wait_ge(xft_ps, n + 1)
                after(act, hs_ps, n)
                act.activation(xfT, bank(4), ACT.Copy).then_inc(xft_sb, 1)

            def swish_exp(n, s):
                act.wait_ge(gc_ready, n + 1)
                act.activation(eg, gc, ACT.Exp, scale=nalpha[:, E:E + 1]).then_inc(eg_act, 1)

            def weight_exp(n, s):
                act.wait_ge(dd_ready, n + 1)
                act.activation(ed[:, 0:TILES], dd, ACT.Exp, scale=1.0)
                act.activation(ed[:, TILES:], dd, ACT.Exp, scale=-1.0).then_inc(ed_ready, 1)

            def tt_copy(n, s):
                act.wait_ge(tt_ps, n + 1)
                after(act, z_ps, n)
                act.activation(tT[0:IH, :], bank(4)[0:IH, :], ACT.Copy).then_inc(tt_sb, 1)

            act.wait_ge(params_ready, 1)
            staged(act, CHUNKS, [(k_copy, 0), (q_expand, 0), (swish_exp, 3), (weight_exp, 3), (v_expand, 0), (exps, 0),
                                 (at_copy, 1), (tt_copy, 3), (xft_copy, 2)], 2)

            def xet_copy(n, s):
                act.wait_ge(xet_ps, n + 1)
                after(act, he_ps, n - 1)
                act.activation(xeT[s % 2], bank(s % 2)[:, 0:128], ACT.Copy).then_inc(xet_sb, 1)

            def sigmoids(n, s):
                e = act.value_load(tile_expert(n), min_val=0, max_val=E - 1)
                act.wait_ge(ge_ready, n + 1)
                after(act, te_ready, n - 1)
                act.activation(ee[s % 2], ge[s % 2], ACT.Sigmoid, scale=alpha[:, bass.ds(e, 1)]).then_inc(ee_ready, 1)

            def tet_copy(n, s):
                act.wait_ge(tet_ps, n + 1)
                after(act, ye_ps, n - 1)
                act.activation(teT[s % 2][0:IH, :], bank(4 + s % 2)[0:IH, 0:128], ACT.Copy).then_inc(tet_sb, 1)

            act.wait_ge(map_ready, 1)
            staged(act, ETILES, [(xet_copy, 0), (sigmoids, 1), (tet_copy, 2)])

        @block.tensor
        def _(pe):
            pe.wait_ge(weights_in, 16)

            def xt(n, s):
                pe.wait_ge(x_in[s % 4], landed(n, s, 4))
                after(pe, xt_sb, n - 1)
                pe.transpose(bank(s % 2)[:, 0:128], xin[s % 4], ident).then_inc(xt_ps, 1)

            def conv(n, s):
                pe.wait_ge(xt_sb, n + 1)
                if isinstance(n, int) and n == 0:
                    pe.wait_ge(conv_ready, 1)
                after(pe, biased, n - 1)
                o, t = bank(2 + s % 2)[0:HALF], XT[s % 2]
                c01, c2, c12, c0 = w("conv01"), w("conv2"), w("conv12"), w("conv0")
                pe.matmul(o[:, 0:D], t[:, 0:HALF], c01, start=True, stop=False)
                pe.matmul(o[:, 0:D], t[:, 1:HALF + 1], c2, start=False, stop=True)
                pe.matmul(o[:, D:2 * D], t[:, 1:HALF + 1], c12, start=True, stop=False)
                pe.matmul(o[:, D:2 * D], t[:, 0:HALF], c0, start=False, stop=True).then_inc(conv_ps, 1)

            def wt(n, s):
                pe.wait_ge(wn_a, n + 1)
                after(pe, wnT_ready, n - 1)
                for k in range(2):
                    i = pe.transpose(bank(4 + s % 2)[:, k * HALF:(k + 1) * HALF],
                                     wn[s % 2][0:HALF, k * D:(k + 1) * D], ident[0:HALF, 0:HALF])
                i.then_inc(wt_ps, 1)

            pe.wait_ge(weights2_in, 16)
            pe.matmul(bank(6)[:, 0:SEG], w("wr"), w("post"), start=True, stop=True)
            for k, key in enumerate(("wq", "wk", "wvp")):
                i = pe.matmul(bank(6)[:, 32 + 2 * k:33 + 2 * k], w(key), w("beta"), start=True, stop=True)
            i.then_inc(setup_mm, 1)
            staged(pe, SEG, [(xt, 0), (conv, 1), (wt, 3)])

            pe.wait_ge(wnT_ready, SEG)
            pe.wait_ge(wqkv_ready, 1)
            pe.wait_ge(consts, 2)

            def q_proj(n, s):
                after(pe, qr_ready, n - 3)
                pe.matmul(bank(s % 4), w("wq"), cols(wnT, n), start=True, stop=True).then_inc(q_ps, 1)

            staged(pe, CHUNKS, [(q_proj, 0)])
            pe.wait_ge(qr_ready, CHUNKS)
            pe.wait_ge(win_ready, 1)

            def bd(c, g):
                after(pe, bdt_ready, 2 * c + g - 1)
                o = bank(4 * g, 4)
                rows_g = slice(g * 64, g * 64 + 64)
                q = qr.rearrange("p (b i) -> p i b", i=SEG)
                for i in range(SEG):
                    t0 = SEG - 1 - i
                    for k in range(2):
                        if i + k == SEG:
                            continue
                        b = q[rows_g, i + k, c * BIG:(c + 1) * BIG]
                        m = pe.matmul(o[:, i * BIG:(i + 1) * BIG], window(k, t0)[rows_g], b,
                                      start=(k == 0), stop=(k == 1 or i == SEG - 1))
                m.then_inc(bd_ps, 1)

            for c in range(POSP // BIG):
                for g in range(GROUPS):
                    bd(c, g)

            def k_proj(n, s):
                after(pe, vt_ready, n)
                pe.matmul(bank(0), w("wk"), cols(wnT, n), start=True, stop=True).then_inc(k_ps, 1)

            def ac(n, s):
                pe.wait_ge(k_sb, n + 1)
                pe.wait_ge(qb_dve, n + 1)
                pe.wait_ge(qb_act, n + 1)
                after(pe, scores, n)
                for g in range(GROUPS):
                    rg = slice(g * 64, g * 64 + 64)
                    for b in range(CB):
                        i = pe.matmul(bank(1 + g)[:, b * SEG:(b + 1) * SEG], Qb[s % 2][rg, b * 128:(b + 1) * 128],
                                      Kt[s % 2][rg, b * SEG:(b + 1) * SEG], start=True, stop=True)
                i.then_inc(ac_ps, 1)

            def v_proj(n, s):
                pe.wait_ge(k_sb, n + 1)
                pe.matmul(bank(0), w("wv"), cols(wnT, n), start=True, stop=True).then_inc(v_ps, 1)

            def pv(n, s):
                pe.wait_ge(pt_ready, n + 1)
                pe.wait_ge(vb_ready, n + 1)
                after(pe, h1_ready, n)
                for g in range(GROUPS):
                    for b in range(CB):
                        i = pe.matmul(bank(3)[g * 64:g * 64 + 64, b * SEG:(b + 1) * SEG],
                                      Vb[:, (g * CB + b) * 64:(g * CB + b + 1) * 64],
                                      PT[s % 2][:, (g * CB + b) * SEG:(g * CB + b + 1) * SEG], start=True, stop=True)
                i.then_inc(pv_ps, 1)

            def wo(n, s):
                pe.wait_ge(at_ready, n + 1)
                for t in range(TILES):
                    i = pe.matmul(bank(3)[:, t * D:(t + 1) * D], at[:, t * 128:(t + 1) * 128], w("wo"), start=True, stop=True)
                i.then_inc(wo_ps, 1)

            def xft(n, s):
                pe.wait_ge(xf_ready, n + 1)
                after(pe, z_added, n)
                for t in range(TILES):
                    i = pe.transpose(bank(4)[:, t * 128:(t + 1) * 128], xf[s % 2][:, t * D:(t + 1) * D], ident)
                i.then_inc(xft_ps, 1)

            def first_products(n, s):
                pe.wait_ge(xft_sb, n + 1)
                after(pe, slot_ready, n)
                for t in range(TILES):
                    i = pe.matmul(bank(5)[:, t * E:(t + 1) * E], xfT[:, t * 128:(t + 1) * 128], w("gate"), start=True, stop=True)
                i.then_inc(logit_ps, 1)
                after(pe, uc_ready, n)
                for t in range(0, TILES, 2):
                    o = bank(6 + t // 2)[:, 0:4 * IH]
                    pe.matmul(o, onesb[0:3, :], b1sh[0:3, :].unsqueeze(1).to_broadcast([3, 2, 2 * IH]), start=True, stop=False)
                    for k in range(2):
                        i = pe.matmul(o[:, k * 2 * IH:(k + 1) * 2 * IH], xfT[:, (t + k) * 128:(t + k + 1) * 128], w("ws1"),
                                      start=False, stop=(k == 1))
                i.then_inc(hs_ps, 1)

            def ranks(n, s):
                pe.wait_ge(both_ready, n + 1)
                a = both[s % 2]
                o = bank(5)[:, 64:64 + TILES * E]
                pe.matmul(o, trib, a, start=True, stop=False)
                pe.matmul(o, onesb, seen[s % 2].unsqueeze(1).to_broadcast([128, TILES, E]), start=False, stop=False)
                for t in range(TILES - 1):
                    k = TILES - 1 - t
                    i = pe.matmul(o[:, (t + 1) * E:], onesb, a[:, t * E:(t + 1) * E].unsqueeze(1).to_broadcast([128, k, E]),
                                  start=False, stop=(t == TILES - 2))
                i.then_inc(rank_ps, 1)

            def turn_t(n, s):
                pe.wait_ge(ts_ready, n + 1)
                for t in range(TILES):
                    i = pe.transpose(bank(4)[0:IH, t * 128:(t + 1) * 128], uc[:, t * IH:(t + 1) * IH], ident)
                i.then_inc(tt_ps, 1)

            def z_products(n, s):
                pe.wait_ge(tt_sb, n + 1)
                for t in range(TILES):
                    i = pe.matmul(bank(4)[:, t * D:(t + 1) * D], tT[0:IH + 1, t * 128:(t + 1) * 128], w("ws2")[0:IH + 1],
                                  start=True, stop=True)
                i.then_inc(z_ps, 1)

            pe.wait_ge(bdt_ready, 2 * POSP // BIG)
            pe.wait_ge(params_ready, 1)
            pe.wait_ge(b1sh_in, 16)
            staged(pe, CHUNKS, [(k_proj, 0), (ac, 0), (v_proj, 0), (ranks, 3), (pv, 1), (turn_t, 3), (wo, 1), (z_products, 3),
                                (xft, 2), (first_products, 2)], 2)

            pe.wait_ge(seen_ready, CHUNKS)
            pe.matmul(bank(0)[:, 0:E], onesb, seen[CHUNKS % 2], start=True, stop=True)
            pe.matmul(bank(0)[0:E, 32:33], seen[CHUNKS % 2], onesb[:, 0:1], start=True, stop=True).then_inc(counts_ps, 1)
            pe.wait_ge(prep, 3)
            pe.matmul(bank(0)[0:E, 64:65], w("tri16")[0:E], cnt[0:E, 2:3], start=True, stop=True).then_inc(prep_mm, 1)
            pe.wait_ge(tri_scaled, 1)
            pe.matmul(bank(4)[:, 0:E], ones1[0:E, :], scaled16[0:E], start=True, stop=True).then_inc(delta_ps, 1)
            pe.wait_ge(prep, 5)
            pe.matmul(bank(0)[0:1, 128:128 + ETILES], ones1[0:E, 0:1], cmp[0:E], start=True, stop=True)
            pe.matmul(bank(1)[0:1, 0:ETILES], cnt[0:E, 2:3], cmp[0:E], start=True, stop=True).then_inc(prep_mm, 1)

            pe.wait_ge(map_ready, 1)
            pe.wait_ge(w1_in, 16)
            pe.wait_ge(w2_scaled, 1)
            pe.wait_ge(b1e_in, 16)

            def xet(n, s):
                pe.wait_ge(xe_in[s % 4], landed(n, s, 4))
                after(pe, xet_sb, n - 1)
                pe.transpose(bank(s % 2)[:, 0:128], xe[s % 4], ident).then_inc(xet_ps, 1)

            def he(n, s):
                e = pe.value_load(tile_expert(n), min_val=0, max_val=E - 1)
                pe.wait_ge(xet_sb, n + 1)
                after(pe, ue_ready, n - 1)
                o = bank(2 + s % 2)[:, 0:2 * IH]
                pe.matmul(o, onesb[0:3, :], b1e[0:3, bass.ds(e * (2 * IH), 2 * IH)], start=True, stop=False)
                pe.matmul(o, xeT[s % 2], w1s[:, bass.ds(e * (2 * IH), 2 * IH)], start=False, stop=True).then_inc(he_ps, 1)

            def tet(n, s):
                pe.wait_ge(te_ready, n + 1)
                after(pe, tet_sb, n - 1)
                pe.transpose(bank(4 + s % 2)[0:IH, 0:128], te[s % 2], ident).then_inc(tet_ps, 1)

            def yt(n, s):
                e = pe.value_load(tile_expert(n), min_val=0, max_val=E - 1)
                pe.wait_ge(tet_sb, n + 1)
                after(pe, ye_ready, n - 1)
                pe.matmul(bank(6 + s % 2)[:, 0:D], teT[s % 2][0:IH + 1, :], w2s[0:IH + 1, bass.ds(e * D, D)],
                          start=True, stop=True).then_inc(ye_ps, 1)

            staged(pe, ETILES, [(xet, 0), (he, 1), (tet, 2), (yt, 3)])

        @block.vector
        def _(dve):
            dve.memset(tT[96:97, :], 1.0)
            dve.wait_ge(weights_in, 16)
            dve.wait_ge(rows_in, 16)
            dve.reciprocal(recip_ks, r("kscale")).then_inc(dve_setup, 1)
            dve.wait_ge(dve_setup, 1)
            dve.tensor_scalar(conv_scaled, conv_scaled, recip_ks, None, ALU.mult).then_inc(conv_ready, 1)
            raw = par[:, :, 3:5]
            dve.scalar_tensor_tensor(absraw.rearrange("p (e f) -> p e f", f=2), raw, -1.0, raw, ALU.mult, ALU.max).then_inc(params_abs, 1)
            dve.tensor_scalar(maxraw.rearrange("p (e f) -> p e f", f=2), raw, 0.0, None, ALU.max).then_inc(params_abs, 1)
            dve.tensor_scalar(nalpha, par[:, :, 0], -1.0, None, ALU.mult)
            dve.tensor_copy(alpha, par[:, :, 0])
            dve.tensor_copy(shift_p, par[:, :, 2])
            dve.wait_ge(params_log, 2)
            dve.tensor_tensor(clamp, maxraw, absraw, ALU.add).then_inc(dve_setup, 1)
            dve.wait_ge(dve_setup, 2)
            dve.tensor_scalar(nclamp, clamp, -1.0, None, ALU.mult)
            dve.wait_ge(weights2_in, 16)
            dve.tensor_scalar(w("ws2")[0:IH], w("ws2")[0:IH], par[0:IH, E, 1:2], None, ALU.mult).then_inc(params_ready, 1)
            dve.wait_ge(setup_mm, 1)
            dve.tensor_tensor(wrdiff, w("rwb"), w("rrb"), ALU.subtract)
            dve.tensor_copy(bk, bank(6)[:, 34:35])
            dve.tensor_copy(bv, bank(6)[:, 36:37])
            dve.tensor_tensor(qbias, bank(6)[:, 32:33], w("rrb"), ALU.add).then_inc(qbias_ready, 1)
            for key in ("wq", "wk", "wv"):
                i = dve.tensor_scalar(w(key), w(key), w("gamma"), None, ALU.mult)
            i.then_inc(wqkv_ready, 1)
            dve.wait_ge(consts, 1)
            dve.wait_ge(qbias_ready, 1)
            a1, a2 = (t.rearrange("p (q t) -> p q t", q=QUADS) for t in (win1, win2))
            for k in range(QUADS):
                m = w("qmask", k, k + 1)
                dve.tensor_scalar(a1[:, k, 0:SEG], bank(6)[:, 0:SEG], m, None, ALU.mult)
                dve.tensor_scalar(a2[:, k, SEG + 1:], bank(6)[:, 0:SEG - 2], m, None, ALU.mult)
                i = dve.tensor_scalar(qmb[:, k:k + 1], wrdiff, m, None, ALU.mult)
            i.then_inc(win_src, 1)
            dve.wait_ge(win_src, 1)
            for k in range(QUADS):
                for a, dst, first, count in ((a1, QV[:, 0:SEG * 128], 0, SEG), (a2, QV[:, SEG * 128:], 0, 16), (a2, PP, 16, 16)):
                    i = dve.tensor_copy(dst.rearrange("p (t q j) -> p q t j", q=QUADS, j=SEG)[:, k], slide(a[:, k], first, count))
            i.then_inc(win_ready, 1)

            def reduce_args(n, s):
                p = slice(0, HALF)
                v, k, q = va[s % 2][p], ka[s % 2][p], ra[s % 2][p]
                dve.wait_ge(conv_ps, n + 1)
                dve.tensor_tensor(v.rearrange("p (s d) -> p s d", s=2), bank(2 + s % 2)[p, 0:2 * D].rearrange("p (s d) -> p s d", s=2),
                                  r("cbias")[p].unsqueeze(1).to_broadcast([HALF, 2, D]), ALU.add).then_inc(biased, 1)
                dve.wait_ge(biased, n + 1)
                dve.tensor_scalar(k, v, INV_TWO_PI, MAGIC, ALU.mult, ALU.add).then_inc(rounded, 1)
                dve.wait_ge(rounded, n + 1)
                dve.tensor_scalar(k, k, MAGIC, None, ALU.subtract).then_inc(multiple, 1)
                dve.wait_ge(multiple, n + 1)
                after(dve, cosine, n - 1)
                dve.scalar_tensor_tensor(v, k, -TWO_PI_HI, v, ALU.mult, ALU.add).then_inc(reduced_hi, 1)
                dve.wait_ge(reduced_hi, n + 1)
                dve.scalar_tensor_tensor(q, k, -TWO_PI_LO, v, ALU.mult, ALU.add).then_inc(reduced, 1)

            def stats(n, s):
                p = slice(0, HALF)
                dve.wait_ge(cosine, n + 1)
                for k in range(2):
                    i = dve.bn_stats(st[p, 6 * k:6 * k + 6], ca[s % 4][p, k * D:(k + 1) * D])
                i.then_inc(stats_a, 1)
                alone(dve, stats_a, n + 1)
                for k in range(2):
                    i = dve.bn_aggr(mv[s % 4][p, 2 * k:2 * k + 2], st[p, 6 * k:6 * k + 6])
                i.then_inc(mv_a, 1)
                dve.wait_ge(mv_a, n + 1)
                after(dve, rr_a, n - 1)
                m = mv[s % 4][p].rearrange("p (s k) -> p s k", s=2)
                o = pw[s % 2][p].rearrange("p (s k) -> p s k", s=2)
                c = 1 / COS_NORM ** 2
                dve.tensor_scalar(o[:, :, 0], m[:, :, 1], c * EPS, None, ALU.add)
                dve.tensor_scalar(o[:, :, 1], m[:, :, 1], 1 + EPS, c * EPS * EPS, ALU.mult, ALU.add).then_inc(pw_a, 1)

            def norms(n, s):
                p = slice(0, HALF)
                dve.wait_ge(rr_a, n + 1)
                m, q = mv[s % 4][p].rearrange("p (s k) -> p s k", s=2), rr[s % 4][p].rearrange("p (s k) -> p s k", s=2)
                after(dve, ha_ready, n - 1)
                o = rs[s % 2][p]
                dve.tensor_scalar(o[:, 0:2], q[:, :, 0], COS_NORM, None, ALU.add)
                dve.scalar_tensor_tensor(o[:, 2:4], m[:, :, 0], -1.0, q[:, :, 0], ALU.mult, ALU.mult).then_inc(rs_a, 1)
                after(dve, wt_ps, n - 1)
                for k in range(2):
                    i = dve.tensor_scalar(wn[s % 2][p, k * D:(k + 1) * D], ca[s % 4][p, k * D:(k + 1) * D], m[:, k, 0:1], q[:, k, 1:2],
                                          ALU.subtract, ALU.mult)
                i.then_inc(wn_a, 1)

            staged(dve, SEG, [(reduce_args, 0), (stats, 1), (norms, 2)])

            for q in ha_stored:
                dve.wait_ge(q, 2 * 16 * SEG // 4)
            dve.wait_ge(pads, 17)
            dve.wait_ge(b1_stored, 16)
            for n in range(2 * POSP // BIG):
                g, c = n % 2, n // 2
                dve.wait_ge(bd_ps, n + 1)
                o = bdt[:, (g * POSP + c * BIG) * SEG:(g * POSP + (c + 1) * BIG) * SEG]
                dve.transpose(o, bank(4 * g, 4).rearrange("p (i b) -> p b i", i=SEG)).then_inc(bdt_ready, 1)

            dve.wait_ge(params_ready, 1)
            dve.wait_ge(win_ready, 1)

            def q_expand(n, s):
                after(dve, ac_ps, n - 1)
                o = Qb[s % 2].rearrange("p (b q i) -> p q b i", q=QUADS, i=SEG)
                q = cols(qr, n).rearrange("p (b i) -> p b i", i=SEG)
                for k in (0, 1):
                    i = dve.tensor_scalar(o[:, k], q, w("qmask", k, k + 1), qmb[:, k:k + 1], ALU.mult, ALU.add)
                i.then_inc(qb_dve, 1)

            def v_turn(n, s):
                dve.wait_ge(v_ps, n + 1)
                after(dve, vb_ready, n - 1)
                dve.transpose(Vt[s % 2], bank(0)).then_inc(vt_ready, 1)

            def add_scores(n, s):
                dve.wait_ge(ac_ps, n + 1)
                dve.tensor_tensor(S[s % 2].rearrange("p (g c) -> p g c", g=GROUPS), bank(1, 2).rearrange("p (g c) -> p g c", g=GROUPS),
                                  bchunk(n), ALU.add).then_inc(scores, 1)
                dve.wait_ge(scores, n + 1)
                after(dve, shifted, n - 1)
                dve.tensor_reduce(mx[s % 2].rearrange("p (g b) -> p g b", g=GROUPS), scores4(s), AX, ALU.max).then_inc(max_ready, 1)

            def sum_exps(n, s):
                dve.wait_ge(exped, n + 1)
                dve.tensor_reduce(sm.rearrange("p (g b) -> p g b", g=GROUPS), scores4(s), AX, ALU.add).then_inc(sums, 1)
                dve.wait_ge(sums, n + 1)
                after(dve, probs, n - 1)
                dve.reciprocal(rc[s % 2], sm).then_inc(rc_ready, 1)

            def turn_p(n, s):
                dve.wait_ge(probs, n + 1)
                after(dve, pv_ps, n - 1)
                dve.transpose(PT[s % 2], S[s % 2]).then_inc(pt_ready, 1)

            def add_h1(n, s):
                dve.wait_ge(wo_ps, n + 1)
                dve.wait_ge(res_in[s % 2], landed(n, s, 2))
                dve.tensor_tensor(cols(wnT, n), bank(3), res[s % 2], ALU.add).then_inc(h1_ready, 1)
                dve.wait_ge(h1_ready, n + 1)
                for t in range(TILES):
                    i = dve.bn_stats(st2[:, t * 6:t * 6 + 6], cols(wnT, n * TILES + t, D))
                i.then_inc(stats_d, 1)
                alone(dve, stats_d, n + 1)
                for t in range(TILES):
                    i = dve.bn_aggr(mv2[s % 2][:, 2 * t:2 * t + 2], st2[:, t * 6:t * 6 + 6])
                i.then_inc(mv_d, 1)

            def norm_ffn(n, s):
                dve.wait_ge(rstd_d, n + 1)
                if not isinstance(n, int) or n >= 2:
                    dve.wait_ge(sent[s % 2], (n - s % 2) * 64)
                for t in range(TILES):
                    i = dve.tensor_scalar(xf[s % 2][:, t * D:(t + 1) * D], cols(wnT, n * TILES + t, D), mv2[s % 2][:, 2 * t:2 * t + 1],
                                          rstd_t[s % 2][:, t:t + 1], ALU.subtract, ALU.mult)
                i.then_inc(xf_ready, 1)

            RT = 6

            def router(n, s):
                def step(i):
                    i.then_inc(rt, 1)

                def done(k):
                    alone(dve, rt, n * RT + k)

                dve.wait_ge(logit_ps, n + 1)
                l3 = lg.rearrange("p (t e) -> p t e", e=E)
                step(dve.tensor_tensor(l3, bank(5)[:, 0:TILES * E].rearrange("p (t e) -> p t e", e=E),
                                       r("gateb").unsqueeze(1).to_broadcast([128, TILES, E]), ALU.add))
                done(1)
                for t in range(TILES):
                    i = dve.max(m8[:, t * 8:t * 8 + 8], lg[:, t * E:(t + 1) * E])
                step(i)
                done(2)
                for t in range(TILES):
                    i = dve.max_index(ix8.bitcast(U32)[:, t * 8:t * 8 + 8], m8[:, t * 8:t * 8 + 8], lg[:, t * E:(t + 1) * E])
                step(i)
                m3 = m8.rearrange("p (t k) -> p t k", k=8)
                after(dve, ed_ready, n)
                dve.tensor_tensor(dd, m3[:, :, 1], m3[:, :, 0], ALU.subtract).then_inc(dd_ready, 1)
                done(3)
                step(dve.tensor_copy(ixf.rearrange("p (k t) -> p t k", k=2), ix8.bitcast(U32).rearrange("p (t k) -> p t k", k=8)[:, :, 0:2]))
                done(4)
                o4 = oh.rearrange("p (k t e) -> p k t e", k=2, e=E)
                i3 = r("iota16").unsqueeze(1).to_broadcast([128, TILES, E])
                for k in range(2):
                    i = dve.tensor_tensor(o4[:, k], i3, ixf[:, k * TILES:(k + 1) * TILES].unsqueeze(2).to_broadcast([128, TILES, E]), ALU.is_equal)
                step(i)
                done(5)
                after(dve, rank_ps, n - 1)
                dve.tensor_tensor(both[s % 2], oh[:, 0:TILES * E], oh[:, TILES * E:], ALU.add).then_inc(both_ready, 1)
                dve.wait_ge(both_ready, n + 1)
                step(dve.tensor_reduce(tsum, both[s % 2].rearrange("p (t e) -> p e t", e=E), AX, ALU.add))
                done(6)
                after(dve, rank_ps, n)
                after(dve, seen_ready, n)
                dve.tensor_tensor(seen[(s + 1) % 2], seen[s % 2], tsum, ALU.add).then_inc(seen_ready, 1)

            def weights_of(n, s):
                dve.wait_ge(ed_ready, n + 1)
                dve.tensor_scalar(ed, ed, 1.0, None, ALU.add).then_inc(ed_plus, 1)
                dve.wait_ge(ed_plus, n + 1)
                dve.reciprocal(cols(wts, n, 2 * TILES), ed).then_inc(wts_ready, 1)

            def slots_of(n, s):
                def done(k):
                    dve.wait_ge(rt2, n * 3 + k)

                dve.wait_ge(rank_ps, n + 1)
                dve.tensor_tensor(rb.rearrange("p (t e) -> p t e", e=E), bank(5)[:, 64:64 + TILES * E].rearrange("p (t e) -> p t e", e=E),
                                  r("ebase").unsqueeze(1).to_broadcast([128, TILES, E]), ALU.add).then_inc(rt2, 1)
                done(1)
                dve.tensor_tensor(ohr.rearrange("p (k c) -> p k c", k=2), oh.rearrange("p (k c) -> p k c", k=2),
                                  rb.unsqueeze(1).to_broadcast([128, 2, TILES * E]), ALU.mult).then_inc(rt2, 1)
                done(2)
                dve.tensor_reduce(slf, ohr.rearrange("p (kt e) -> p kt e", e=E), AX, ALU.add).then_inc(rt2, 1)
                done(3)
                dve.tensor_copy(cols(slots, n, 2 * TILES), slf)
                dve.tensor_copy(cols(chosen, n, 2 * TILES), ixf)
                dve.tensor_copy(sl32[s % 2].bitcast(I32), slf).then_inc(slot_ready, 1)

            def swiglu_a(n, s):
                hs = bank(6, 2).rearrange("p (a c) -> p a c", a=2)[:, :, 0:4 * IH].rearrange("p a (k u h) -> p a k u h", k=2, u=2)
                gv, uv = (t.rearrange("p (a k h) -> p a k h", a=2, k=2) for t in (gc, uc))
                dve.wait_ge(hs_ps, n + 1)
                for a in range(2):
                    i = dve.tensor_scalar(gv[:, a], hs[:, a, :, 0], clamp[:, 2 * E:2 * E + 1], nclamp[:, 2 * E:2 * E + 1], ALU.min, ALU.max)
                i.then_inc(gc_ready, 1)
                after(dve, tt_ps, n)
                for a in range(2):
                    i = dve.tensor_scalar(uv[:, a], hs[:, a, :, 1], clamp[:, 2 * E + 1:2 * E + 2], nclamp[:, 2 * E + 1:2 * E + 2], ALU.min, ALU.max)
                i.then_inc(uc_ready, 1)

            def swiglu_b(n, s):
                dve.wait_ge(eg_act, n + 1)
                dve.tensor_scalar(eg, eg, 1.0, None, ALU.add).then_inc(eg_dve, 1)
                dve.wait_ge(eg_dve, n * 3 + 1)
                dve.reciprocal(eg, eg).then_inc(eg_dve, 1)
                dve.wait_ge(eg_dve, n * 3 + 2)
                dve.tensor_tensor(eg, gc, eg, ALU.mult).then_inc(eg_dve, 1)
                dve.wait_ge(eg_dve, n * 3 + 3)
                dve.scalar_tensor_tensor(uc, uc, par[:, E, 2:3], eg, ALU.add, ALU.mult).then_inc(ts_ready, 1)

            def add_z(n, s):
                dve.wait_ge(z_ps, n + 1)
                dve.tensor_tensor(cols(wnT, n), bank(4), cols(wnT, n), ALU.add).then_inc(z_added, 1)

            staged(dve, CHUNKS, [(q_expand, 0), (swiglu_a, 3), (router, 3), (add_scores, 0), (v_turn, 0), (turn_p, 1),
                                 (swiglu_b, 3), (slots_of, 3), (weights_of, 3), (sum_exps, 0), (add_h1, 1), (add_z, 3),
                                 (norm_ffn, 2)], 2)

            dve.wait_ge(zeros_ready, 1)
            dve.wait_ge(counts_ps, 1)
            dve.wait_ge(w2_in, 16)
            dve.tensor_tensor(w2s[0:IH].rearrange("p (e d) -> p e d", e=E), w2s[0:IH].rearrange("p (e d) -> p e d", e=E),
                              par[0:IH, 0:E, 1].unsqueeze(2).to_broadcast([IH, E, D]), ALU.mult).then_inc(w2_scaled, 1)
            dve.memset(ones1, 1.0)
            for t in teT:
                dve.memset(t[96:97, :], 1.0)
            dve.tensor_tensor(cnt1[0:1, 0:E].bitcast(I32), bank(0)[0:1, 0:E], r("ebase")[0:1], ALU.add)
            ci = cnt.bitcast(I32)
            dve.tensor_scalar(ci[0:E, 0:1], bank(0)[0:E, 32:33], 127.0, None, ALU.add).then_inc(prep, 1)
            dve.wait_ge(prep, 1)
            dve.tensor_scalar(ci[0:E, 1:2], ci[0:E, 0:1], 7, None, ALU.arith_shift_right).then_inc(prep, 1)
            dve.wait_ge(prep, 2)
            dve.tensor_copy(cnt[0:E, 2:3], ci[0:E, 1:2]).then_inc(prep, 1)
            dve.wait_ge(prep, 3)
            dve.tensor_scalar(scaled16[0:E], w("stri16")[0:E], cnt[0:E, 2:3], 128.0, ALU.mult, ALU.mult).then_inc(tri_scaled, 1)
            dve.wait_ge(prep_mm, 1)
            dve.tensor_copy(cnt[0:E, 3:4], bank(0)[0:E, 64:65]).then_inc(prep, 1)
            dve.wait_ge(prep, 4)
            dve.tensor_scalar(cmp[0:E], w("iota")[0:E], cnt[0:E, 3:4], None, ALU.is_ge).then_inc(prep, 1)
            dve.wait_ge(prep_mm, 2)
            ex, first, use, tmp = (rowf[0:1, k * ETILES:(k + 1) * ETILES] for k in range(4))
            dve.tensor_copy(ex, bank(0)[0:1, 128:128 + ETILES])
            dve.tensor_tensor(first, w("iota")[0:1], bank(1)[0:1, 0:ETILES], ALU.subtract).then_inc(prep, 1)
            dve.wait_ge(prep, 6)
            dve.tensor_scalar(use, ex, float(E), None, ALU.is_lt)
            dve.tensor_scalar(tmp, ex, float(REGION), -float(DUMMY), ALU.mult, ALU.add).then_inc(prep, 1)
            dve.wait_ge(prep, 7)
            dve.scalar_tensor_tensor(tmp, first, 128.0, tmp, ALU.mult, ALU.add).then_inc(prep, 1)
            dve.wait_ge(prep, 8)
            dve.tensor_tensor(tmp, tmp, use, ALU.mult)
            dve.tensor_tensor(rowe[0:1].bitcast(I32), ex, use, ALU.mult).then_inc(prep, 1)
            dve.wait_ge(prep, 9)
            dve.tensor_scalar(rowi[0:1].bitcast(I32), tmp, float(DUMMY), None, ALU.add).then_inc(map_ready, 1)
            dve.wait_ge(map_ready, 1)
            dve.wait_ge(delta_ps, 1)
            dve.tensor_tensor(delta, bank(4)[:, 0:E], r("ebase"), ALU.subtract).then_inc(looked, 1)
            dve.wait_ge(looked, 1)
            l3 = look.rearrange("p (n e) -> p n e", e=E)
            dve.wait_ge(slot_ready, CHUNKS)
            dve.tensor_tensor(l3, r("iota16").unsqueeze(1).to_broadcast([128, 2 * TOKT, E]),
                              chosen.unsqueeze(2).to_broadcast([128, 2 * TOKT, E]), ALU.is_equal).then_inc(looked, 1)
            dve.wait_ge(looked, 2)
            dve.tensor_tensor(l3, l3, delta.unsqueeze(1).to_broadcast([128, 2 * TOKT, E]), ALU.mult).then_inc(looked, 1)
            dve.wait_ge(looked, 3)
            dve.tensor_reduce(chosen, l3, AX, ALU.add).then_inc(looked, 1)
            dve.wait_ge(looked, 4)
            dve.tensor_tensor(yrow, chosen, slots, ALU.add).then_inc(looked, 1)

            def clip_e(n, s):
                e = dve.value_load(tile_expert(n), min_val=0, max_val=E - 1)
                dve.wait_ge(he_ps, n + 1)
                h = bank(2 + s % 2)
                dve.tensor_scalar(ge[s % 2], h[:, 0:IH], clamp[:, bass.ds(2 * e, 1)], nclamp[:, bass.ds(2 * e, 1)], ALU.min, ALU.max).then_inc(ge_ready, 1)
                dve.tensor_scalar(ue[s % 2], h[:, IH:2 * IH], clamp[:, bass.ds(2 * e + 1, 1)], nclamp[:, bass.ds(2 * e + 1, 1)],
                                  ALU.min, ALU.max).then_inc(ue_ready, 1)

            def gate_e(n, s):
                e = dve.value_load(tile_expert(n), min_val=0, max_val=E - 1)
                dve.wait_ge(ee_ready, n + 1)
                dve.tensor_tensor(ee[s % 2], ge[s % 2], ee[s % 2], ALU.mult).then_inc(m_ready, 1)
                dve.wait_ge(m_ready, n + 1)
                after(dve, tet_ps, n - 1)
                dve.scalar_tensor_tensor(te[s % 2], ue[s % 2], shift_p[:, bass.ds(e, 1)], ee[s % 2], ALU.add, ALU.mult).then_inc(te_ready, 1)

            def y_copy(n, s):
                dve.wait_ge(ye_ps, n + 1)
                if not isinstance(n, int) or n >= 4:
                    dve.wait_ge(ye_out[s % 4], (n - s % 4) * 4)
                dve.tensor_copy(ye[s % 4], bank(6 + s % 2)[:, 0:D]).then_inc(ye_ready, 1)

            staged(dve, ETILES, [(clip_e, 0), (gate_e, 1), (y_copy, 2)])

            def indices(n, s):
                after(dve, f_ready, n - 3)
                dve.tensor_copy(idx[s % 4], slots_kt(n, s)).then_inc(idx_ready, 1)

            def slots_kt(n, s):
                v = yrow.rearrange("p (c k t) -> p c t k", k=2, t=TILES)
                return v[:, n // TILES, s % 4] if isinstance(n, int) else v[:, bass.ds((n - s % 4) // TILES, 1), s % 4].rearrange("p o k -> p (o k)")

            def wts_k(n, s, k):
                at0 = (n - s % 4) * 2 + k * TILES + s % 4
                return wts[:, at0:at0 + 1] if isinstance(n, int) else wts[:, bass.ds(at0, 1)]

            def combine(n, s):
                dve.wait_ge(g_in[s % 4], landed2(n, s))
                if not isinstance(n, int) or n >= 4:
                    dve.wait_ge(stored[s % 4], (n - s % 4) * 4)
                dve.scalar_tensor_tensor(of[s % 4], g0[s % 4], wts_k(n, s, 0), cols(wnT, n, D), ALU.mult, ALU.add).then_inc(f_half, 1)
                dve.wait_ge(f_half, n + 1)
                dve.scalar_tensor_tensor(of[s % 4], g1[s % 4], wts_k(n, s, 1), of[s % 4], ALU.mult, ALU.add).then_inc(f_ready, 1)

            def landed2(n, s):
                return (n - s % 4) * 8 + 32

            dve.wait_ge(wts_ready, CHUNKS)
            dve.wait_ge(looked, 5)
            dve.wait_ge(z_added, CHUNKS)
            staged(dve, TOKT, [(indices, 0), (combine, 3)])


def kernel(**inputs):
    import concourse.bacc as bacc
    from concourse.bass_utils import run_bass_kernel_spmd

    f = np.float32
    a = {k: np.asarray(v) for k, v in inputs.items()}
    p = "L0_attn_"
    perm = np.array([(2 * q + g) * DH + d for g in range(GROUPS) for q in range(QUADS) for d in range(DH)])
    wide = np.zeros((128, W_ALL), f)

    def put(key, v):
        v = np.asarray(v)
        wide[:v.shape[0], W_AT[key][0]:W_AT[key][1]] = v

    ck = a["L0_tok_kernel"]
    put("conv01", ck[0:2].reshape(2 * CIN, D))
    put("conv2", ck[2])
    wide[CIN:, W_AT["conv0"][0]:W_AT["conv0"][1]] = ck[0]
    put("conv12", ck[1:3].reshape(2 * CIN, D))
    qkv = a[p + "Wqkv"]
    put("wq", qkv[0:D][perm].T)
    put("wk", qkv[D:2 * D][perm].T)
    put("wv", qkv[2 * D:].T)
    put("wvp", qkv[2 * D:][perm].T)
    put("wo", a[p + "Wo"].T[perm])
    put("wr", a[p + "Wr"][perm].T)
    pos = np.arange(SEG - 1, -1, -1, dtype=f)
    inv = f(1.0) / (f(10000.0) ** (np.arange(0, D, 2, dtype=f) / f(D)))
    ang = (pos[:, None] * inv[None, :]).astype(f)
    put("post", np.concatenate([np.sin(ang), np.cos(ang)], axis=1).T)
    put("ident", np.eye(128))
    put("rwb", a[p + "r_w_bias"].reshape(D)[perm][:, None])
    put("rrb", a[p + "r_r_bias"].reshape(D)[perm][:, None])
    put("gamma", a[p + "ln_gamma"][:, None])
    put("beta", a[p + "ln_beta"][:, None])
    m = "L0_ffn_"

    def halves(t):
        return np.concatenate([t[..., 0::2], t[..., 1::2]], axis=-1)

    put("gate", a[m + "gate_w"])
    put("ws1", halves(a[m + "shared_w1"]))
    put("ws2", np.concatenate([a[m + "shared_w2"], a[m + "shared_b2"][None]]))
    put("iota", np.tile(np.arange(ETILES, dtype=f), (128, 1)))
    part = np.arange(128)
    put("qmask", (part[:, None] % 64 // DH == np.arange(QUADS)).astype(f))
    put("pmask", (part[:, None] // SEG == np.arange(QUADS)).astype(f))
    put("tri16", np.triu(np.ones((E, E), f)))
    put("stri16", np.triu(np.ones((E, E), f), 1))
    put("pmask3", (part[:3, None] >= np.arange(3)).astype(f))
    act = np.concatenate([a[m + "expert_act"], a[m + "shared_act"][None]])
    rows = np.concatenate([a["L0_tok_bias"], a["L0_tok_kernel_scale"], a[m + "gate_b"], act.reshape(-1),
                           np.arange(E, dtype=f), np.arange(E, dtype=f) * REGION])[None]
    arrays = {
        "x": a["x"].reshape(SEG, WIDTH // 2, 2 * CIN),
        "weights": wide,
        "rows": rows,
        "w1": halves(a[m + "expert_w1"]).transpose(1, 0, 2),
        "w2": np.concatenate([a[m + "expert_w2"], a[m + "expert_b2"][:, None, :]], axis=1).transpose(1, 0, 2),
        "b1": halves(np.concatenate([a[m + "expert_b1"], a[m + "shared_b1"][None]])).reshape(1, -1),
    }
    arrays = {k: np.ascontiguousarray(v, dtype=v.dtype) for k, v in arrays.items()}
    nc = bacc.Bacc("TRN2", target_bir_lowering=False, num_devices=1)
    args = [nc.dram_tensor(k, v.shape, mybir.dt.from_np(v.dtype), kind="ExternalInput").ap() for k, v in arrays.items()]
    out = nc.dram_tensor("out", (POSP, SEG, D), F32, kind="ExternalOutput").ap()
    build(nc, *args, out)
    got = run_bass_kernel_spmd(nc, [arrays], core_ids=[0]).results[0]["out"]
    return np.ascontiguousarray(got[:POS].transpose(1, 0, 2))
```

```python
from contextlib import ExitStack

import numpy as np

import concourse.bass as bass
from concourse import mybir

F32 = mybir.dt.float32
BF16 = mybir.dt.bfloat16
I32 = mybir.dt.int32
U32 = mybir.dt.uint32
ALU = mybir.AluOpType
ACT = mybir.ActivationFunctionType
AX = mybir.AxisListType.X

SEG, WIDTH, CIN, TAPS, D = 32, 256, 64, 3, 128
POS = WIDTH - TAPS + 1
HALF = POS // 2
POSP = 256
HEADS, DH = 8, 16
GROUPS, QUADS = 2, 4
E, IH = 16, 96
CB = 16
CHUNKS = POSP // CB
CC = CB * SEG
TILES = CC // 128
TOKT = SEG * POSP // 128
BIG = 128
REGION = SEG * POSP + 128
DUMMY = E * REGION
ETILES = 2 * TOKT + E
NB1 = (E + 1) * 2 * IH
WIN = 2 * SEG - 1
MAGIC = float(1.5 * 2 ** 23)
TWO_PI_HI = float(np.float32(6.28125))
TWO_PI_LO = float(np.float32(2 * np.pi - 6.28125))
INV_TWO_PI = float(np.float32(1 / (2 * np.pi)))
EPS = 1e-5
COS_NORM = float(np.sqrt(np.float32(2.0 / D)))
SCALE = 1.0 / DH ** 0.5

W_COLS = dict(conv01=D, conv2=D, conv12=D, conv0=D, ident=128, wq=D, wk=D, wv=D, wo=D, wr=D, wvp=D, post=SEG,
              rwb=1, rrb=1, gamma=1, beta=1, gate=E, ws1=2 * IH, ws2=D, iota=ETILES, qmask=QUADS,
              pmask=QUADS, tri16=E, stri16=E, pmask3=3)
W_AT = {}
_at = 0
for _k, _n in W_COLS.items():
    W_AT[_k] = (_at, _at + _n)
    _at += _n
W_ALL = _at
W_EARLY = W_AT['wq'][0]
R_COLS = dict(cbias=D, kscale=1, gateb=E, act=5 * (E + 1), iota16=E, ebase=E)
R_AT = {}
_at = 0
for _k, _n in R_COLS.items():
    R_AT[_k] = (_at, _at + _n)
    _at += _n
R_ALL = _at


def staged(eng, total, stages, unroll=4, head=None):
    lag = max(l for _, l in stages)
    first = lag + (unroll if head is None else head)
    loops = (total - first) // unroll
    last = first + loops * unroll

    def step(j):
        for fn, l in stages:
            if 0 <= j - l < total:
                fn(j - l, (j - l) % unroll)

    for j in range(first):
        step(j)
    if loops > 1:
        with eng.Fori(first, last - unroll + 1, unroll) as at:
            for u in range(unroll):
                for fn, l in stages:
                    n = at + (u - l) if u != l else at
                    fn(n, (first + u - l) % unroll)
    else:
        last = first
    for j in range(last, total + lag):
        step(j)


def after(eng, sem, value):
    if not isinstance(value, int) or value > 0:
        eng.wait_ge(sem, value)


def alone(eng, sem, value):
    if not isinstance(value, int):
        value = eng.snap(eng.to_reg(value))
        eng.wait_ge(sem, 1)
    after(eng, sem, value)


def landed(n, s, ring):
    return (n - s % ring) * (16 // ring) + 16


TW1 = 0
TW2 = TW1 + 2 * IH
TPAR = TW2 + D
TB1 = TPAR + 8
TW = TB1 + IH
STORE_LAG = 18
RING = 8


def build(nc, x, weights, rows, w1, w2, b1, out):
    with ExitStack() as ctx:
        def sb(name, cols, dt=F32):
            return ctx.enter_context(nc.sbuf_tensor(name, [128, cols], dt))[:, :]

        def sem(name):
            return ctx.enter_context(nc.semaphore(name))

        def sems(name, n):
            return [sem(f"{name}{i}") for i in range(n)]

        res_d = nc.dram_tensor("res_d", [POSP, SEG, D], F32, kind="Internal").ap()
        b1s_d = nc.dram_tensor("b1s_d", [3, NB1], BF16, kind="Internal").ap()
        xs_d = nc.dram_tensor("xs_d", [DUMMY + 128, D], F32, kind="Internal").ap()
        ys_d = nc.dram_tensor("ys_d", [ETILES * 128, D], F32, kind="Internal").ap()

        wnT = sb("wnT", POSP * SEG)
        qr = sb("qr", POSP * SEG)
        bdt = sb("bdt", GROUPS * POSP * SEG)
        W = sb("W", W_ALL)
        R = sb("R", R_ALL)
        yrow = sb("yrow", CHUNKS * 2 * TILES, I32)
        onesb = sb("onesb", 128, BF16)
        trib = sb("trib", 128, BF16)
        b1sh = sb("b1sh", 2 * IH, BF16)

        def w(key, a=0, b=None):
            lo, hi = W_AT[key]
            return W[:, lo + a:(hi if b is None else lo + b)]

        def r(key, a=0, b=None):
            lo, hi = R_AT[key]
            return R[:, lo + a:(hi if b is None else lo + b)]

        slots = w("wvp")
        chosen = w("wr")
        wts = w("wq")

        QV = sb("QV", 3 * CB * 128)
        Qb = [QV[:, u * CB * 128:(u + 1) * CB * 128] for u in range(2)]
        Vb = QV[:, 2 * CB * 128:]
        SS = sb("SS", 2 * GROUPS * CC)
        S = [SS[:, u * GROUPS * CC:(u + 1) * GROUPS * CC] for u in range(2)]
        Kb = [sb(f"Kb{u}", GROUPS * CC) for u in range(2)]
        Vt = [sb(f"Vt{u}", CC) for u in range(2)]
        PP = sb("PP", 2 * GROUPS * CC)
        PT = [PP[:, u * GROUPS * CC:(u + 1) * GROUPS * CC] for u in range(2)]
        at = w("conv01", 0, CC)
        res = [sb(f"res{u}", CC) for u in range(2)]
        xf = [bdt[:, u * CC:(u + 1) * CC] for u in range(4)]
        xfT = bdt[:, POSP * SEG:POSP * SEG + CC]
        tT = sb("tT", CC)
        gc = sb("gc", TILES * IH)
        eg = sb("eg", TILES * IH)
        uc = [sb(f"uc{u}", TILES * IH) for u in range(2)]
        small = sb("small", 1300)
        used = [0]

        def tiny(cols):
            used[0] += cols
            return small[:, used[0] - cols:used[0]]

        neg_half = tiny(8)
        half_pi = tiny(1)
        recip_ks = tiny(1)
        conv_scaled = w("conv01", 0, 4 * D)
        bq, bk, bv = tiny(1), tiny(1), tiny(1)
        qbias = tiny(1)
        wrdiff = tiny(1)
        qmb = tiny(QUADS)
        win = bdt[:, 12288:12288 + 2 * QUADS * WIN]
        win1, win2 = win[:, 0:QUADS * WIN], win[:, QUADS * WIN:]
        par = r("act").rearrange("p (e f) -> p e f", f=5)
        absraw, expraw, clamp, nclamp, maxraw = (tiny(2 * (E + 1)) for _ in range(5))
        half_alpha = tiny(1)

        mx = [tiny(GROUPS * CB) for _ in range(2)]
        sm = tiny(GROUPS * CB)
        rc = [tiny(GROUPS * CB) for _ in range(2)]
        st2 = tiny(TILES * 6)
        mv2 = [tiny(TILES * 2) for _ in range(2)]
        vp2 = tiny(TILES)
        rstd_t = [tiny(TILES) for _ in range(2)]
        sl32 = [tiny(2 * TILES) for _ in range(4)]
        alpha, shift_p = tiny(E + 1), tiny(E + 1)
        rt2 = sem("slot_steps")
        b1_tmp = sem("b1_rests")
        lg = tiny(TILES * E)
        m8 = tiny(TILES * 8)
        ix8 = tiny(TILES * 8)
        ixf = tiny(2 * TILES)
        oh = tiny(2 * TILES * E)
        rb = tiny(TILES * E)
        ohr = tiny(2 * TILES * E)
        slf = tiny(2 * TILES)
        dd = tiny(TILES)
        ed = tiny(2 * TILES)
        both = [tiny(TILES * E // 2) for _ in range(2)]
        both = [b.bitcast(BF16) for b in both]
        seen = [tiny(E // 2).bitcast(BF16) for _ in range(2)]
        tsum = tiny(E)

        assert used[0] <= 1300
        def window(k, t0):
            if k == 0:
                return QV[:, t0 * 128:(t0 + 1) * 128]
            return QV[:, (SEG + t0) * 128:(SEG + t0 + 1) * 128] if t0 < 16 else PP[:, (t0 - 16) * 128:(t0 - 15) * 128]

        def slide(v, first, count):
            return bass.AP(tensor=v.tensor, offset=v.offset + first, ap=[v.ap[0], [1, count], [1, SEG]])

        ps = ctx.enter_context(nc.psum_tensor("ps", [128, 8 * 512], F32))[:, :]

        def bank(n, k=1):
            return ps[:, n * 512:(n + k) * 512]

        taken = [0]

        def in_bdt(cols):
            taken[0] += cols
            return bdt[:, taken[0] - cols:taken[0]]

        xin = [in_bdt(128) for _ in range(4)]
        XT = [in_bdt(128) for _ in range(2)]
        va = [in_bdt(2 * D) for _ in range(2)]
        ka = [in_bdt(2 * D) for _ in range(2)]
        ra = [in_bdt(2 * D) for _ in range(2)]
        ca = [in_bdt(2 * D) for _ in range(4)]
        st = in_bdt(12)
        mv = [in_bdt(4) for _ in range(4)]
        pw = [in_bdt(4) for _ in range(2)]
        rr = [in_bdt(4) for _ in range(4)]
        rs = [in_bdt(4) for _ in range(2)]
        wn = [in_bdt(2 * D) for _ in range(2)]
        ha = [in_bdt(2 * D) for _ in range(4)]
        zpad = in_bdt(D)
        b1f = in_bdt(NB1)[0:3]
        b1h = in_bdt(NB1 // 2)[0:3].bitcast(BF16)
        b1t = in_bdt(NB1 // 2)[0:3].bitcast(BF16)
        taken[0] = 4 * CC
        mine = [in_bdt(TW) for _ in range(RING)]
        xeT = [in_bdt(128) for _ in range(2)]
        teT = [in_bdt(128) for _ in range(2)]
        te = [in_bdt(IH) for _ in range(2)]
        cnt = in_bdt(8)
        cmp = in_bdt(ETILES)
        ones1 = in_bdt(128)
        rowi, rowe = in_bdt(ETILES), in_bdt(ETILES)
        scaled16, delta = in_bdt(E), in_bdt(E)
        rowf = in_bdt(4 * ETILES)
        cnt1 = in_bdt(2 * E)
        zeros = in_bdt(D)
        assert taken[0] <= POSP * SEG
        taken[0] = POSP * SEG + CC
        table = in_bdt(E * TW)
        table3 = table.rearrange("p (e c) -> p e c", e=E)
        assert taken[0] <= GROUPS * POSP * SEG
        look = SS[:, 0:2 * TOKT * E]
        taken[0] = 0

        def in_qr(cols):
            taken[0] += cols
            return qr[:, taken[0] - cols:taken[0]]

        xe = [in_qr(D) for _ in range(RING)]
        ye = [in_qr(D) for _ in range(RING)]
        ge, ee, ue = ([in_qr(IH) for _ in range(RING)] for _ in range(3))
        g0 = [in_qr(D) for _ in range(4)]
        g1 = [in_qr(D) for _ in range(4)]
        of = [in_qr(D) for _ in range(4)]
        idx = [in_qr(2).bitcast(I32) for _ in range(4)]

        ident = w("ident")
        weights_in, weights2_in, rows_in, b1_in = sem("weights_in"), sem("weights2_in"), sem("rows_in"), sem("b1_in")
        consts = sem("consts")
        conv_ready = sem("conv_ready")
        setup_mm, rk_ready, wqkv_ready = sem("setup_mm"), sem("rk_ready"), sem("wqkv_ready")
        qbias_ready, win_ready, dve_setup = sem("qbias_ready"), sem("win_ready"), sem("dve_setup")
        params_abs, params_log, params_ready = sem("params_abs"), sem("params_log"), sem("params_ready")
        b1_parts, b1_stored, b1sh_in = sem("b1_parts"), sem("b1_stored"), sem("b1sh_in")
        pads = sem("pads")
        x_in = sems("x_in", 4)
        xt_ps, xt_sb, conv_ps = sem("xt_ps"), sem("xt_sb"), sem("conv_ps")
        biased, arg_steps, reduced = (sem(n) for n in ("biased", "arg_steps", "reduced"))
        absolute, cosine = sem("absolute"), sem("cosine")
        stats_a, mv_a, pw_a, rr_a, rs_a, wn_a = (sem(n) for n in ("stats_a", "mv_a", "pw_a", "rr_a", "rs_a", "wn_a"))
        ha_ready, ha_stored, wt_ps, wnT_ready = sem("ha_ready"), sems("ha_stored", 4), sem("wt_ps"), sem("wnT_ready")
        q_ps, qr_ready, bd_ps, bdt_ready = sem("q_ps"), sem("qr_ready"), sem("bd_ps"), sem("bdt_ready")
        k_ps, k_sb, v_ps, vt_ready, vb_ready = (sem(n) for n in ("k_ps", "k_sb", "v_ps", "vt_ready", "vb_ready"))
        qb_dve, qb_act, ac_ps, scores = sem("qb_dve"), sem("qb_act"), sem("ac_ps"), sem("scores")
        max_ready, shifted, exped, sums, rc_ready, probs, pt_ready = (sem(n) for n in (
            "max_ready", "shifted", "exped", "sums", "rc_ready", "probs", "pt_ready"))
        pv_ps, at_ready, wo_ps = sem("pv_ps"), sem("at_ready"), sem("wo_ps")
        res_in, h1_ready = sems("res_in", 2), sem("h1_ready")
        stats_d, mv_d, vp_d, rstd_d, xf_ready = (sem(n) for n in ("stats_d", "mv_d", "vp_d", "rstd_d", "xf_ready"))
        xft_ps, xft_sb, logit_ps, hs_ps = (sem(n) for n in ("xft_ps", "xft_sb", "logit_ps", "hs_ps"))
        gc_ready, eg_act, eg_dve, uc_ready, ts_ready = (sem(n) for n in (
            "gc_ready", "eg_act", "eg_dve", "uc_ready", "ts_ready"))
        tt_ps, tt_sb, z_ps, z_added = (sem(n) for n in ("tt_ps", "tt_sb", "z_ps", "z_added"))
        win_src, tri_scaled, delta_ps, looked = sem("win_src"), sem("tri_scaled"), sem("delta_ps"), sem("looked")
        rt, ed_plus = sem("router_steps"), sem("ed_plus")
        both_ready, seen_ready, rank_ps, slot_ready, dd_ready, ed_ready, wts_ready = (sem(n) for n in (
            "both_ready", "seen_ready", "rank_ps", "slot_ready", "dd_ready", "ed_ready", "wts_ready"))
        sent = sems("sent", 4)
        experts_in, b1e_in, table_ready = sem("experts_in"), sem("b1e_in"), sem("table_ready")
        table_cleared, mine_ready = sem("table_cleared"), sem("mine_ready")
        zeros_ready, counts_ps, prep, prep_mm, map_ready, tails = (sem(n) for n in (
            "zeros_ready", "counts_ps", "prep", "prep_mm", "map_ready", "tails"))
        xe_in, ye_out = sems("xe_in", RING), sems("ye_out", RING)
        xet_ps, xet_sb, he_ps, ge_ready, ee_ready, m_ready, ue_ready, te_ready = (sem(n) for n in (
            "xet_ps", "xet_sb", "he_ps", "ge_ready", "ee_ready", "m_ready", "ue_ready", "te_ready"))
        tet_ps, tet_sb, ye_ps, ye_ready = (sem(n) for n in ("tet_ps", "tet_sb", "ye_ps", "ye_ready"))
        idx_ready, g_in, f_half, f_ready, stored = sem("idx_ready"), sems("g_in", 4), sem("f_half"), sem("f_ready"), sems("stored", 4)

        def cols(t, n, width=CC):
            return t[:, n * width:(n + 1) * width] if isinstance(n, int) else t[:, bass.ds(n * width, width)]

        def bchunk(n):
            v = bdt.rearrange("p (g c) -> p g c", g=GROUPS)
            return (v[:, :, n * CC:(n + 1) * CC] if isinstance(n, int) else v[:, :, bass.ds(n * CC, CC)])

        def scores4(s):
            return S[s % 2].rearrange("p (g b j) -> p g b j", g=GROUPS, j=SEG)

        def tiled(t, k=TILES):
            return t.rearrange("p (t d) -> p t d", t=k)

        block = ctx.enter_context(nc.Block())

        @block.sync
        def _(sp):
            sp.dma_start(W[:, 0:W_EARLY], weights[:, 0:W_EARLY]).then_inc(weights_in, 16)
            sp.dma_start(R, rows[0:1, :].to_broadcast([128, R_ALL])).then_inc(rows_in, 16)
            sp.dma_start(W[:, W_EARLY:], weights[:, W_EARLY:]).then_inc(weights2_in, 16)
            sp.dma_start(b1f, b1[0:1, :].to_broadcast([3, NB1])).then_inc(b1_in, 16)

            def load_x(n, s):
                after(sp, xt_ps, n - 3)
                sp.dma_start(xin[s % 4], x[n] if isinstance(n, int) else
                             x[bass.ds(n, 1)].rearrange("o p c -> (o p) c")).then_inc(x_in[s % 4], 16)

            def store_res(n, s):
                sp.wait_ge(ha_ready, n + 1)
                dst = res_d.rearrange("(p s) i d -> p i s d", s=2)
                src = ha[s % 4].rearrange("p (s d) -> p s d", s=2)
                for a, b in ((0, 112), (112, HALF)):
                    v = dst[a:b, n] if isinstance(n, int) else \
                        dst[a:b, bass.ds(n, 1)].rearrange("p o s d -> p (o s) d")
                    sp.dma_start(v, src[a:b]).then_inc(ha_stored[s % 4], 16)

            staged(sp, SEG, [(load_x, 0), (store_res, 3)])
            sp.wait_ge(pads, 1)
            sp.dma_start(res_d[POS:POSP].rearrange("b i d -> (b i) d"), zpad[0:64, :]).then_inc(pads, 16)
            sp.wait_ge(b1_parts, 5)
            sp.dma_start(b1s_d, b1h).then_inc(b1_stored, 16)
            sp.wait_ge(b1_stored, 16)
            sp.dma_start(b1sh[0:3, :], b1s_d[:, E * 2 * IH:]).then_inc(b1sh_in, 16)
            for q in ha_stored:
                sp.wait_ge(q, 2 * 16 * SEG // 4)
            sp.wait_ge(pads, 17)

            def load_res(n, s):
                after(sp, h1_ready, n - 1)
                v = res_d.rearrange("(t b) i d -> (b i) t d", b=128 // SEG)
                v = v[:, n * TILES:(n + 1) * TILES] if isinstance(n, int) else v[:, bass.ds(n * TILES, TILES)]
                sp.dma_start(tiled(res[s % 2]), v).then_inc(res_in[s % 2], 16)

            staged(sp, CHUNKS, [(load_res, 0)], 2)

            sp.wait_ge(pt_ready, CHUNKS)
            sp.dma_start(table3[:, :, TW1:TW2], w1).then_inc(experts_in, 16)
            sp.dma_start(table3[:, :, TW2:TPAR], w2).then_inc(experts_in, 16)
            sp.wait_ge(table_cleared, 1)
            sp.dma_start(table.bitcast(BF16).rearrange("p (e c) -> p e c", e=E)[0:3, :, 2 * TB1:],
                         b1s_d[:, 0:E * 2 * IH].rearrange("p (e c) -> p e c", e=E)).then_inc(b1e_in, 16)
            sp.wait_ge(zeros_ready, 1)
            sp.wait_ge(map_ready, 1)
            sp.dma_start(xs_d[DUMMY:DUMMY + 128, :], zeros).then_inc(tails, 16)
            with sp.Fori(0, E) as e:
                c = sp.value_load(cnt1.bitcast(I32)[0:1, bass.ds(e, 1)], min_val=0, max_val=E * REGION)
                sp.dma_start(xs_d[bass.ds(c, 128), :], zeros).then_inc(tails, 16)
            sp.wait_ge(tails, 16 * (E + 1))
            for q in sent:
                sp.wait_ge(q, 16 * 2 * TOKT // 4)

            def tile_row(n):
                i = rowi.bitcast(I32)
                i = i[0:1, n:n + 1] if isinstance(n, int) else i[0:1, bass.ds(n, 1)]
                return sp.value_load(i, min_val=0, max_val=DUMMY)

            def load_xe(n, s):
                after(sp, xet_ps, n - RING + 1)
                sp.dma_start(xe[s], xs_d[bass.ds(tile_row(n), 128), :]).then_inc(xe_in[s], 16)

            def store_ye(n, s):
                sp.wait_ge(ye_ready, n + 1)
                v = ys_d.rearrange("(t r) d -> t r d", r=128)
                v = v[n] if isinstance(n, int) else v[bass.ds(n, 1)].rearrange("o r d -> (o r) d")
                sp.dma_start(v, ye[s]).then_inc(ye_out[s], 16)

            staged(sp, ETILES, [(load_xe, 0), (store_ye, STORE_LAG)], RING)

            def store_out(n, s):
                sp.wait_ge(f_ready, n + 1)
                v = out.rearrange("(t b) i d -> t (b i) d", b=128 // SEG)
                v = v[n] if isinstance(n, int) else v[bass.ds(n, 1)].rearrange("o r d -> (o r) d")
                sp.dma_start(v, of[s % 4]).then_inc(stored[s % 4], 16)

            staged(sp, TOKT, [(store_out, 0)])
            for q in stored:
                sp.wait_ge(q, 16 * TOKT // 4)

        @block.gpsimd
        def _(pool):
            pool.memset(neg_half, -0.5)
            pool.memset(half_pi, float(np.pi / 2))
            pool.memset(onesb, 1.0)
            pool.memset(zpad, 0.0).then_inc(pads, 1)
            pool.memset(win, 0.0)
            pool.memset(seen[0], 0.0)
            pool.memset(trib, 1.0)
            for t in Kb:
                pool.memset(t, 0.0)
            pool.memset(wnT[:, POS * SEG:], 0.0).then_inc(consts, 1)
            pool.wait_ge(consts, 1)
            pool.affine_select(out=trib, in_=trib, compare_op=ALU.is_gt, fill=0.0, base=0,
                               pattern=[[1, 128]], channel_multiplier=-1).then_inc(consts, 1)

            def split_b1():
                pool.wait_ge(b1_in, 16)
                pool.wait_ge(weights2_in, 16)
                pool.tensor_copy(b1h, b1f).then_inc(b1_parts, 1)
                t = b1t
                for k in (1, 2):
                    pool.wait_ge(b1_parts, 2 * k - 1)
                    pool.tensor_scalar(t, b1h, w("pmask3", k, k + 1)[0:3, :], None, ALU.mult).then_inc(b1_tmp, 1)
                    pool.wait_ge(b1_tmp, 2 * k - 1)
                    pool.tensor_tensor(b1f, b1f, t, ALU.subtract).then_inc(b1_tmp, 1)
                    pool.wait_ge(b1_tmp, 2 * k)
                    pool.tensor_copy(b1h, b1f).then_inc(b1_parts, 2)

            def rstd_a(n, s):
                alone(pool, pw_a, n + 1)
                alone(pool, wn_a, n - 3)
                pool.tensor_tensor(rr[s % 4][0:HALF, :], pw[s % 2][0:HALF, :], neg_half[0:HALF, 0:4], ALU.pow).then_inc(rr_a, 1)

            def residual_a(n, s):
                alone(pool, rs_a, n + 1)
                if not isinstance(n, int) or n >= 4:
                    alone(pool, ha_stored[s % 4], (n - s % 4) * 8)
                for k in range(2):
                    c = ca[s % 4][0:HALF, k * D:(k + 1) * D]
                    o = pool.tensor_scalar(ha[s % 4][0:HALF, k * D:(k + 1) * D], c, rs[s % 2][0:HALF, k:k + 1],
                                           rs[s % 2][0:HALF, 2 + k:3 + k], ALU.mult, ALU.add)
                o.then_inc(ha_ready, 1)

            staged(pool, SEG, [(rstd_a, 0), (residual_a, 1)])
            split_b1()

            def shift(n, s):
                alone(pool, max_ready, n + 1)
                m = mx[s % 2].rearrange("p (g b) -> p g b", g=GROUPS).unsqueeze(3).to_broadcast([128, GROUPS, CB, SEG])
                v = scores4(s)
                for g in range(GROUPS):
                    o = pool.tensor_tensor(v[:, g], v[:, g], m[:, g], ALU.subtract)
                o.then_inc(shifted, 1)

            def normalise(n, s):
                alone(pool, rc_ready, n + 1)
                m = rc[s % 2].rearrange("p (g b) -> p g b", g=GROUPS).unsqueeze(3).to_broadcast([128, GROUPS, CB, SEG])
                v = scores4(s)
                for g in range(GROUPS):
                    o = pool.tensor_tensor(v[:, g], v[:, g], m[:, g], ALU.mult)
                o.then_inc(probs, 1)

            def rstd(n, s):
                alone(pool, mv_d, n + 1)
                alone(pool, rstd_d, n)
                pool.tensor_scalar(vp2, tiled(mv2[s % 2])[:, :, 1], EPS, None, ALU.add).then_inc(vp_d, 1)
                alone(pool, vp_d, n + 1)
                pool.tensor_tensor(rstd_t[s % 2], vp2, neg_half[:, 0:TILES], ALU.pow).then_inc(rstd_d, 1)

            def dispatch(n, s):
                alone(pool, slot_ready, n + 1)
                for k in range(2):
                    for t in range(TILES):
                        pool.indirect_dma_start(
                            out=xs_d, out_offset=bass.IndirectOffsetOnAxis(
                                ap=sl32[s].bitcast(I32)[:, k * TILES + t:k * TILES + t + 1], axis=0),
                            in_=xf[s][:, t * D:(t + 1) * D], in_offset=None).then_inc(sent[s], 16)

            staged(pool, CHUNKS, [(dispatch, 6), (normalise, 2), (shift, 1), (rstd, 3)], 4, 2)
            pool.wait_ge(pt_ready, CHUNKS)
            pool.memset(zeros, 0.0).then_inc(zeros_ready, 1)

            pool.memset(table3[:, :, TB1:], 0.0).then_inc(table_cleared, 1)

            def fetch(n, s):
                i = rowe.bitcast(I32)
                i = i[0:1, n:n + 1] if isinstance(n, int) else i[0:1, bass.ds(n, 1)]
                c = pool.value_load(i, min_val=0, max_val=(E - 1) * TW)
                alone(pool, ye_ps, n - RING + 1)
                pool.tensor_copy(mine[s], table[:, bass.ds(c, TW)]).then_inc(mine_ready, 1)

            pool.wait_ge(map_ready, 1)
            pool.wait_ge(table_ready, 1)
            pool.wait_ge(b1e_in, 16)
            pool.wait_ge(experts_in, 32)
            staged(pool, ETILES, [(fetch, 0)], RING)
            for q in ye_out:
                pool.wait_ge(q, 16 * ETILES // RING)

            def gather(n, s):
                alone(pool, idx_ready, n + 1)
                for k, g in ((0, g0), (1, g1)):
                    pool.indirect_dma_start(
                        out=g[s % 4], out_offset=None, in_=ys_d,
                        in_offset=bass.IndirectOffsetOnAxis(ap=idx[s % 4][:, k:k + 1], axis=0)).then_inc(g_in[s % 4], 16)

            staged(pool, TOKT, [(gather, 0)])

        @block.scalar
        def _(act):
            act.wait_ge(params_abs, 2)
            act.activation(expraw, absraw, ACT.Exp, scale=-1.0).then_inc(params_log, 1)
            act.wait_ge(params_log, 1)
            act.activation(absraw, expraw, ACT.Ln, bias=1.0).then_inc(params_log, 1)

            def xt_copy(n, s):
                act.wait_ge(xt_ps, n + 1)
                after(act, conv_ps, n - 1)
                act.activation(XT[s % 2], bank(s % 2)[:, 0:128], ACT.Copy).then_inc(xt_sb, 1)

            def cosines(n, s):
                act.wait_ge(reduced, n + 1)
                act.activation(ra[s % 2][0:HALF], ra[s % 2][0:HALF], ACT.Abs).then_inc(absolute, 1)
                act.wait_ge(absolute, n + 1)
                after(act, ha_ready, n - 3)
                after(act, wn_a, n - 3)
                act.activation(ca[s % 4][0:HALF], ra[s % 2][0:HALF], ACT.Sin, bias=half_pi[0:HALF, :], scale=-1.0).then_inc(cosine, 1)

            def wt_copy(n, s):
                act.wait_ge(wt_ps, n + 1)
                v = wnT.rearrange("d (p s i) -> d i s p", s=2, i=SEG)
                v = v[:, n, :, 0:HALF] if isinstance(n, int) else v[:, bass.ds(n, 1), :, 0:HALF].rearrange("d o s p -> d (o s) p")
                act.activation(v, bank(4 + s % 2)[:, 0:2 * HALF].rearrange("d (s p) -> d s p", s=2), ACT.Copy).then_inc(wnT_ready, 1)

            act.wait_ge(consts, 1)
            staged(act, SEG, [(xt_copy, 0), (cosines, 1), (wt_copy, 3)])

            def q_copy(n, s):
                act.wait_ge(q_ps, n + 1)
                if isinstance(n, int) and n == 0:
                    act.wait_ge(qbias_ready, 1)
                act.activation(cols(qr, n), bank(s % 4), ACT.Identity, bias=qbias).then_inc(qr_ready, 1)

            staged(act, CHUNKS, [(q_copy, 0)])

            def k_copy(n, s):
                act.wait_ge(k_ps, n + 1)
                after(act, ac_ps, n - 1)
                for g in range(GROUPS):
                    rg = slice(g * 64, g * 64 + 64)
                    o = Kb[s % 2].rearrange("p (b g j) -> p g b j", g=GROUPS, j=SEG)[rg, g]
                    i = act.activation(o, bank(0)[rg].rearrange("p (b j) -> p b j", j=SEG), ACT.Identity, bias=bk[rg])
                i.then_inc(k_sb, 1)

            def q_expand(n, s):
                after(act, ac_ps, n - 1)
                if isinstance(n, int) and n == 0:
                    act.wait_ge(bd_ps, 2 * POSP // BIG)
                o = Qb[s % 2].rearrange("p (b q i) -> p q b i", q=QUADS, i=SEG)
                q = cols(qr, n).rearrange("p (b i) -> p b i", i=SEG)
                for k in (2, 3):
                    i = act.activation(o[:, k], q, ACT.Identity, scale=w("qmask", k, k + 1), bias=qmb[:, k:k + 1])
                i.then_inc(qb_act, 1)

            def exps(n, s):
                act.wait_ge(shifted, n + 1)
                act.activation(S[s % 2], S[s % 2], ACT.Exp, scale=SCALE).then_inc(exped, 1)

            def v_expand(n, s):
                act.wait_ge(vt_ready, n + 1)
                after(act, pv_ps, n)
                o = Vb.rearrange("p (g b q d) -> p q g b d", g=GROUPS, b=CB, q=QUADS)
                v = Vt[s % 2].rearrange("p (b g d) -> p g b d", g=GROUPS, d=DH)
                for k in range(QUADS):
                    i = act.activation(o[:, k], v, ACT.Copy, scale=w("pmask", k, k + 1))
                i.then_inc(vb_ready, 1)

            def at_copy(n, s):
                act.wait_ge(pv_ps, n + 1)
                after(act, wo_ps, n)
                act.activation(at, bank(3), ACT.Identity, bias=bv).then_inc(at_ready, 1)

            def xft_copy(n, s):
                act.wait_ge(xft_ps, n + 1)
                after(act, hs_ps, n)
                act.activation(xfT, bank(4), ACT.Copy).then_inc(xft_sb, 1)

            def swish_tanh(n, s):
                act.wait_ge(gc_ready, n + 1)
                act.activation(eg, gc, ACT.Tanh, scale=half_alpha).then_inc(eg_act, 1)

            def weight_exp(n, s):
                act.wait_ge(dd_ready, n + 1)
                act.activation(ed[:, 0:TILES], dd, ACT.Exp, scale=1.0)
                act.activation(ed[:, TILES:], dd, ACT.Exp, scale=-1.0).then_inc(ed_ready, 1)

            def tt_copy(n, s):
                act.wait_ge(tt_ps, n + 1)
                after(act, z_ps, n)
                act.activation(tT[0:IH, :], bank(4)[0:IH, :], ACT.Copy).then_inc(tt_sb, 1)

            act.wait_ge(params_ready, 1)
            staged(act, CHUNKS, [(at_copy, 3), (swish_tanh, 5), (weight_exp, 5), (q_expand, 0), (v_expand, 2), (tt_copy, 6),
                                 (exps, 1), (xft_copy, 4), (k_copy, 0)], 4, 2)

            def xet_copy(n, s):
                act.wait_ge(xet_ps, n + 1)
                after(act, he_ps, n - 1)
                act.activation(xeT[s % 2], bank(s % 2)[:, 0:128], ACT.Copy).then_inc(xet_sb, 1)

            def sigmoids(n, s):
                act.wait_ge(ge_ready, n + 1)
                after(act, te_ready, n - RING + 1)
                act.activation(ee[s], ge[s], ACT.Sigmoid, scale=mine[s][:, TPAR + 5:TPAR + 6]).then_inc(ee_ready, 1)

            def tet_copy(n, s):
                act.wait_ge(tet_ps, n + 1)
                after(act, ye_ps, n - 1)
                act.activation(teT[s % 2][0:IH, :], bank(4 + s % 2)[0:IH, 0:128], ACT.Copy).then_inc(tet_sb, 1)

            def y_copy(n, s):
                act.wait_ge(ye_ps, n + 1)
                if not isinstance(n, int) or n >= RING:
                    act.wait_ge(ye_out[s], (n - s) * 2)
                act.activation(ye[s], bank(6 + s % 2)[:, 0:D], ACT.Copy).then_inc(ye_ready, 1)

            act.wait_ge(map_ready, 1)
            staged(act, ETILES, [(xet_copy, 0), (sigmoids, 3), (tet_copy, 6), (y_copy, 8)], RING)

        @block.tensor
        def _(pe):
            pe.wait_ge(weights_in, 16)

            def xt(n, s):
                pe.wait_ge(x_in[s % 4], landed(n, s, 4))
                after(pe, xt_sb, n - 1)
                pe.transpose(bank(s % 2)[:, 0:128], xin[s % 4], ident).then_inc(xt_ps, 1)

            def conv(n, s):
                pe.wait_ge(xt_sb, n + 1)
                if isinstance(n, int) and n == 0:
                    pe.wait_ge(conv_ready, 1)
                after(pe, biased, n - 1)
                o, t = bank(2 + s % 2)[0:HALF], XT[s % 2]
                c01, c2, c12, c0 = w("conv01"), w("conv2"), w("conv12"), w("conv0")
                pe.matmul(o[:, 0:D], t[:, 0:HALF], c01, start=True, stop=False)
                pe.matmul(o[:, 0:D], t[:, 1:HALF + 1], c2, start=False, stop=True)
                pe.matmul(o[:, D:2 * D], t[:, 1:HALF + 1], c12, start=True, stop=False)
                pe.matmul(o[:, D:2 * D], t[:, 0:HALF], c0, start=False, stop=True).then_inc(conv_ps, 1)

            def wt(n, s):
                pe.wait_ge(wn_a, n + 1)
                after(pe, wnT_ready, n - 1)
                for k in range(2):
                    i = pe.transpose(bank(4 + s % 2)[:, k * HALF:(k + 1) * HALF],
                                     wn[s % 2][0:HALF, k * D:(k + 1) * D], ident[0:HALF, 0:HALF])
                i.then_inc(wt_ps, 1)

            pe.wait_ge(weights2_in, 16)
            pe.matmul(bank(6)[:, 0:SEG], w("wr"), w("post"), start=True, stop=True)
            for k, key in enumerate(("wq", "wk", "wvp")):
                i = pe.matmul(bank(6)[:, 32 + 2 * k:33 + 2 * k], w(key), w("beta"), start=True, stop=True)
            i.then_inc(setup_mm, 1)
            staged(pe, SEG, [(xt, 0), (conv, 1), (wt, 3)])

            pe.wait_ge(wnT_ready, SEG)
            pe.wait_ge(wqkv_ready, 1)
            pe.wait_ge(consts, 2)

            def q_proj(n, s):
                after(pe, qr_ready, n - 3)
                pe.matmul(bank(s % 4), w("wq"), cols(wnT, n), start=True, stop=True).then_inc(q_ps, 1)

            staged(pe, CHUNKS, [(q_proj, 0)])
            pe.wait_ge(qr_ready, CHUNKS)
            pe.wait_ge(win_ready, 1)

            def bd(c, g):
                after(pe, bdt_ready, 2 * c + g)
                o = bank(0, 8)
                rows_g = slice(g * 64, g * 64 + 64)
                q = qr.rearrange("p (b i) -> p i b", i=SEG)
                for i in range(SEG):
                    t0 = SEG - 1 - i
                    for k in range(2):
                        if i + k == SEG:
                            continue
                        b = q[rows_g, i + k, c * BIG:(c + 1) * BIG]
                        m = pe.matmul(o[:, i * BIG:(i + 1) * BIG], window(k, t0)[rows_g], b,
                                      start=(k == 0), stop=(k == 1 or i == SEG - 1))
                m.then_inc(bd_ps, 1)

            for c in range(POSP // BIG):
                for g in range(GROUPS):
                    bd(c, g)

            def k_proj(n, s):
                after(pe, vt_ready, n)
                pe.matmul(bank(0), w("wk"), cols(wnT, n), start=True, stop=True).then_inc(k_ps, 1)

            def ac(n, s):
                pe.wait_ge(k_sb, n + 1)
                pe.wait_ge(qb_dve, n + 1)
                pe.wait_ge(qb_act, n + 1)
                after(pe, scores, n)
                for b in range(CB):
                    i = pe.matmul(bank(1, 2)[:, b * 64:(b + 1) * 64], Qb[s % 2][:, b * 128:(b + 1) * 128],
                                  Kb[s % 2][:, b * 64:(b + 1) * 64], start=True, stop=True)
                i.then_inc(ac_ps, 1)

            def v_proj(n, s):
                pe.wait_ge(k_sb, n + 1)
                pe.matmul(bank(0), w("wv"), cols(wnT, n), start=True, stop=True).then_inc(v_ps, 1)

            def pv(n, s):
                pe.wait_ge(pt_ready, n + 1)
                pe.wait_ge(vb_ready, n + 1)
                after(pe, h1_ready, n)
                for g in range(GROUPS):
                    for b in range(CB):
                        i = pe.matmul(bank(3)[g * 64:g * 64 + 64, b * SEG:(b + 1) * SEG],
                                      Vb[:, (g * CB + b) * 64:(g * CB + b + 1) * 64],
                                      PT[s % 2][:, (g * CB + b) * SEG:(g * CB + b + 1) * SEG], start=True, stop=True)
                i.then_inc(pv_ps, 1)

            def wo(n, s):
                pe.wait_ge(at_ready, n + 1)
                for t in range(TILES):
                    i = pe.matmul(bank(3)[:, t * D:(t + 1) * D], at[:, t * 128:(t + 1) * 128], w("wo"), start=True, stop=True)
                i.then_inc(wo_ps, 1)

            def xft(n, s):
                pe.wait_ge(xf_ready, n + 1)
                after(pe, z_added, n - 1)
                for t in range(TILES):
                    i = pe.transpose(bank(4)[:, t * 128:(t + 1) * 128], xf[s][:, t * D:(t + 1) * D], ident)
                i.then_inc(xft_ps, 1)

            def first_products(n, s):
                pe.wait_ge(xft_sb, n + 1)
                after(pe, slot_ready, n)
                for t in range(TILES):
                    i = pe.matmul(bank(5)[:, t * E:(t + 1) * E], xfT[:, t * 128:(t + 1) * 128], w("gate"), start=True, stop=True)
                i.then_inc(logit_ps, 1)
                after(pe, uc_ready, n)
                for t in range(0, TILES, 2):
                    o = bank(6 + t // 2)[:, 0:4 * IH]
                    pe.matmul(o, onesb[0:3, :], b1sh[0:3, :].unsqueeze(1).to_broadcast([3, 2, 2 * IH]), start=True, stop=False)
                    for k in range(2):
                        i = pe.matmul(o[:, k * 2 * IH:(k + 1) * 2 * IH], xfT[:, (t + k) * 128:(t + k + 1) * 128], w("ws1"),
                                      start=False, stop=(k == 1))
                i.then_inc(hs_ps, 1)

            def ranks(n, s):
                pe.wait_ge(both_ready, n + 1)
                a = both[s % 2]
                o = bank(5)[:, 64:64 + TILES * E]
                pe.matmul(o, trib, a, start=True, stop=False)
                pe.matmul(o, onesb, seen[s % 2].unsqueeze(1).to_broadcast([128, TILES, E]), start=False, stop=False)
                for t in range(TILES - 1):
                    k = TILES - 1 - t
                    i = pe.matmul(o[:, (t + 1) * E:], onesb, a[:, t * E:(t + 1) * E].unsqueeze(1).to_broadcast([128, k, E]),
                                  start=False, stop=(t == TILES - 2))
                i.then_inc(rank_ps, 1)

            def turn_t(n, s):
                pe.wait_ge(ts_ready, n + 1)
                pe.wait_ge(xft_sb, min(n + 2, CHUNKS) if isinstance(n, int) else n + 2)
                for t in range(TILES):
                    i = pe.transpose(bank(4)[0:IH, t * 128:(t + 1) * 128], uc[s % 2][:, t * IH:(t + 1) * IH], ident)
                i.then_inc(tt_ps, 1)

            def z_products(n, s):
                pe.wait_ge(tt_sb, n + 1)
                for t in range(TILES):
                    i = pe.matmul(bank(4)[:, t * D:(t + 1) * D], tT[0:IH + 1, t * 128:(t + 1) * 128], w("ws2")[0:IH + 1],
                                  start=True, stop=True)
                i.then_inc(z_ps, 1)

            pe.wait_ge(bdt_ready, 2 * POSP // BIG)
            pe.wait_ge(params_ready, 1)
            pe.wait_ge(b1sh_in, 16)
            staged(pe, CHUNKS, [(pv, 3), (ac, 1), (wo, 3), (v_proj, 1), (turn_t, 6), (ranks, 5), (z_products, 6), (xft, 4),
                                (k_proj, 0), (first_products, 4)], 4, 2)

            pe.wait_ge(seen_ready, CHUNKS)
            pe.matmul(bank(0)[:, 0:E], onesb, seen[CHUNKS % 2], start=True, stop=True)
            pe.matmul(bank(0)[0:E, 32:33], seen[CHUNKS % 2], onesb[:, 0:1], start=True, stop=True).then_inc(counts_ps, 1)
            pe.wait_ge(prep, 3)
            pe.matmul(bank(0)[0:E, 64:65], w("tri16")[0:E], cnt[0:E, 2:3], start=True, stop=True).then_inc(prep_mm, 1)
            pe.wait_ge(tri_scaled, 1)
            pe.matmul(bank(4)[:, 0:E], ones1[0:E, :], scaled16[0:E], start=True, stop=True).then_inc(delta_ps, 1)
            pe.wait_ge(prep, 5)
            pe.matmul(bank(0)[0:1, 128:128 + ETILES], ones1[0:E, 0:1], cmp[0:E], start=True, stop=True)
            pe.matmul(bank(1)[0:1, 0:ETILES], cnt[0:E, 2:3], cmp[0:E], start=True, stop=True).then_inc(prep_mm, 1)

            pe.wait_ge(map_ready, 1)

            def xet(n, s):
                pe.wait_ge(xe_in[s], landed(n, s, RING))
                after(pe, xet_sb, n - 1)
                pe.transpose(bank(s % 2)[:, 0:128], xe[s], ident).then_inc(xet_ps, 1)

            def he(n, s):
                pe.wait_ge(xet_sb, n + 1)
                pe.wait_ge(mine_ready, n + 1)
                after(pe, ue_ready, n - 1)
                o = bank(2 + s % 2)[:, 0:2 * IH]
                pe.matmul(o, onesb[0:3, :], mine[s].bitcast(BF16)[0:3, 2 * TB1:], start=True, stop=False)
                pe.matmul(o, xeT[s % 2], mine[s][:, TW1:TW2], start=False, stop=True).then_inc(he_ps, 1)

            def tet(n, s):
                pe.wait_ge(te_ready, n + 1)
                after(pe, tet_sb, n - 1)
                pe.transpose(bank(4 + s % 2)[0:IH, 0:128], te[s % 2], ident).then_inc(tet_ps, 1)

            def yt(n, s):
                pe.wait_ge(tet_sb, n + 1)
                after(pe, ye_ready, n - 1)
                pe.matmul(bank(6 + s % 2)[:, 0:D], teT[s % 2][0:IH + 1, :], mine[s][0:IH + 1, TW2:TPAR],
                          start=True, stop=True).then_inc(ye_ps, 1)

            staged(pe, ETILES, [(xet, 0), (he, 2), (tet, 6), (yt, 8)], RING)

        @block.vector
        def _(dve):
            dve.memset(tT[96:97, :], 1.0)
            dve.wait_ge(weights_in, 16)
            dve.wait_ge(rows_in, 16)
            dve.reciprocal(recip_ks, r("kscale")).then_inc(dve_setup, 1)
            dve.wait_ge(dve_setup, 1)
            dve.tensor_scalar(conv_scaled, conv_scaled, recip_ks, None, ALU.mult).then_inc(conv_ready, 1)
            raw = par[:, :, 3:5]
            dve.scalar_tensor_tensor(absraw.rearrange("p (e f) -> p e f", f=2), raw, -1.0, raw, ALU.mult, ALU.max).then_inc(params_abs, 1)
            dve.tensor_scalar(maxraw.rearrange("p (e f) -> p e f", f=2), raw, 0.0, None, ALU.max).then_inc(params_abs, 1)
            dve.tensor_scalar(half_alpha, par[:, E, 0:1], 0.5, None, ALU.mult)
            dve.tensor_copy(alpha, par[:, :, 0])
            dve.tensor_copy(shift_p, par[:, :, 2])
            dve.wait_ge(params_log, 2)
            dve.tensor_tensor(clamp, maxraw, absraw, ALU.add).then_inc(dve_setup, 1)
            dve.wait_ge(dve_setup, 2)
            dve.tensor_scalar(nclamp, clamp, -1.0, None, ALU.mult)
            dve.wait_ge(weights2_in, 16)
            dve.tensor_scalar(w("ws2")[0:IH], w("ws2")[0:IH], par[0:IH, E, 1:2], 0.5, ALU.mult, ALU.mult).then_inc(params_ready, 1)
            dve.wait_ge(setup_mm, 1)
            dve.tensor_tensor(wrdiff, w("rwb"), w("rrb"), ALU.subtract)
            dve.tensor_copy(bk, bank(6)[:, 34:35])
            dve.tensor_copy(bv, bank(6)[:, 36:37])
            dve.tensor_tensor(qbias, bank(6)[:, 32:33], w("rrb"), ALU.add).then_inc(qbias_ready, 1)
            for key in ("wq", "wk", "wv"):
                i = dve.tensor_scalar(w(key), w(key), w("gamma"), None, ALU.mult)
            i.then_inc(wqkv_ready, 1)
            dve.wait_ge(consts, 1)
            dve.wait_ge(qbias_ready, 1)
            a1, a2 = (t.rearrange("p (q t) -> p q t", q=QUADS) for t in (win1, win2))
            for k in range(QUADS):
                m = w("qmask", k, k + 1)
                dve.tensor_scalar(a1[:, k, 0:SEG], bank(6)[:, 0:SEG], m, None, ALU.mult)
                dve.tensor_scalar(a2[:, k, SEG + 1:], bank(6)[:, 0:SEG - 2], m, None, ALU.mult)
                i = dve.tensor_scalar(qmb[:, k:k + 1], wrdiff, m, None, ALU.mult)
            i.then_inc(win_src, 1)
            dve.wait_ge(win_src, 1)
            for k in range(QUADS):
                for a, dst, first, count in ((a1, QV[:, 0:SEG * 128], 0, SEG), (a2, QV[:, SEG * 128:], 0, 16), (a2, PP, 16, 16)):
                    i = dve.tensor_copy(dst.rearrange("p (t q j) -> p q t j", q=QUADS, j=SEG)[:, k], slide(a[:, k], first, count))
            i.then_inc(win_ready, 1)

            def reduce_args(n, s):
                p = slice(0, HALF)
                v, k, q = va[s % 2][p], ka[s % 2][p], ra[s % 2][p]
                dve.wait_ge(conv_ps, n + 1)
                dve.tensor_tensor(v.rearrange("p (s d) -> p s d", s=2), bank(2 + s % 2)[p, 0:2 * D].rearrange("p (s d) -> p s d", s=2),
                                  r("cbias")[p].unsqueeze(1).to_broadcast([HALF, 2, D]), ALU.add).then_inc(biased, 1)
                dve.wait_ge(biased, n + 1)
                dve.tensor_scalar(k, v, INV_TWO_PI, MAGIC, ALU.mult, ALU.add).then_inc(arg_steps, 1)
                dve.wait_ge(arg_steps, 3 * n + 1)
                dve.tensor_scalar(k, k, MAGIC, None, ALU.subtract).then_inc(arg_steps, 1)
                dve.wait_ge(arg_steps, 3 * n + 2)
                after(dve, cosine, n - 1)
                dve.scalar_tensor_tensor(v, k, -TWO_PI_HI, v, ALU.mult, ALU.add).then_inc(arg_steps, 1)
                dve.wait_ge(arg_steps, 3 * n + 3)
                dve.scalar_tensor_tensor(q, k, -TWO_PI_LO, v, ALU.mult, ALU.add).then_inc(reduced, 1)

            def stats(n, s):
                p = slice(0, HALF)
                dve.wait_ge(cosine, n + 1)
                for k in range(2):
                    i = dve.bn_stats(st[p, 6 * k:6 * k + 6], ca[s % 4][p, k * D:(k + 1) * D])
                i.then_inc(stats_a, 1)
                alone(dve, stats_a, n + 1)
                for k in range(2):
                    i = dve.bn_aggr(mv[s % 4][p, 2 * k:2 * k + 2], st[p, 6 * k:6 * k + 6])
                i.then_inc(mv_a, 1)
                dve.wait_ge(mv_a, n + 1)
                after(dve, rr_a, n - 1)
                m = mv[s % 4][p].rearrange("p (s k) -> p s k", s=2)
                o = pw[s % 2][p].rearrange("p (s k) -> p s k", s=2)
                c = 1 / COS_NORM ** 2
                dve.tensor_scalar(o[:, :, 0], m[:, :, 1], c * EPS, None, ALU.add)
                dve.tensor_scalar(o[:, :, 1], m[:, :, 1], 1 + EPS, c * EPS * EPS, ALU.mult, ALU.add).then_inc(pw_a, 1)

            def norms(n, s):
                p = slice(0, HALF)
                dve.wait_ge(rr_a, n + 1)
                m, q = mv[s % 4][p].rearrange("p (s k) -> p s k", s=2), rr[s % 4][p].rearrange("p (s k) -> p s k", s=2)
                after(dve, ha_ready, n - 1)
                o = rs[s % 2][p]
                dve.tensor_scalar(o[:, 0:2], q[:, :, 0], COS_NORM, None, ALU.add)
                dve.scalar_tensor_tensor(o[:, 2:4], m[:, :, 0], -1.0, q[:, :, 0], ALU.mult, ALU.mult).then_inc(rs_a, 1)
                after(dve, wt_ps, n - 1)
                for k in range(2):
                    i = dve.tensor_scalar(wn[s % 2][p, k * D:(k + 1) * D], ca[s % 4][p, k * D:(k + 1) * D], m[:, k, 0:1], q[:, k, 1:2],
                                          ALU.subtract, ALU.mult)
                i.then_inc(wn_a, 1)

            staged(dve, SEG, [(reduce_args, 0), (stats, 1), (norms, 2)])

            for q in ha_stored:
                dve.wait_ge(q, 2 * 16 * SEG // 4)
            dve.wait_ge(pads, 17)
            dve.wait_ge(b1_stored, 16)
            for n in range(2 * POSP // BIG):
                g, c = n % 2, n // 2
                dve.wait_ge(bd_ps, n + 1)
                o = bdt[:, (g * POSP + c * BIG) * SEG:(g * POSP + (c + 1) * BIG) * SEG]
                dve.transpose(o, bank(0, 8).rearrange("p (i b) -> p b i", i=SEG)).then_inc(bdt_ready, 1)

            dve.wait_ge(params_ready, 1)
            dve.wait_ge(win_ready, 1)

            def q_expand(n, s):
                after(dve, ac_ps, n - 1)
                o = Qb[s % 2].rearrange("p (b q i) -> p q b i", q=QUADS, i=SEG)
                q = cols(qr, n).rearrange("p (b i) -> p b i", i=SEG)
                for k in (0, 1):
                    i = dve.tensor_scalar(o[:, k], q, w("qmask", k, k + 1), qmb[:, k:k + 1], ALU.mult, ALU.add)
                i.then_inc(qb_dve, 1)

            def v_turn(n, s):
                dve.wait_ge(v_ps, n + 1)
                after(dve, vb_ready, n - 1)
                dve.transpose(Vt[s % 2], bank(0)).then_inc(vt_ready, 1)

            def add_scores(n, s):
                dve.wait_ge(ac_ps, n + 1)
                dve.tensor_tensor(scores4(s), bank(1, 2).rearrange("p (b g j) -> p g b j", g=GROUPS, j=SEG),
                                  bchunk(n).rearrange("p g (b j) -> p g b j", j=SEG), ALU.add).then_inc(scores, 1)
                dve.wait_ge(scores, n + 1)
                after(dve, shifted, n - 1)
                dve.tensor_reduce(mx[s % 2].rearrange("p (g b) -> p g b", g=GROUPS), scores4(s), AX, ALU.max).then_inc(max_ready, 1)

            def sum_exps(n, s):
                dve.wait_ge(exped, n + 1)
                dve.tensor_reduce(sm.rearrange("p (g b) -> p g b", g=GROUPS), scores4(s), AX, ALU.add).then_inc(sums, 1)
                dve.wait_ge(sums, n + 1)
                after(dve, probs, n - 1)
                dve.reciprocal(rc[s % 2], sm).then_inc(rc_ready, 1)

            def turn_p(n, s):
                dve.wait_ge(probs, n + 1)
                after(dve, pv_ps, n - 1)
                dve.transpose(PT[s % 2], S[s % 2]).then_inc(pt_ready, 1)

            def add_h1(n, s):
                dve.wait_ge(wo_ps, n + 1)
                dve.wait_ge(res_in[s % 2], landed(n, s, 2))
                dve.tensor_tensor(cols(wnT, n), bank(3), res[s % 2], ALU.add).then_inc(h1_ready, 1)
                dve.wait_ge(h1_ready, n + 1)
                for t in range(TILES):
                    i = dve.bn_stats(st2[:, t * 6:t * 6 + 6], cols(wnT, n * TILES + t, D))
                i.then_inc(stats_d, 1)
                alone(dve, stats_d, n + 1)
                for t in range(TILES):
                    i = dve.bn_aggr(mv2[s % 2][:, 2 * t:2 * t + 2], st2[:, t * 6:t * 6 + 6])
                i.then_inc(mv_d, 1)

            def norm_ffn(n, s):
                dve.wait_ge(rstd_d, n + 1)
                if not isinstance(n, int) or n >= 4:
                    dve.wait_ge(sent[s], (n - s) * 32)
                for t in range(TILES):
                    i = dve.tensor_scalar(xf[s][:, t * D:(t + 1) * D], cols(wnT, n * TILES + t, D), mv2[s % 2][:, 2 * t:2 * t + 1],
                                          rstd_t[s % 2][:, t:t + 1], ALU.subtract, ALU.mult)
                i.then_inc(xf_ready, 1)

            RT = 6

            def router(n, s):
                def step(i):
                    i.then_inc(rt, 1)

                def done(k):
                    alone(dve, rt, n * RT + k)

                dve.wait_ge(logit_ps, n + 1)
                l3 = lg.rearrange("p (t e) -> p t e", e=E)
                step(dve.tensor_tensor(l3, bank(5)[:, 0:TILES * E].rearrange("p (t e) -> p t e", e=E),
                                       r("gateb").unsqueeze(1).to_broadcast([128, TILES, E]), ALU.add))
                done(1)
                for t in range(TILES):
                    i = dve.max(m8[:, t * 8:t * 8 + 8], lg[:, t * E:(t + 1) * E])
                step(i)
                done(2)
                for t in range(TILES):
                    i = dve.max_index(ix8.bitcast(U32)[:, t * 8:t * 8 + 8], m8[:, t * 8:t * 8 + 8], lg[:, t * E:(t + 1) * E])
                step(i)
                m3 = m8.rearrange("p (t k) -> p t k", k=8)
                after(dve, ed_ready, n)
                dve.tensor_tensor(dd, m3[:, :, 1], m3[:, :, 0], ALU.subtract).then_inc(dd_ready, 1)
                done(3)
                step(dve.tensor_copy(ixf.rearrange("p (k t) -> p t k", k=2), ix8.bitcast(U32).rearrange("p (t k) -> p t k", k=8)[:, :, 0:2]))
                done(4)
                o4 = oh.rearrange("p (k t e) -> p k t e", k=2, e=E)
                i3 = r("iota16").unsqueeze(1).to_broadcast([128, TILES, E])
                for k in range(2):
                    i = dve.tensor_tensor(o4[:, k], i3, ixf[:, k * TILES:(k + 1) * TILES].unsqueeze(2).to_broadcast([128, TILES, E]), ALU.is_equal)
                step(i)
                done(5)
                after(dve, rank_ps, n - 1)
                dve.tensor_tensor(both[s % 2], oh[:, 0:TILES * E], oh[:, TILES * E:], ALU.add).then_inc(both_ready, 1)
                dve.wait_ge(both_ready, n + 1)
                step(dve.tensor_reduce(tsum, both[s % 2].rearrange("p (t e) -> p e t", e=E), AX, ALU.add))
                done(6)
                after(dve, rank_ps, n)
                after(dve, seen_ready, n)
                dve.tensor_tensor(seen[(s + 1) % 2], seen[s % 2], tsum, ALU.add).then_inc(seen_ready, 1)

            def weights_of(n, s):
                dve.wait_ge(ed_ready, n + 1)
                dve.tensor_scalar(ed, ed, 1.0, None, ALU.add).then_inc(ed_plus, 1)
                dve.wait_ge(ed_plus, n + 1)
                dve.reciprocal(cols(wts, n, 2 * TILES), ed).then_inc(wts_ready, 1)

            def slots_of(n, s):
                def done(k):
                    dve.wait_ge(rt2, n * 3 + k)

                dve.wait_ge(rank_ps, n + 1)
                dve.tensor_tensor(rb.rearrange("p (t e) -> p t e", e=E), bank(5)[:, 64:64 + TILES * E].rearrange("p (t e) -> p t e", e=E),
                                  r("ebase").unsqueeze(1).to_broadcast([128, TILES, E]), ALU.add).then_inc(rt2, 1)
                done(1)
                dve.tensor_tensor(ohr.rearrange("p (k c) -> p k c", k=2), oh.rearrange("p (k c) -> p k c", k=2),
                                  rb.unsqueeze(1).to_broadcast([128, 2, TILES * E]), ALU.mult).then_inc(rt2, 1)
                done(2)
                dve.tensor_reduce(slf, ohr.rearrange("p (kt e) -> p kt e", e=E), AX, ALU.add).then_inc(rt2, 1)
                done(3)
                dve.tensor_copy(cols(slots, n, 2 * TILES), slf)
                dve.tensor_copy(cols(chosen, n, 2 * TILES), ixf)
                dve.tensor_copy(sl32[s].bitcast(I32), slf).then_inc(slot_ready, 1)

            def swiglu_a(n, s):
                hs = bank(6, 2).rearrange("p (a c) -> p a c", a=2)[:, :, 0:4 * IH].rearrange("p a (k u h) -> p a k u h", k=2, u=2)
                gv, uv = (t.rearrange("p (a k h) -> p a k h", a=2, k=2) for t in (gc, uc[s % 2]))
                dve.wait_ge(hs_ps, n + 1)
                for a in range(2):
                    i = dve.tensor_scalar(gv[:, a], hs[:, a, :, 0], clamp[:, 2 * E:2 * E + 1], nclamp[:, 2 * E:2 * E + 1], ALU.min, ALU.max)
                i.then_inc(gc_ready, 1)
                after(dve, tt_ps, n - 1)
                for a in range(2):
                    i = dve.tensor_scalar(uv[:, a], hs[:, a, :, 1], clamp[:, 2 * E + 1:2 * E + 2], nclamp[:, 2 * E + 1:2 * E + 2], ALU.min, ALU.max)
                i.then_inc(uc_ready, 1)

            def swiglu_b(n, s):
                dve.wait_ge(eg_act, n + 1)
                dve.scalar_tensor_tensor(eg, eg, 1.0, gc, ALU.add, ALU.mult).then_inc(eg_dve, 1)
                dve.wait_ge(eg_dve, n + 1)
                dve.scalar_tensor_tensor(uc[s % 2], uc[s % 2], par[:, E, 2:3], eg, ALU.add, ALU.mult).then_inc(ts_ready, 1)

            def add_z(n, s):
                dve.wait_ge(z_ps, n + 1)
                dve.tensor_tensor(cols(wnT, n), bank(4), cols(wnT, n), ALU.add).then_inc(z_added, 1)

            staged(dve, CHUNKS, [(router, 5), (sum_exps, 2), (norm_ffn, 4), (swiglu_a, 5), (q_expand, 0), (add_scores, 1),
                                 (add_h1, 3), (v_turn, 1), (add_z, 6), (swiglu_b, 5), (slots_of, 5), (turn_p, 2),
                                 (weights_of, 5)], 4, 2)

            dve.wait_ge(zeros_ready, 1)
            dve.wait_ge(counts_ps, 1)
            dve.wait_ge(experts_in, 32)
            for k, v in enumerate((clamp[:, 0:2 * E:2], nclamp[:, 0:2 * E:2], clamp[:, 1:2 * E:2], nclamp[:, 1:2 * E:2],
                                   shift_p[:, 0:E], alpha[:, 0:E], alpha[:, 0:E], alpha[:, 0:E])):
                dve.tensor_copy(table3[:, :, TPAR + k], v)
            dve.tensor_tensor(table3[0:IH, :, TW2:TPAR], table3[0:IH, :, TW2:TPAR],
                              par[0:IH, 0:E, 1].unsqueeze(2).to_broadcast([IH, E, D]), ALU.mult).then_inc(table_ready, 1)
            dve.memset(ones1, 1.0)
            for t in teT:
                dve.memset(t[96:97, :], 1.0)
            dve.tensor_tensor(cnt1[0:1, 0:E].bitcast(I32), bank(0)[0:1, 0:E], r("ebase")[0:1], ALU.add)
            ci = cnt.bitcast(I32)
            dve.tensor_scalar(ci[0:E, 0:1], bank(0)[0:E, 32:33], 127.0, None, ALU.add).then_inc(prep, 1)
            dve.wait_ge(prep, 1)
            dve.tensor_scalar(ci[0:E, 1:2], ci[0:E, 0:1], 7, None, ALU.arith_shift_right).then_inc(prep, 1)
            dve.wait_ge(prep, 2)
            dve.tensor_copy(cnt[0:E, 2:3], ci[0:E, 1:2]).then_inc(prep, 1)
            dve.wait_ge(prep, 3)
            dve.tensor_scalar(scaled16[0:E], w("stri16")[0:E], cnt[0:E, 2:3], 128.0, ALU.mult, ALU.mult).then_inc(tri_scaled, 1)
            dve.wait_ge(prep_mm, 1)
            dve.tensor_copy(cnt[0:E, 3:4], bank(0)[0:E, 64:65]).then_inc(prep, 1)
            dve.wait_ge(prep, 4)
            dve.tensor_scalar(cmp[0:E], w("iota")[0:E], cnt[0:E, 3:4], None, ALU.is_ge).then_inc(prep, 1)
            dve.wait_ge(prep_mm, 2)
            ex, first, use, tmp = (rowf[0:1, k * ETILES:(k + 1) * ETILES] for k in range(4))
            dve.tensor_copy(ex, bank(0)[0:1, 128:128 + ETILES])
            dve.tensor_tensor(first, w("iota")[0:1], bank(1)[0:1, 0:ETILES], ALU.subtract).then_inc(prep, 1)
            dve.wait_ge(prep, 6)
            dve.tensor_scalar(use, ex, float(E), None, ALU.is_lt)
            dve.tensor_scalar(tmp, ex, float(REGION), -float(DUMMY), ALU.mult, ALU.add).then_inc(prep, 1)
            dve.wait_ge(prep, 7)
            dve.scalar_tensor_tensor(tmp, first, 128.0, tmp, ALU.mult, ALU.add).then_inc(prep, 1)
            dve.wait_ge(prep, 8)
            dve.tensor_tensor(tmp, tmp, use, ALU.mult)
            dve.scalar_tensor_tensor(rowe[0:1].bitcast(I32), ex, float(TW), use, ALU.mult, ALU.mult).then_inc(prep, 1)
            dve.wait_ge(prep, 9)
            dve.tensor_scalar(rowi[0:1].bitcast(I32), tmp, float(DUMMY), None, ALU.add).then_inc(map_ready, 1)
            dve.wait_ge(map_ready, 1)
            dve.wait_ge(delta_ps, 1)
            dve.tensor_tensor(delta, bank(4)[:, 0:E], r("ebase"), ALU.subtract).then_inc(looked, 1)
            dve.wait_ge(looked, 1)
            l3 = look.rearrange("p (n e) -> p n e", e=E)
            dve.wait_ge(slot_ready, CHUNKS)
            dve.tensor_tensor(l3, r("iota16").unsqueeze(1).to_broadcast([128, 2 * TOKT, E]),
                              chosen.unsqueeze(2).to_broadcast([128, 2 * TOKT, E]), ALU.is_equal).then_inc(looked, 1)
            dve.wait_ge(looked, 2)
            dve.tensor_tensor(l3, l3, delta.unsqueeze(1).to_broadcast([128, 2 * TOKT, E]), ALU.mult).then_inc(looked, 1)
            dve.wait_ge(looked, 3)
            dve.tensor_reduce(chosen, l3, AX, ALU.add).then_inc(looked, 1)
            dve.wait_ge(looked, 4)
            dve.tensor_tensor(yrow, chosen, slots, ALU.add).then_inc(looked, 1)

            def clip_e(n, s):
                dve.wait_ge(he_ps, n + 1)
                h, p = bank(2 + s % 2), mine[s][:, TPAR:]
                dve.tensor_scalar(ge[s], h[:, 0:IH], p[:, 0:1], p[:, 1:2], ALU.min, ALU.max).then_inc(ge_ready, 1)
                dve.tensor_scalar(ue[s], h[:, IH:2 * IH], p[:, 2:3], p[:, 3:4], ALU.min, ALU.max).then_inc(ue_ready, 1)

            def gate_e(n, s):
                dve.wait_ge(ee_ready, n + 1)
                dve.tensor_tensor(ee[s], ge[s], ee[s], ALU.mult).then_inc(m_ready, 1)
                dve.wait_ge(m_ready, n + 1)
                after(dve, tet_ps, n - 1)
                dve.scalar_tensor_tensor(te[s % 2], ue[s], mine[s][:, TPAR + 4:TPAR + 5], ee[s], ALU.add, ALU.mult).then_inc(te_ready, 1)

            staged(dve, ETILES, [(clip_e, 0), (gate_e, 2)], RING)

            def indices(n, s):
                after(dve, f_ready, n - 3)
                dve.tensor_copy(idx[s % 4], slots_kt(n, s)).then_inc(idx_ready, 1)

            def slots_kt(n, s):
                v = yrow.rearrange("p (c k t) -> p c t k", k=2, t=TILES)
                return v[:, n // TILES, s % 4] if isinstance(n, int) else v[:, bass.ds((n - s % 4) // TILES, 1), s % 4].rearrange("p o k -> p (o k)")

            def wts_k(n, s, k):
                at0 = (n - s % 4) * 2 + k * TILES + s % 4
                return wts[:, at0:at0 + 1] if isinstance(n, int) else wts[:, bass.ds(at0, 1)]

            def combine(n, s):
                dve.wait_ge(g_in[s % 4], landed2(n, s))
                if not isinstance(n, int) or n >= 4:
                    dve.wait_ge(stored[s % 4], (n - s % 4) * 4)
                dve.scalar_tensor_tensor(of[s % 4], g0[s % 4], wts_k(n, s, 0), cols(wnT, n, D), ALU.mult, ALU.add).then_inc(f_half, 1)
                dve.wait_ge(f_half, n + 1)
                dve.scalar_tensor_tensor(of[s % 4], g1[s % 4], wts_k(n, s, 1), of[s % 4], ALU.mult, ALU.add).then_inc(f_ready, 1)

            def landed2(n, s):
                return (n - s % 4) * 8 + 32

            dve.wait_ge(wts_ready, CHUNKS)
            dve.wait_ge(looked, 5)
            dve.wait_ge(z_added, CHUNKS)
            staged(dve, TOKT, [(indices, 0), (combine, 3)])


def kernel(**inputs):
    import concourse.bacc as bacc
    from concourse.bass_utils import run_bass_kernel_spmd

    f = np.float32
    a = {k: np.asarray(v) for k, v in inputs.items()}
    p = "L0_attn_"
    perm = np.array([(2 * q + g) * DH + d for g in range(GROUPS) for q in range(QUADS) for d in range(DH)])
    wide = np.zeros((128, W_ALL), f)

    def put(key, v):
        v = np.asarray(v)
        wide[:v.shape[0], W_AT[key][0]:W_AT[key][1]] = v

    ck = a["L0_tok_kernel"]
    put("conv01", ck[0:2].reshape(2 * CIN, D))
    put("conv2", ck[2])
    wide[CIN:, W_AT["conv0"][0]:W_AT["conv0"][1]] = ck[0]
    put("conv12", ck[1:3].reshape(2 * CIN, D))
    qkv = a[p + "Wqkv"]
    put("wq", qkv[0:D][perm].T)
    put("wk", qkv[D:2 * D][perm].T)
    put("wv", qkv[2 * D:].T)
    put("wvp", qkv[2 * D:][perm].T)
    put("wo", a[p + "Wo"].T[perm])
    put("wr", a[p + "Wr"][perm].T)
    pos = np.arange(SEG - 1, -1, -1, dtype=f)
    inv = f(1.0) / (f(10000.0) ** (np.arange(0, D, 2, dtype=f) / f(D)))
    ang = (pos[:, None] * inv[None, :]).astype(f)
    put("post", np.concatenate([np.sin(ang), np.cos(ang)], axis=1).T)
    put("ident", np.eye(128))
    put("rwb", a[p + "r_w_bias"].reshape(D)[perm][:, None])
    put("rrb", a[p + "r_r_bias"].reshape(D)[perm][:, None])
    put("gamma", a[p + "ln_gamma"][:, None])
    put("beta", a[p + "ln_beta"][:, None])
    m = "L0_ffn_"

    def halves(t):
        return np.concatenate([t[..., 0::2], t[..., 1::2]], axis=-1)

    put("gate", a[m + "gate_w"])
    put("ws1", halves(a[m + "shared_w1"]))
    put("ws2", np.concatenate([a[m + "shared_w2"], a[m + "shared_b2"][None]]))
    put("iota", np.tile(np.arange(ETILES, dtype=f), (128, 1)))
    part = np.arange(128)
    put("qmask", (part[:, None] % 64 // DH == np.arange(QUADS)).astype(f))
    put("pmask", (part[:, None] // SEG == np.arange(QUADS)).astype(f))
    put("tri16", np.triu(np.ones((E, E), f)))
    put("stri16", np.triu(np.ones((E, E), f), 1))
    put("pmask3", (part[:3, None] >= np.arange(3)).astype(f))
    act = np.concatenate([a[m + "expert_act"], a[m + "shared_act"][None]])
    rows = np.concatenate([a["L0_tok_bias"], a["L0_tok_kernel_scale"], a[m + "gate_b"], act.reshape(-1),
                           np.arange(E, dtype=f), np.arange(E, dtype=f) * REGION])[None]
    arrays = {
        "x": a["x"].reshape(SEG, WIDTH // 2, 2 * CIN),
        "weights": wide,
        "rows": rows,
        "w1": halves(a[m + "expert_w1"]).transpose(1, 0, 2),
        "w2": np.concatenate([a[m + "expert_w2"], a[m + "expert_b2"][:, None, :],
                              np.zeros((E, 127 - IH, D), f)], axis=1).transpose(1, 0, 2),
        "b1": halves(np.concatenate([a[m + "expert_b1"], a[m + "shared_b1"][None]])).reshape(1, -1),
    }
    arrays = {k: np.ascontiguousarray(v, dtype=v.dtype) for k, v in arrays.items()}
    nc = bacc.Bacc("TRN2", target_bir_lowering=False, num_devices=1)
    args = [nc.dram_tensor(k, v.shape, mybir.dt.from_np(v.dtype), kind="ExternalInput").ap() for k, v in arrays.items()]
    out = nc.dram_tensor("out", (POSP, SEG, D), F32, kind="ExternalOutput").ap()
    build(nc, *args, out)
    got = run_bass_kernel_spmd(nc, [arrays], core_ids=[0]).results[0]["out"]
    return np.ascontiguousarray(got[:POS].transpose(1, 0, 2))
```

```python
from contextlib import ExitStack

import numpy as np

import concourse.bass as bass
from concourse import mybir

F32 = mybir.dt.float32
BF16 = mybir.dt.bfloat16
I32 = mybir.dt.int32
U32 = mybir.dt.uint32
ALU = mybir.AluOpType
ACT = mybir.ActivationFunctionType
AX = mybir.AxisListType.X

SEG, WIDTH, CIN, TAPS, D = 32, 256, 64, 3, 128
POS = WIDTH - TAPS + 1
HALF = POS // 2
POSP = 256
DH = 16
GROUPS, QUADS = 2, 4
E, IH = 16, 96
CB = 16
CHUNKS = POSP // CB
CC = CB * SEG
TILES = CC // 128
TOKT = SEG * POSP // 128
BIG = 128
REGION = SEG * POSP + 128
DUMMY = E * REGION
TOKENS = SEG * POSP
XW = D + 1
ETILES = 2 * TOKT + E
NB1 = (E + 1) * 2 * IH
WIN = 2 * SEG - 1
FIRST = E + 2 * IH
MAGIC = float(1.5 * 2 ** 23)
TWO_PI_HI = float(np.float32(6.28125))
TWO_PI_LO = float(np.float32(2 * np.pi - 6.28125))
INV_TWO_PI = float(np.float32(1 / (2 * np.pi)))
EPS = 1e-5
COS_NORM = float(np.sqrt(np.float32(2.0 / D)))
SCALE = 1.0 / DH ** 0.5

W_COLS = dict(conv01=D, conv2=D, conv12=D, conv0=D, ident=128, wq=D, wk=D, wv=D, wo=D, wvp=D, post=SEG,
              rwb=1, rrb=1, gamma=1, beta=1, gate=E, ws1=2 * IH, ws2=D, iota=ETILES, qmask=QUADS,
              pmask=QUADS, tri16=E, place=ETILES)
W_AT = {}
_at = 0
for _k, _n in W_COLS.items():
    W_AT[_k] = (_at, _at + _n)
    _at += _n
W_ALL = _at
W_EARLY = W_AT['wq'][0]
B_COLS = dict(wr0=D, wr1=D)
B_AT = {}
_at = 0
for _k, _n in B_COLS.items():
    B_AT[_k] = (_at, _at + _n)
    _at += _n
B_ALL = _at
R_COLS = dict(cbias=D, kscale=1, gateb=E, act=5 * (E + 1), iota16=E, ebase=E)
R_AT = {}
_at = 0
for _k, _n in R_COLS.items():
    R_AT[_k] = (_at, _at + _n)
    _at += _n
R_ALL = _at


def staged(eng, total, stages, unroll=4, head=None):
    lag = max(l for _, l in stages)
    first = lag + (unroll if head is None else head)
    loops = (total - first) // unroll
    last = first + loops * unroll

    def step(j):
        for fn, l in stages:
            if 0 <= j - l < total:
                fn(j - l, (j - l) % unroll)

    for j in range(first):
        step(j)
    if loops > 1:
        with eng.Fori(first, last - unroll + 1, unroll) as at:
            for u in range(unroll):
                for fn, l in stages:
                    n = at + (u - l) if u != l else at
                    fn(n, (first + u - l) % unroll)
    else:
        last = first
    for j in range(last, total + lag):
        step(j)


def after(eng, sem, value):
    if not isinstance(value, int) or value > 0:
        eng.wait_ge(sem, value)


def alone(eng, sem, value):
    if not isinstance(value, int):
        value = eng.snap(eng.to_reg(value))
        eng.wait_ge(sem, 1)
    after(eng, sem, value)


def landed(n, s, ring):
    return (n - s % ring) * (16 // ring) + 16


TW1 = 0
TW2 = TW1 + 2 * IH
TPAR = TW2 + D
TB1 = TPAR + 8
TW = TB1 + IH
RING = 8


def build(nc, x, weights, b_weights, rows, w1, w2, b1, out):
    with ExitStack() as ctx:
        def sb(name, cols, dt=F32):
            return ctx.enter_context(nc.sbuf_tensor(name, [128, cols], dt))[:, :]

        def sem(name):
            return ctx.enter_context(nc.semaphore(name))

        def sems(name, n):
            return [sem(f"{name}{i}") for i in range(n)]

        res_d = nc.dram_tensor("res_d", [POSP, SEG, D], F32, kind="Internal").ap()
        b1s_d = nc.dram_tensor("b1s_d", [3, NB1], BF16, kind="Internal").ap()
        xs_d = nc.dram_tensor("xs_d", [DUMMY + 128, XW], F32, kind="Internal").ap()
        ys_d = nc.dram_tensor("ys_d", [ETILES * 128 + 2 * TOKENS, D], F32, kind="Internal").ap()

        wnT = sb("wnT", POSP * SEG)
        qr = sb("qr", POSP * SEG)
        bdt = sb("bdt", GROUPS * POSP * SEG)
        W = sb("W", W_ALL)
        R = sb("R", R_ALL)
        onesb = sb("onesb", 128, BF16)
        trib = sb("trib", 128, BF16)
        b1sh = sb("b1sh", FIRST, BF16)

        def w(key, a=0, b=None):
            lo, hi = W_AT[key]
            return W[:, lo + a:(hi if b is None else lo + b)]

        def r(key, a=0, b=None):
            lo, hi = R_AT[key]
            return R[:, lo + a:(hi if b is None else lo + b)]

        wts = w("wq")

        QVP = sb("QVP", 3 * CB * 128 + 2 * GROUPS * CC)
        QV = QVP[:, 0:3 * CB * 128]
        Qb = [QV[:, u * CB * 128:(u + 1) * CB * 128] for u in range(2)]
        Vb = QV[:, 2 * CB * 128:]
        SS = sb("SS", 2 * GROUPS * CC)
        S = [SS[:, u * GROUPS * CC:(u + 1) * GROUPS * CC] for u in range(2)]
        Kb = [sb(f"Kb{u}", GROUPS * CC) for u in range(2)]
        Vt = [sb(f"Vt{u}", CC) for u in range(2)]
        PP = QVP[:, 3 * CB * 128:]
        PT = [PP[:, u * GROUPS * CC:(u + 1) * GROUPS * CC] for u in range(2)]
        at = w("conv01", 0, CC)
        res = [sb(f"res{u}", CC) for u in range(2)]
        xf = [[bdt[:, k * POSP * SEG + u * TILES * XW:k * POSP * SEG + (u + 1) * TILES * XW].rearrange("p (t c) -> p t c", c=XW)
               for u in range(4)] for k in range(2)]
        xfT = sb("xfT", CC)
        tT = sb("tT", CC)
        gc = sb("gc", TILES * IH)
        eg = sb("eg", TILES * IH)
        uc = [sb(f"uc{u}", TILES * IH) for u in range(2)]
        small = sb("small", 928)
        used = [0]

        def tiny(cols):
            used[0] += cols
            return small[:, used[0] - cols:used[0]]

        neg_half = tiny(8)
        half_pi = tiny(1)
        recip_ks = tiny(1)
        conv_scaled = w("conv01", 0, 4 * D)
        bq, bk, bv = tiny(1), tiny(1), tiny(1)
        qbias = tiny(1)
        wrdiff = tiny(1)
        qmb = tiny(QUADS)
        win = [bdt[:, 12288 + g * QUADS * WIN:12288 + (g + 1) * QUADS * WIN] for g in range(GROUPS)]
        par = r("act").rearrange("p (e f) -> p e f", f=5)
        absraw, expraw, clamp, nclamp, maxraw = (tiny(2 * (E + 1)) for _ in range(5))
        half_alpha = tiny(1)

        mx = [tiny(GROUPS * CB) for _ in range(2)]
        sm = tiny(GROUPS * CB)
        rc = [tiny(GROUPS * CB) for _ in range(2)]
        st2 = tiny(TILES * 6)
        mv2 = [tiny(TILES * 2) for _ in range(2)]
        vp2 = tiny(TILES)
        rstd_t = [tiny(TILES) for _ in range(2)]
        sl32 = [tiny(2 * TILES) for _ in range(4)]
        alpha, shift_p = tiny(E + 1), tiny(E + 1)
        rt2 = sem("slot_steps")
        lg = tiny(TILES * E)
        m8 = tiny(TILES * 8)
        ix8 = tiny(TILES * 8)
        ixf = tiny(2 * TILES)
        oh = tiny(2 * TILES * E)
        rb = tiny(TILES * E)
        ohr = w("wvp", 0, 2 * TILES * E)
        slf = tiny(2 * TILES)
        dd = tiny(TILES)
        ed = tiny(2 * TILES)
        both = [tiny(TILES * E // 2) for _ in range(2)]
        both = [b.bitcast(BF16) for b in both]
        seen = [tiny(E // 2).bitcast(BF16) for _ in range(2)]
        tsum = tiny(E)

        assert used[0] <= 928
        def wb(key):
            return SS[:, B_AT[key][0]:B_AT[key][1]]

        twice = bdt

        def window(g, t0):
            return QVP[:, (g * SEG + t0) * 128:(g * SEG + t0 + 1) * 128]

        def slide(v, first, count):
            return bass.AP(tensor=v.tensor, offset=v.offset + first, ap=[v.ap[0], [1, count], [1, SEG]])

        zeros = sb("zeros", XW)
        ps = ctx.enter_context(nc.psum_tensor("ps", [128, 8 * 512], F32))[:, :]

        def bank(n, k=1):
            return ps[:, n * 512:(n + k) * 512]

        taken = [0]

        def in_bdt(cols):
            taken[0] += cols
            return bdt[:, taken[0] - cols:taken[0]]

        xin = [in_bdt(128) for _ in range(4)]
        XT = [in_bdt(128) for _ in range(2)]
        va = [in_bdt(2 * D) for _ in range(2)]
        ka = [in_bdt(2 * D) for _ in range(2)]
        ra = [in_bdt(2 * D) for _ in range(2)]
        ca = [in_bdt(2 * D) for _ in range(8)]
        st = in_bdt(12)
        mv = [in_bdt(4) for _ in range(4)]
        pw = [in_bdt(4) for _ in range(2)]
        rr = [in_bdt(4) for _ in range(4)]
        rs = [in_bdt(6) for _ in range(2)]
        wn = [in_bdt(2 * D) for _ in range(2)]
        ha = [in_bdt(2 * D) for _ in range(4)]
        zpad = in_bdt(D)
        ones_a = in_bdt(128)
        b1f = in_bdt(IH // 3)[0:NB1 * 3 // IH]
        b1h = [in_bdt(IH // 6)[0:NB1 * 3 // IH].bitcast(BF16) for _ in range(3)]
        taken[0] = 4 * TILES * XW
        mine = [in_bdt(TW) for _ in range(RING)]
        xeT = [in_bdt(128) for _ in range(2)]
        teT = [in_bdt(128) for _ in range(2)]
        te = [in_bdt(IH) for _ in range(2)]
        cnt = in_bdt(8)
        cmp = in_bdt(ETILES)
        ones1 = in_bdt(128)
        rowi, rowe = in_bdt(ETILES), in_bdt(ETILES)
        rowf = in_bdt(4 * ETILES)
        cnt1 = in_bdt(2 * E)
        assert taken[0] <= POSP * SEG
        table = QVP[:, 0:E * TW]
        table3 = table.rearrange("p (e c) -> p e c", e=E)
        taken[0] = 0

        def in_qr(cols):
            taken[0] += cols
            return qr[:, taken[0] - cols:taken[0]]

        xe = [in_qr(XW) for _ in range(RING)]
        ye = [in_qr(D) for _ in range(RING)]
        place = [in_qr(1) for _ in range(RING)]
        ge, ee, ue = ([in_qr(IH) for _ in range(RING)] for _ in range(3))
        gk = [[bdt[:, (k * 4 + u) * CC:(k * 4 + u + 1) * CC] for u in range(4)] for k in range(2)]
        of = [bdt[:, (8 + u) * CC:(9 + u) * CC] for u in range(4)]

        ident = w("ident")
        weights_in, weights2_in, rows_in, b1_in = sem("weights_in"), sem("weights2_in"), sem("rows_in"), sem("b1_in")
        consts = sem("consts")
        setup_mm, wqkv_ready = sem("setup_mm"), sem("wqkv_ready")
        qbias_ready, win_ready, dve_setup = sem("qbias_ready"), sem("win_ready"), sem("dve_setup")
        params_abs, params_log, params_ready = sem("params_abs"), sem("params_log"), sem("params_ready")
        b1_parts, b1_stored, b1sh_in = sem("b1_parts"), sem("b1_stored"), sem("b1sh_in")
        pads, twice_in, twice_ready = sem("pads"), sems("twice_in", 2), sem("twice_ready")
        x_in = sems("x_in", 4)
        xt_ps, xt_sb, conv_ps = sem("xt_ps"), sem("xt_sb"), sem("conv_ps")
        biased, arg_steps, reduced = (sem(n) for n in ("biased", "arg_steps", "reduced"))
        absolute, cosine = sem("absolute"), sem("cosine")
        stats_a, mv_a, pw_a, rr_a, rs_a, wn_a = (sem(n) for n in ("stats_a", "mv_a", "pw_a", "rr_a", "rs_a", "wn_a"))
        ha_ready, ha_stored, wt_ps, wnT_ready = sem("ha_ready"), sems("ha_stored", 4), sem("wt_ps"), sem("wnT_ready")
        q_ps, qr_odd_ready, qr_ready, bd_ps, bdt_ready = sem("q_ps"), sem("qr_odd_ready"), sem("qr_ready"), sem("bd_ps"), sem("bdt_ready")
        k_ps, k_sb, v_ps, vt_ready, vb_ready = (sem(n) for n in ("k_ps", "k_sb", "v_ps", "vt_ready", "vb_ready"))
        qb_dve, qb_act, ac_ps, scores = sem("qb_dve"), sem("qb_act"), sem("ac_ps"), sem("scores")
        max_ready, shifted, exped, sums, rc_ready, probs, pt_ready = (sem(n) for n in (
            "max_ready", "shifted", "exped", "sums", "rc_ready", "probs", "pt_ready"))
        pv_ps, at_ready, wo_ps = sem("pv_ps"), sem("at_ready"), sem("wo_ps")
        res_in, h1_ready = sems("res_in", 2), sem("h1_ready")
        stats_d, mv_d, vp_d, rstd_d, xf_ready = (sem(n) for n in ("stats_d", "mv_d", "vp_d", "rstd_d", "xf_ready"))
        xft_ps, xft_sb, hs_ps = (sem(n) for n in ("xft_ps", "xft_sb", "hs_ps"))
        gc_ready, eg_act, eg_dve, uc_ready, ts_ready = (sem(n) for n in (
            "gc_ready", "eg_act", "eg_dve", "uc_ready", "ts_ready"))
        tt_ps, tt_sb, z_ps, z_added = (sem(n) for n in ("tt_ps", "tt_sb", "z_ps", "z_added"))
        tail_at, win_src, twin_ready = sem("tail_at"), sem("win_src"), sem("twin_ready")
        rt, ed_plus = sem("router_steps"), sem("ed_plus")
        both_ready, seen_ready, rank_ps, slot_ready, dd_ready, ed_ready, wts_ready = (sem(n) for n in (
            "both_ready", "seen_ready", "rank_ps", "slot_ready", "dd_ready", "ed_ready", "wts_ready"))
        sent = sems("sent", 4)
        experts_in, b1e_in, table_ready = sem("experts_in"), sem("b1e_in"), sem("table_ready")
        table_cleared, mine_ready = sem("table_cleared"), sem("mine_ready")
        zeros_ready, counts_ps, prep, prep_mm, map_ready, tails = (sem(n) for n in (
            "zeros_ready", "counts_ps", "prep", "prep_mm", "map_ready", "tails"))
        xe_in, ye_out = sems("xe_in", RING), sems("ye_out", RING)
        xet_ps, xet_sb, he_ps, ge_ready, ee_ready, m_ready, ue_ready, te_ready = (sem(n) for n in (
            "xet_ps", "xet_sb", "he_ps", "ge_ready", "ee_ready", "m_ready", "ue_ready", "te_ready"))
        tet_ps, tet_sb, ye_ps, ye_ready = (sem(n) for n in ("tet_ps", "tet_sb", "ye_ps", "ye_ready"))
        g_in, f_half, f_scaled, f_ready, stored = sems("g_in", 4), sem("f_half"), sem("f_scaled"), sem("f_ready"), sems("stored", 4)

        def cols(t, n, width=CC):
            return t[:, n * width:(n + 1) * width] if isinstance(n, int) else t[:, bass.ds(n * width, width)]

        def bchunk(n):
            v = bdt.rearrange("p (g c) -> p g c", g=GROUPS)
            return (v[:, :, n * CC:(n + 1) * CC] if isinstance(n, int) else v[:, :, bass.ds(n * CC, CC)])

        def scores4(s):
            return S[s % 2].rearrange("p (g b j) -> p g b j", g=GROUPS, j=SEG)

        def tiled(t, k=TILES):
            return t.rearrange("p (t d) -> p t d", t=k)

        def q_copies(n):
            at1 = POSP * SEG + n * CC
            return ((cols(qr, n), bank(n % 8), qbias),
                    (twice[0:64, n * CC:(n + 1) * CC], bank(n % 8)[0:64], qbias[0:64]),
                    (twice[64:128, at1:at1 + CC - 1], bank(n % 8)[64:128, 1:CC], qbias[64:128]))

        def weight_of(n, k, t):
            at0 = (2 * n + k) * TILES + t
            return wts[:, at0:at0 + 1] if isinstance(n, int) else wts[:, bass.ds(at0, 1)]

        block = ctx.enter_context(nc.Block())

        @block.sync
        def _(sp):
            sp.dma_start(W[:, 0:W_EARLY], weights[:, 0:W_EARLY]).then_inc(weights_in, 16)
            sp.dma_start(R, rows[0:1, :].to_broadcast([128, R_ALL])).then_inc(rows_in, 16)
            sp.dma_start(W[:, W_EARLY:], weights[:, W_EARLY:]).then_inc(weights2_in, 16)
            sp.dma_start(SS[:, 0:B_ALL], b_weights).then_inc(weights2_in, 16)
            sp.dma_start(b1f, b1.rearrange("o (p c) -> (o p) c", c=IH // 3)).then_inc(b1_in, 16)

            def load_x(n, s):
                after(sp, xt_ps, n - 3)
                sp.dma_start(xin[s % 4], x[n] if isinstance(n, int) else
                             x[bass.ds(n, 1)].rearrange("o p c -> (o p) c")).then_inc(x_in[s % 4], 16)

            def store_res(n, s):
                sp.wait_ge(ha_ready, n + 1)
                dst = res_d.rearrange("(p s) i d -> p i s d", s=2)
                src = ha[s % 4].rearrange("p (s d) -> p s d", s=2)
                for a, b in ((0, 112), (112, HALF)):
                    v = dst[a:b, n] if isinstance(n, int) else \
                        dst[a:b, bass.ds(n, 1)].rearrange("p o s d -> p (o s) d")
                    sp.dma_start(v, src[a:b]).then_inc(ha_stored[s % 4], 16)

            staged(sp, SEG, [(load_x, 0), (store_res, 12)])
            sp.wait_ge(pads, 1)
            sp.dma_start(res_d[POS:POSP].rearrange("b i d -> (b i) d"), zpad[0:64, :]).then_inc(pads, 16)
            sp.wait_ge(b1_parts, 5)
            for k in range(3):
                sp.dma_start(b1s_d[k].rearrange("(p c) -> p c", c=IH // 3), b1h[k]).then_inc(b1_stored, 16)
            sp.wait_ge(b1_stored, 48)
            sp.wait_ge(consts, 1)
            sp.dma_start(b1sh[0:3, E:], b1s_d[:, E * 2 * IH:]).then_inc(b1sh_in, 16)
            for q in ha_stored:
                sp.wait_ge(q, 2 * 16 * SEG // 4)
            sp.wait_ge(pads, 17)

            for n in range(CHUNKS):
                sp.wait_ge((qr_ready, qr_odd_ready)[n % 2], n // 2 * 3 + 1)
                c0, c1 = n * CC, n * CC + CC
                sp.dma_start(twice[64:128, c0:c1 - 1], qr[0:64, c0 + 1:c1]).then_inc(twice_in[n // 8], 16)
                sp.dma_start(twice[0:64, POSP * SEG + c0:POSP * SEG + c1], qr[64:128, c0:c1]).then_inc(twice_in[n // 8], 16)

            def load_res(n, s):
                after(sp, h1_ready, n - 1)
                v = res_d.rearrange("(t b) i d -> (b i) t d", b=128 // SEG)
                v = v[:, n * TILES:(n + 1) * TILES] if isinstance(n, int) else v[:, bass.ds(n * TILES, TILES)]
                sp.dma_start(tiled(res[s % 2]), v).then_inc(res_in[s % 2], 16)

            staged(sp, CHUNKS, [(load_res, 0)], 2)

            sp.wait_ge(pv_ps, CHUNKS)
            sp.dma_start(table3[:, :, TW1:TW2], w1).then_inc(experts_in, 16)
            sp.dma_start(table3[:, :, TW2:TPAR], w2).then_inc(experts_in, 16)
            sp.wait_ge(table_cleared, 1)
            sp.dma_start(table.bitcast(BF16).rearrange("p (e c) -> p e c", e=E)[0:3, :, 2 * TB1:],
                         b1s_d[:, 0:E * 2 * IH].rearrange("p (e c) -> p e c", e=E)).then_inc(b1e_in, 16)
            sp.wait_ge(zeros_ready, 1)
            sp.dma_start(xs_d[DUMMY:DUMMY + 128, :], zeros).then_inc(tails, 16)
            sp.wait_ge(tail_at, 1)
            for e in range(0, E, 2):
                c = sp.value_load(cnt1.bitcast(I32)[0:1, e:e + 1], min_val=0, max_val=E * REGION)
                sp.dma_start(xs_d[bass.ds(c, 128), :], zeros).then_inc(tails, 16)
            sp.wait_ge(map_ready, 1)
            sp.wait_ge(tails, 16 * (E + 1))
            for q in sent:
                sp.wait_ge(q, 16 * 2 * TOKT // 4)

            def tile_row(n):
                i = rowi.bitcast(I32)
                i = i[0:1, n:n + 1] if isinstance(n, int) else i[0:1, bass.ds(n, 1)]
                return sp.value_load(i, min_val=0, max_val=DUMMY)

            def load_xe(n, s):
                after(sp, ue_ready, n - RING + 1)
                sp.dma_start(xe[s], xs_d[bass.ds(tile_row(n), 128), :]).then_inc(xe_in[s], 16)

            staged(sp, ETILES, [(load_xe, 0)], RING)
            for q in ye_out:
                sp.wait_ge(q, 16 * ETILES // RING)

            def load_y(n, s):
                after(sp, f_ready, n - 3)
                for k in range(2):
                    v = ys_d[ETILES * 128 + k * TOKENS:ETILES * 128 + (k + 1) * TOKENS].rearrange("(t r) d -> r t d", r=128)
                    v = v[:, n * TILES:(n + 1) * TILES] if isinstance(n, int) else v[:, bass.ds(n * TILES, TILES)]
                    sp.dma_start(tiled(gk[k][s]), v).then_inc(g_in[s], 16)

            staged(sp, CHUNKS, [(load_y, 0)])
            for q in stored:
                sp.wait_ge(q, 16 * CHUNKS // 4)

        @block.gpsimd
        def _(pool):
            pool.memset(neg_half, -0.5)
            pool.memset(half_pi, float(np.pi / 2))
            pool.memset(onesb, 1.0)
            pool.memset(ones_a, 1.0)
            pool.memset(zpad, 0.0).then_inc(pads, 1)
            pool.memset(zeros, 0.0).then_inc(zeros_ready, 1)
            pool.memset(bdt[:, 12288:12288 + GROUPS * QUADS * WIN], 0.0)
            pool.memset(seen[0], 0.0)
            pool.memset(trib, 1.0)
            pool.memset(b1sh, 0.0)
            for t in Kb:
                pool.memset(t, 0.0)
            pool.memset(wnT[:, POS * SEG:], 0.0).then_inc(consts, 1)
            pool.wait_ge(consts, 1)
            pool.affine_select(out=trib, in_=trib, compare_op=ALU.is_gt, fill=0.0, base=0,
                               pattern=[[1, 128]], channel_multiplier=-1).then_inc(consts, 1)

            pool.wait_ge(b1_in, 16)
            pool.tensor_copy(b1h[0], b1f).then_inc(b1_parts, 1)
            for k in (1, 2):
                pool.wait_ge(b1_parts, 2 * k - 1)
                pool.tensor_tensor(b1f, b1f, b1h[k - 1], ALU.subtract).then_inc(b1_parts, 1)
                pool.wait_ge(b1_parts, 2 * k)
                pool.tensor_copy(b1h[k], b1f).then_inc(b1_parts, 1)

            def rstd_a(n, s):
                alone(pool, pw_a, n + 1)
                alone(pool, wn_a, n - 3)
                pool.tensor_tensor(rr[s % 4][0:HALF, :], pw[s % 2][0:HALF, :], neg_half[0:HALF, 0:4], ALU.pow).then_inc(rr_a, 1)

            def residual_a(n, s):
                alone(pool, rs_a, n + 1)
                if not isinstance(n, int) or n >= 4:
                    alone(pool, ha_stored[s % 4], (n - s % 4) * 8)
                for k in range(2):
                    c = ca[s % 8][0:HALF, k * D:(k + 1) * D]
                    o = pool.tensor_scalar(ha[s % 4][0:HALF, k * D:(k + 1) * D], c, rs[s % 2][0:HALF, k:k + 1],
                                           rs[s % 2][0:HALF, 2 + k:3 + k], ALU.mult, ALU.add)
                o.then_inc(ha_ready, 1)

            staged(pool, SEG, [(rstd_a, 0), (residual_a, 2)], 8, 4)

            def shift(n, s):
                alone(pool, max_ready, n + 1)
                m = mx[s % 2].rearrange("p (g b) -> p g b", g=GROUPS).unsqueeze(3).to_broadcast([128, GROUPS, CB, SEG])
                v = scores4(s)
                for g in range(GROUPS):
                    o = pool.tensor_tensor(v[:, g], v[:, g], m[:, g], ALU.subtract)
                o.then_inc(shifted, 1)

            def normalise(n, s):
                alone(pool, rc_ready, n + 1)
                m = rc[s % 2].rearrange("p (g b) -> p g b", g=GROUPS).unsqueeze(3).to_broadcast([128, GROUPS, CB, SEG])
                v = scores4(s)
                for g in range(GROUPS):
                    o = pool.tensor_tensor(v[:, g], v[:, g], m[:, g], ALU.mult)
                o.then_inc(probs, 1)

            def rstd(n, s):
                alone(pool, mv_d, n + 1)
                alone(pool, rstd_d, n)
                pool.tensor_scalar(vp2, tiled(mv2[s % 2])[:, :, 1], EPS, None, ALU.add).then_inc(vp_d, 1)
                alone(pool, vp_d, n + 1)
                pool.tensor_tensor(rstd_t[s % 2], vp2, neg_half[:, 0:TILES], ALU.pow).then_inc(rstd_d, 1)

            def dispatch(n, s):
                alone(pool, slot_ready, n + 1)
                alone(pool, twin_ready, n + 1)
                for k in range(2):
                    for t in range(TILES):
                        pool.indirect_dma_start(
                            out=xs_d, out_offset=bass.IndirectOffsetOnAxis(
                                ap=sl32[s].bitcast(I32)[:, k * TILES + t:k * TILES + t + 1], axis=0),
                            in_=xf[k][s][:, t], in_offset=None).then_inc(sent[s], 16)

            staged(pool, CHUNKS, [(dispatch, 6), (normalise, 2), (shift, 1), (rstd, 3)], 4, 2)

            def scatter(n, s):
                alone(pool, ye_ready, n + 1)
                pool.indirect_dma_start(
                    out=ys_d, out_offset=bass.IndirectOffsetOnAxis(ap=place[s].bitcast(I32), axis=0),
                    in_=ye[s], in_offset=None).then_inc(ye_out[s], 16)

            staged(pool, ETILES, [(scatter, 0)], RING)

            def add_first(n, s):
                alone(pool, f_half, n + 1)
                alone(pool, f_scaled, n + 1)
                pool.tensor_tensor(of[s], of[s], gk[0][s], ALU.add).then_inc(f_ready, 1)

            staged(pool, CHUNKS, [(add_first, 0)])

        @block.scalar
        def _(act):
            act.wait_ge(params_abs, 2)
            act.activation(expraw, absraw, ACT.Exp, scale=-1.0).then_inc(params_log, 1)
            act.wait_ge(params_log, 1)
            act.activation(absraw, expraw, ACT.Ln, bias=1.0).then_inc(params_log, 1)

            def xt_copy(n, s):
                act.wait_ge(xt_ps, n + 1)
                after(act, conv_ps, n - 1)
                act.activation(XT[s % 2], bank(s % 2)[:, 0:128], ACT.Copy).then_inc(xt_sb, 1)

            def conv_copy(n, s):
                act.wait_ge(conv_ps, n + 1)
                after(act, reduced, n - 1)
                act.activation(va[s % 2][0:HALF], bank(2 + s % 2)[0:HALF, 0:2 * D], ACT.Copy).then_inc(biased, 1)

            def norms(n, s):
                act.wait_ge(rs_a, n + 1)
                after(act, wt_ps, n - 1)
                for k in range(2):
                    i = act.activation(wn[s % 2][0:HALF, k * D:(k + 1) * D], ca[s % 8][0:HALF, k * D:(k + 1) * D], ACT.Identity,
                                       scale=rr[s % 4][0:HALF, 2 * k + 1:2 * k + 2], bias=rs[s % 2][0:HALF, 4 + k:5 + k])
                i.then_inc(wn_a, 1)

            def cosines(n, s):
                act.wait_ge(reduced, n + 1)
                act.activation(ra[s % 2][0:HALF], ra[s % 2][0:HALF], ACT.Abs).then_inc(absolute, 1)
                act.wait_ge(absolute, n + 1)
                after(act, ha_ready, n - 7)
                act.activation(ca[s % 8][0:HALF], ra[s % 2][0:HALF], ACT.Sin, bias=half_pi[0:HALF, :], scale=-1.0).then_inc(cosine, 1)

            def wt_copy(n, s):
                act.wait_ge(wt_ps, n + 1)
                v = wnT.rearrange("d (p s i) -> d i s p", s=2, i=SEG)
                v = v[:, n, :, 0:HALF] if isinstance(n, int) else v[:, bass.ds(n, 1), :, 0:HALF].rearrange("d o s p -> d (o s) p")
                act.activation(v, bank(4 + s % 2)[:, 0:2 * HALF].rearrange("d (s p) -> d s p", s=2), ACT.Copy).then_inc(wnT_ready, 1)

            act.wait_ge(consts, 1)
            staged(act, SEG, [(xt_copy, 0), (conv_copy, 2), (cosines, 4), (norms, 8), (wt_copy, 10)], 8, 4)

            act.wait_ge(qbias_ready, 1)
            act.wait_ge(win_ready, 1)
            for q in ha_stored:
                act.wait_ge(q, 2 * 16 * SEG // 4)
            act.wait_ge(b1_stored, 48)
            for n in range(0, CHUNKS, 2):
                act.wait_ge(q_ps, n + 1)
                for dst, src, bias in q_copies(n):
                    act.activation(dst, src, ACT.Identity, bias=bias).then_inc(qr_ready, 1)

            def k_copy(n, s):
                act.wait_ge(k_ps, n + 1)
                after(act, ac_ps, n - 1)
                for g in range(GROUPS):
                    rg = slice(g * 64, g * 64 + 64)
                    o = Kb[s % 2].rearrange("p (b g j) -> p g b j", g=GROUPS, j=SEG)[rg, g]
                    i = act.activation(o, bank(0)[rg].rearrange("p (b j) -> p b j", j=SEG), ACT.Identity, bias=bk[rg])
                i.then_inc(k_sb, 1)

            def q_expand(n, s):
                after(act, ac_ps, n - 1)
                if isinstance(n, int) and n == 0:
                    act.wait_ge(bd_ps, 2 * POSP // BIG)
                o = Qb[s % 2].rearrange("p (b q i) -> p q b i", q=QUADS, i=SEG)
                q = cols(qr, n).rearrange("p (b i) -> p b i", i=SEG)
                for k in (2, 3):
                    i = act.activation(o[:, k], q, ACT.Identity, scale=w("qmask", k, k + 1), bias=qmb[:, k:k + 1])
                i.then_inc(qb_act, 1)

            def exps(n, s):
                act.wait_ge(shifted, n + 1)
                act.activation(S[s % 2], S[s % 2], ACT.Exp, scale=SCALE).then_inc(exped, 1)

            def v_expand(n, s):
                act.wait_ge(vt_ready, n + 1)
                after(act, pv_ps, n)
                o = Vb.rearrange("p (g b q d) -> p q g b d", g=GROUPS, b=CB, q=QUADS)
                v = Vt[s % 2].rearrange("p (b g d) -> p g b d", g=GROUPS, d=DH)
                for k in range(QUADS):
                    i = act.activation(o[:, k], v, ACT.Copy, scale=w("pmask", k, k + 1))
                i.then_inc(vb_ready, 1)

            def at_copy(n, s):
                act.wait_ge(pv_ps, n + 1)
                after(act, wo_ps, n)
                act.activation(at, bank(3), ACT.Identity, bias=bv).then_inc(at_ready, 1)

            def xft_copy(n, s):
                act.wait_ge(xft_ps, n + 1)
                after(act, hs_ps, n)
                act.activation(xfT, bank(4), ACT.Copy).then_inc(xft_sb, 1)

            def twin(n, s):
                act.wait_ge(xf_ready, n + 1)
                act.activation(xf[1][s][:, :, 0:D], xf[0][s][:, :, 0:D], ACT.Copy).then_inc(twin_ready, 1)

            def swish_tanh(n, s):
                act.wait_ge(gc_ready, n + 1)
                act.activation(eg, gc, ACT.Tanh, scale=half_alpha).then_inc(eg_act, 1)

            def weight_exp(n, s):
                act.wait_ge(dd_ready, n + 1)
                act.activation(ed[:, 0:TILES], dd, ACT.Exp, scale=1.0)
                act.activation(ed[:, TILES:], dd, ACT.Exp, scale=-1.0).then_inc(ed_ready, 1)

            def tt_copy(n, s):
                act.wait_ge(tt_ps, n + 1)
                after(act, z_ps, n)
                act.activation(tT[0:IH, :], bank(4)[0:IH, :], ACT.Copy).then_inc(tt_sb, 1)

            act.wait_ge(params_ready, 1)
            staged(act, CHUNKS, [(q_expand, 0), (at_copy, 3), (weight_exp, 5), (tt_copy, 6), (swish_tanh, 5), (v_expand, 2), (exps, 1), (twin, 4), (xft_copy, 4), (k_copy, 0)], 4, 2)

            def fetch(n, s):
                i = rowe.bitcast(I32)
                i = i[0:1, n:n + 1] if isinstance(n, int) else i[0:1, bass.ds(n, 1)]
                c = act.value_load(i, min_val=0, max_val=(E - 1) * TW)
                act.activation(mine[s], table[:, bass.ds(c, TW)], ACT.Copy).then_inc(mine_ready, 1)

            def sigmoids(n, s):
                act.wait_ge(ge_ready, n + 1)
                act.activation(ee[s], ge[s], ACT.Sigmoid, scale=mine[s][:, TPAR + 5:TPAR + 6]).then_inc(ee_ready, 1)

            def tet_copy(n, s):
                act.wait_ge(tet_ps, n + 1)
                act.activation(teT[s % 2][0:IH, :], bank(4 + s % 2)[0:IH, 0:128], ACT.Copy).then_inc(tet_sb, 1)

            def y_copy(n, s):
                act.wait_ge(ye_ps, n + 1)
                if not isinstance(n, int) or n >= RING:
                    act.wait_ge(ye_out[s], (n - s) * 2)
                act.activation(ye[s], bank(6 + s % 2)[:, 0:D], ACT.Copy).then_inc(ye_ready, 1)

            act.wait_ge(pv_ps, CHUNKS)
            act.activation(table3[:, :, TB1:], zeros[:, 0:IH].unsqueeze(1).to_broadcast([128, E, IH]), ACT.Copy).then_inc(table_cleared, 1)
            act.wait_ge(tail_at, 1)
            for e in range(1, E, 2):
                c = act.value_load(cnt1.bitcast(I32)[0:1, e:e + 1], min_val=0, max_val=E * REGION)
                act.dma_start(xs_d[bass.ds(c, 128), :], zeros).then_inc(tails, 16)
            act.wait_ge(map_ready, 1)
            act.wait_ge(table_ready, 1)
            act.wait_ge(b1e_in, 16)
            staged(act, ETILES, [(y_copy, 8), (fetch, 0), (sigmoids, 3), (tet_copy, 6)], RING)

            def store_out(n, s):
                act.wait_ge(f_ready, n + 1)
                v = out.rearrange("(t b) i d -> (b i) t d", b=128 // SEG)
                v = v[:, n * TILES:(n + 1) * TILES] if isinstance(n, int) else v[:, bass.ds(n * TILES, TILES)]
                act.dma_start(v, tiled(of[s])).then_inc(stored[s], 16)

            def scale_first(n, s):
                alone(act, g_in[s], (n - s) * 8 + 32)
                for t in range(TILES):
                    c = slice(t * D, (t + 1) * D)
                    i = act.activation(gk[0][s][:, c], gk[0][s][:, c], ACT.Copy, scale=weight_of(n, 0, t))
                i.then_inc(f_scaled, 1)

            act.wait_ge(wts_ready, CHUNKS)
            staged(act, CHUNKS, [(scale_first, 0), (store_out, 2)])

        @block.tensor
        def _(pe):
            pe.wait_ge(weights_in, 16)
            pe.wait_ge(rows_in, 16)

            def xt(n, s):
                pe.wait_ge(x_in[s % 4], landed(n, s, 4))
                after(pe, xt_sb, n - 1)
                pe.transpose(bank(s % 2)[:, 0:128], xin[s % 4], ident).then_inc(xt_ps, 1)

            def conv(n, s):
                pe.wait_ge(xt_sb, n + 1)
                if isinstance(n, int) and n == 0:
                    pe.wait_ge(consts, 1)
                    pe.wait_ge(dve_setup, 2)
                after(pe, biased, n - 1)
                o, t = bank(2 + s % 2)[0:HALF], XT[s % 2]
                c01, c2, c12, c0 = w("conv01"), w("conv2"), w("conv12"), w("conv0")
                pe.matmul(o[:, 0:2 * D], ones_a[0:1, 0:HALF], r("cbias")[0:1].unsqueeze(1).to_broadcast([1, 2, D]),
                          start=True, stop=False)
                pe.matmul(o[:, 0:D], t[:, 0:HALF], c01, start=False, stop=False)
                pe.matmul(o[:, 0:D], t[:, 1:HALF + 1], c2, start=False, stop=False)
                pe.matmul(o[:, D:2 * D], t[:, 1:HALF + 1], c12, start=False, stop=False)
                pe.matmul(o[:, D:2 * D], t[:, 0:HALF], c0, start=False, stop=True).then_inc(conv_ps, 1)

            def wt(n, s):
                pe.wait_ge(wn_a, n + 1)
                after(pe, wnT_ready, n - 1)
                for k in range(2):
                    i = pe.transpose(bank(4 + s % 2)[:, k * HALF:(k + 1) * HALF],
                                     wn[s % 2][0:HALF, k * D:(k + 1) * D], ident[0:HALF, 0:HALF])
                i.then_inc(wt_ps, 1)

            pe.wait_ge(weights2_in, 32)
            for g in range(GROUPS):
                pe.matmul(bank(6)[:, g * SEG:(g + 1) * SEG], wb(f"wr{g}"), w("post"), start=True, stop=True)
            for k, key in enumerate(("wq", "wk", "wvp")):
                i = pe.matmul(bank(6)[:, 72 + 2 * k:73 + 2 * k], w(key), w("beta"), start=True, stop=True)
            i.then_inc(setup_mm, 1)
            staged(pe, SEG, [(xt, 0), (conv, 2), (wt, 10)], 8, 4)

            pe.wait_ge(wnT_ready, SEG)
            pe.wait_ge(wqkv_ready, 1)
            pe.wait_ge(consts, 2)

            for n in range(CHUNKS):
                if n >= 8:
                    pe.wait_ge((qr_ready, qr_odd_ready)[n % 2], ((n - 8) // 2 + 1) * 3)
                pe.matmul(bank(n % 8), w("wq"), cols(wnT, n), start=True, stop=True).then_inc(q_ps, 1)
            pe.wait_ge(win_ready, 1)

            def bd(c, g):
                after(pe, bdt_ready, 2 * c + g)
                pe.wait_ge(twice_ready, c + 1)
                o = bank(0, 8)
                q = twice[:, g * POSP * SEG:(g + 1) * POSP * SEG].rearrange("p (b i) -> p i b", i=SEG)
                for i in range(SEG):
                    m = pe.matmul(o[:, i * BIG:(i + 1) * BIG], window(g, SEG - 1 - i), q[:, i, c * BIG:(c + 1) * BIG],
                                  start=True, stop=True)
                m.then_inc(bd_ps, 1)

            for c in range(POSP // BIG):
                for g in range(GROUPS):
                    bd(c, g)

            def k_proj(n, s):
                after(pe, vt_ready, n)
                pe.matmul(bank(0), w("wk"), cols(wnT, n), start=True, stop=True).then_inc(k_ps, 1)

            def ac(n, s):
                pe.wait_ge(k_sb, n + 1)
                pe.wait_ge(qb_dve, n + 1)
                pe.wait_ge(qb_act, n + 1)
                after(pe, scores, n)
                for b in range(CB):
                    i = pe.matmul(bank(1, 2)[:, b * 64:(b + 1) * 64], Qb[s % 2][:, b * 128:(b + 1) * 128],
                                  Kb[s % 2][:, b * 64:(b + 1) * 64], start=True, stop=True)
                i.then_inc(ac_ps, 1)

            def v_proj(n, s):
                pe.wait_ge(k_sb, n + 1)
                pe.matmul(bank(0), w("wv"), cols(wnT, n), start=True, stop=True).then_inc(v_ps, 1)

            def pv(n, s):
                pe.wait_ge(pt_ready, n + 1)
                pe.wait_ge(vb_ready, n + 1)
                after(pe, h1_ready, n)
                for g in range(GROUPS):
                    for b in range(CB):
                        i = pe.matmul(bank(3)[g * 64:g * 64 + 64, b * SEG:(b + 1) * SEG],
                                      Vb[:, (g * CB + b) * 64:(g * CB + b + 1) * 64],
                                      PT[s % 2][:, (g * CB + b) * SEG:(g * CB + b + 1) * SEG], start=True, stop=True)
                i.then_inc(pv_ps, 1)

            def wo(n, s):
                pe.wait_ge(at_ready, n + 1)
                for t in range(TILES):
                    i = pe.matmul(bank(3)[:, t * D:(t + 1) * D], at[:, t * 128:(t + 1) * 128], w("wo"), start=True, stop=True)
                i.then_inc(wo_ps, 1)

            def xft(n, s):
                pe.wait_ge(xf_ready, n + 1)
                after(pe, z_added, n - 1)
                for t in range(TILES):
                    i = pe.transpose(bank(4)[:, t * 128:(t + 1) * 128], xf[0][s][:, t, 0:D], ident)
                i.then_inc(xft_ps, 1)

            def first_products(n, s):
                pe.wait_ge(xft_sb, n + 1)
                after(pe, uc_ready, n)
                both_w = W[:, W_AT["gate"][0]:W_AT["ws1"][1]]
                for t in range(0, TILES, 2):
                    o = bank(6 + t // 2)[:, 0:2 * FIRST]
                    pe.matmul(o, onesb[0:3, :], b1sh[0:3, :].unsqueeze(1).to_broadcast([3, 2, FIRST]), start=True, stop=False)
                    for k in range(2):
                        i = pe.matmul(o[:, k * FIRST:(k + 1) * FIRST], xfT[:, (t + k) * 128:(t + k + 1) * 128], both_w,
                                      start=False, stop=(k == 1))
                i.then_inc(hs_ps, 1)

            def ranks(n, s):
                pe.wait_ge(both_ready, n + 1)
                a = both[s % 2]
                o = bank(5)[:, 64:64 + TILES * E]
                pe.matmul(o, trib, a, start=True, stop=False)
                pe.matmul(o, onesb, seen[s % 2].unsqueeze(1).to_broadcast([128, TILES, E]), start=False, stop=False)
                for t in range(TILES - 1):
                    k = TILES - 1 - t
                    i = pe.matmul(o[:, (t + 1) * E:], onesb, a[:, t * E:(t + 1) * E].unsqueeze(1).to_broadcast([128, k, E]),
                                  start=False, stop=(t == TILES - 2))
                i.then_inc(rank_ps, 1)

            def turn_t(n, s):
                pe.wait_ge(ts_ready, n + 1)
                pe.wait_ge(xft_sb, min(n + 2, CHUNKS) if isinstance(n, int) else n + 2)
                for t in range(TILES):
                    i = pe.transpose(bank(4)[0:IH, t * 128:(t + 1) * 128], uc[s % 2][:, t * IH:(t + 1) * IH], ident)
                i.then_inc(tt_ps, 1)

            def z_products(n, s):
                pe.wait_ge(tt_sb, n + 1)
                for t in range(TILES):
                    i = pe.matmul(bank(4)[:, t * D:(t + 1) * D], tT[0:IH + 1, t * 128:(t + 1) * 128], w("ws2")[0:IH + 1],
                                  start=True, stop=True)
                i.then_inc(z_ps, 1)

            pe.wait_ge(bdt_ready, 2 * POSP // BIG)
            pe.wait_ge(params_ready, 1)
            pe.wait_ge(b1sh_in, 16)
            staged(pe, CHUNKS, [(ac, 1), (turn_t, 6), (pv, 3), (v_proj, 1), (wo, 3), (z_products, 6), (ranks, 5), (xft, 4), (k_proj, 0), (first_products, 4)], 4, 2)

            pe.wait_ge(seen_ready, CHUNKS)
            pe.matmul(bank(0)[:, 0:E], onesb, seen[CHUNKS % 2], start=True, stop=True)
            pe.matmul(bank(0)[0:E, 32:33], seen[CHUNKS % 2], onesb[:, 0:1], start=True, stop=True).then_inc(counts_ps, 1)
            pe.wait_ge(prep, 3)
            pe.matmul(bank(0)[0:E, 64:65], w("tri16")[0:E], cnt[0:E, 2:3], start=True, stop=True).then_inc(prep_mm, 1)
            pe.wait_ge(prep, 5)
            pe.matmul(bank(0)[0:1, 128:128 + ETILES], ones1[0:E, 0:1], cmp[0:E], start=True, stop=True)
            pe.matmul(bank(1)[0:1, 0:ETILES], cnt[0:E, 2:3], cmp[0:E], start=True, stop=True).then_inc(prep_mm, 1)

            pe.wait_ge(map_ready, 1)

            def xet(n, s):
                pe.wait_ge(xe_in[s], landed(n, s, RING))
                pe.transpose(bank(s % 2)[:, 0:128], xe[s][:, 0:D], ident).then_inc(xet_ps, 1)

            def he(n, s):
                pe.wait_ge(xet_sb, n + 1)
                pe.wait_ge(mine_ready, n + 1)
                after(pe, ue_ready, n - 1)
                o = bank(2 + s % 2)[:, 0:2 * IH]
                pe.matmul(o, onesb[0:3, :], mine[s].bitcast(BF16)[0:3, 2 * TB1:], start=True, stop=False)
                pe.matmul(o, xeT[s % 2], mine[s][:, TW1:TW2], start=False, stop=True).then_inc(he_ps, 1)

            def tet(n, s):
                pe.wait_ge(te_ready, n + 1)
                pe.transpose(bank(4 + s % 2)[0:IH, 0:128], te[s % 2], ident).then_inc(tet_ps, 1)

            def yt(n, s):
                pe.wait_ge(tet_sb, n + 1)
                after(pe, ye_ready, n - 1)
                pe.matmul(bank(6 + s % 2)[:, 0:D], teT[s % 2][0:IH + 1, :], mine[s][0:IH + 1, TW2:TPAR],
                          start=True, stop=True).then_inc(ye_ps, 1)

            staged(pe, ETILES, [(yt, 8), (tet, 6), (he, 2), (xet, 0)], RING)

        @block.vector
        def _(dve):
            dve.memset(tT[96:97, :], 1.0)
            dve.wait_ge(weights_in, 16)
            dve.wait_ge(rows_in, 16)
            dve.reciprocal(recip_ks, r("kscale")).then_inc(dve_setup, 1)
            dve.wait_ge(dve_setup, 1)
            dve.tensor_scalar(conv_scaled, conv_scaled, recip_ks, None, ALU.mult).then_inc(dve_setup, 1)
            raw = par[:, :, 3:5]
            dve.scalar_tensor_tensor(absraw.rearrange("p (e f) -> p e f", f=2), raw, -1.0, raw, ALU.mult, ALU.max).then_inc(params_abs, 1)
            dve.tensor_scalar(maxraw.rearrange("p (e f) -> p e f", f=2), raw, 0.0, None, ALU.max).then_inc(params_abs, 1)
            dve.tensor_scalar(half_alpha, par[:, E, 0:1], 0.5, None, ALU.mult)
            dve.tensor_copy(alpha, par[:, :, 0])
            dve.tensor_copy(shift_p, par[:, :, 2])
            dve.wait_ge(params_log, 2)
            dve.tensor_tensor(clamp, maxraw, absraw, ALU.add).then_inc(dve_setup, 1)
            dve.wait_ge(dve_setup, 3)
            dve.tensor_scalar(nclamp, clamp, -1.0, None, ALU.mult)
            dve.wait_ge(weights2_in, 32)
            dve.tensor_scalar(w("ws2")[0:IH], w("ws2")[0:IH], par[0:IH, E, 1:2], 0.5, ALU.mult, ALU.mult).then_inc(params_ready, 1)
            dve.wait_ge(setup_mm, 1)
            dve.tensor_tensor(wrdiff, w("rwb"), w("rrb"), ALU.subtract)
            dve.tensor_copy(bk, bank(6)[:, 74:75])
            dve.tensor_copy(bv, bank(6)[:, 76:77])
            dve.tensor_tensor(qbias, bank(6)[:, 72:73], w("rrb"), ALU.add).then_inc(qbias_ready, 1)
            for key in ("wq", "wk", "wv"):
                i = dve.tensor_scalar(w(key), w(key), w("gamma"), None, ALU.mult)
            i.then_inc(wqkv_ready, 1)
            dve.wait_ge(consts, 1)
            dve.wait_ge(qbias_ready, 1)
            for k in range(QUADS):
                for g in range(GROUPS):
                    a = win[g].rearrange("p (q t) -> p q t", q=QUADS)[:, k]
                    m = w("qmask", k, k + 1)
                    rk = bank(6)[:, g * SEG:(g + 1) * SEG]
                    dve.tensor_scalar(a[0:64, 0:SEG], rk[0:64], m[0:64], None, ALU.mult)
                    dve.tensor_scalar(a[64:128, SEG + 1:], rk[64:128, 0:SEG - 2], m[64:128], None, ALU.mult)
                i = dve.tensor_scalar(qmb[:, k:k + 1], wrdiff, w("qmask", k, k + 1), None, ALU.mult)
            i.then_inc(win_src, 1)
            half = slice(0, HALF)

            def round_turns(n, s):
                dve.wait_ge(biased, n + 1)
                dve.tensor_scalar(ka[s % 2][half], va[s % 2][half], INV_TWO_PI, MAGIC, ALU.mult, ALU.add).then_inc(arg_steps, 1)

            def whole_turns(n, s):
                dve.wait_ge(arg_steps, 3 * n + 1)
                dve.tensor_scalar(ka[s % 2][half], ka[s % 2][half], MAGIC, None, ALU.subtract).then_inc(arg_steps, 1)

            def reduce_hi(n, s):
                dve.wait_ge(arg_steps, 3 * n + 2)
                v = va[s % 2][half]
                dve.scalar_tensor_tensor(v, ka[s % 2][half], -TWO_PI_HI, v, ALU.mult, ALU.add).then_inc(arg_steps, 1)

            def reduce_lo(n, s):
                dve.wait_ge(arg_steps, 3 * n + 3)
                after(dve, cosine, n - 1)
                dve.scalar_tensor_tensor(ra[s % 2][half], ka[s % 2][half], -TWO_PI_LO, va[s % 2][half],
                                         ALU.mult, ALU.add).then_inc(reduced, 1)

            def stats(n, s):
                dve.wait_ge(cosine, n + 1)
                for k in range(2):
                    i = dve.bn_stats(st[half, 6 * k:6 * k + 6], ca[s % 8][half, k * D:(k + 1) * D])
                i.then_inc(stats_a, 1)

            def mean_var(n, s):
                alone(dve, stats_a, n + 1)
                for k in range(2):
                    i = dve.bn_aggr(mv[s % 4][half, 2 * k:2 * k + 2], st[half, 6 * k:6 * k + 6])
                i.then_inc(mv_a, 1)

            def powers_of(n, s):
                dve.wait_ge(mv_a, n + 1)
                after(dve, rr_a, n - 1)
                m = mv[s % 4][half].rearrange("p (s k) -> p s k", s=2)
                o = pw[s % 2][half].rearrange("p (s k) -> p s k", s=2)
                c = 1 / COS_NORM ** 2
                dve.tensor_scalar(o[:, :, 0], m[:, :, 1], c * EPS, None, ALU.add)
                dve.tensor_scalar(o[:, :, 1], m[:, :, 1], 1 + EPS, c * EPS * EPS, ALU.mult, ALU.add).then_inc(pw_a, 1)

            def residual_scale(n, s):
                dve.wait_ge(rr_a, n + 1)
                m, q = mv[s % 4][half].rearrange("p (s k) -> p s k", s=2), rr[s % 4][half].rearrange("p (s k) -> p s k", s=2)
                after(dve, ha_ready, n - 1)
                after(dve, wn_a, n - 1)
                o = rs[s % 2][half]
                dve.tensor_scalar(o[:, 0:2], q[:, :, 0], COS_NORM, None, ALU.add)
                dve.scalar_tensor_tensor(o[:, 2:4], m[:, :, 0], -1.0, q[:, :, 0], ALU.mult, ALU.mult)
                dve.scalar_tensor_tensor(o[:, 4:6], m[:, :, 0], -1.0, q[:, :, 1], ALU.mult, ALU.mult).then_inc(rs_a, 1)

            staged(dve, SEG, [(round_turns, 0), (stats, 2), (whole_turns, 0), (mean_var, 2), (reduce_hi, 0), (powers_of, 2),
                              (reduce_lo, 0), (residual_scale, 4)], 8, 4)

            dve.wait_ge(win_src, 1)
            for g in range(GROUPS):
                for k in range(QUADS):
                    i = dve.tensor_copy(QVP[:, g * SEG * 128:(g + 1) * SEG * 128].rearrange("p (t q j) -> p q t j", q=QUADS, j=SEG)[:, k],
                                        slide(win[g].rearrange("p (q t) -> p q t", q=QUADS)[:, k], 0, SEG))
            i.then_inc(win_ready, 1)

            for q in ha_stored:
                dve.wait_ge(q, 2 * 16 * SEG // 4)
            dve.wait_ge(pads, 17)
            dve.wait_ge(b1_stored, 48)
            for n in range(1, CHUNKS, 2):
                dve.wait_ge(q_ps, n + 1)
                for dst, src, bias in q_copies(n):
                    dve.tensor_scalar(dst, src, bias, None, ALU.add).then_inc(qr_odd_ready, 1)
            dve.wait_ge(qr_ready, 3 * CHUNKS // 2)
            dve.wait_ge(qr_odd_ready, 3 * CHUNKS // 2)
            last = twice.rearrange("p (g c b i) -> p g c b i", g=GROUPS, c=2, i=SEG)[64:128, :, :, :, SEG - 1]
            for c in range(2):
                dve.wait_ge(twice_in[c], 16 * CHUNKS)
                dve.memset(last[:, :, c], 0.0).then_inc(twice_ready, 1)
            for n in range(2 * POSP // BIG):
                g, c = n % 2, n // 2
                dve.wait_ge(bd_ps, n + 1)
                o = bdt[:, (g * POSP + c * BIG) * SEG:(g * POSP + (c + 1) * BIG) * SEG]
                dve.transpose(o, bank(0, 8).rearrange("p (i b) -> p b i", i=SEG)).then_inc(bdt_ready, 1)

            dve.wait_ge(params_ready, 1)
            dve.wait_ge(win_ready, 1)

            def q_expand(n, s):
                after(dve, ac_ps, n - 1)
                o = Qb[s % 2].rearrange("p (b q i) -> p q b i", q=QUADS, i=SEG)
                q = cols(qr, n).rearrange("p (b i) -> p b i", i=SEG)
                for k in (0, 1):
                    i = dve.tensor_scalar(o[:, k], q, w("qmask", k, k + 1), qmb[:, k:k + 1], ALU.mult, ALU.add)
                i.then_inc(qb_dve, 1)

            def v_turn(n, s):
                dve.wait_ge(v_ps, n + 1)
                after(dve, vb_ready, n - 1)
                dve.transpose(Vt[s % 2], bank(0)).then_inc(vt_ready, 1)

            def add_scores(n, s):
                dve.wait_ge(ac_ps, n + 1)
                dve.tensor_tensor(scores4(s), bank(1, 2).rearrange("p (b g j) -> p g b j", g=GROUPS, j=SEG),
                                  bchunk(n).rearrange("p g (b j) -> p g b j", j=SEG), ALU.add).then_inc(scores, 1)
                dve.wait_ge(scores, n + 1)
                after(dve, shifted, n - 1)
                dve.tensor_reduce(mx[s % 2].rearrange("p (g b) -> p g b", g=GROUPS), scores4(s), AX, ALU.max).then_inc(max_ready, 1)

            def sum_exps(n, s):
                dve.wait_ge(exped, n + 1)
                dve.tensor_reduce(sm.rearrange("p (g b) -> p g b", g=GROUPS), scores4(s), AX, ALU.add).then_inc(sums, 1)
                dve.wait_ge(sums, n + 1)
                after(dve, probs, n - 1)
                dve.reciprocal(rc[s % 2], sm).then_inc(rc_ready, 1)

            def turn_p(n, s):
                dve.wait_ge(probs, n + 1)
                after(dve, pv_ps, n - 1)
                dve.transpose(PT[s % 2], S[s % 2]).then_inc(pt_ready, 1)

            def add_h1(n, s):
                dve.wait_ge(wo_ps, n + 1)
                dve.wait_ge(res_in[s % 2], landed(n, s, 2))
                dve.tensor_tensor(cols(wnT, n), bank(3), res[s % 2], ALU.add).then_inc(h1_ready, 1)
                dve.wait_ge(h1_ready, n + 1)
                for t in range(TILES):
                    i = dve.bn_stats(st2[:, t * 6:t * 6 + 6], cols(wnT, n * TILES + t, D))
                i.then_inc(stats_d, 1)
                alone(dve, stats_d, n + 1)
                for t in range(TILES):
                    i = dve.bn_aggr(mv2[s % 2][:, 2 * t:2 * t + 2], st2[:, t * 6:t * 6 + 6])
                i.then_inc(mv_d, 1)

            def norm_ffn(n, s):
                dve.wait_ge(rstd_d, n + 1)
                if not isinstance(n, int) or n >= 4:
                    dve.wait_ge(sent[s], (n - s) * 32)
                for k in range(2):
                    dve.tensor_scalar(xf[k][s][:, :, D], cols(w("place"), n, TILES), float(ETILES * 128 + k * TOKENS), None, ALU.add)
                for t in range(TILES):
                    i = dve.tensor_scalar(xf[0][s][:, t, 0:D], cols(wnT, n * TILES + t, D), mv2[s % 2][:, 2 * t:2 * t + 1],
                                          rstd_t[s % 2][:, t:t + 1], ALU.subtract, ALU.mult)
                i.then_inc(xf_ready, 1)

            RT = 6

            def router(n, s):
                def step(i):
                    i.then_inc(rt, 1)

                def done(k):
                    alone(dve, rt, n * RT + k)

                dve.wait_ge(hs_ps, n + 1)
                v = bank(6, 2).rearrange("p (a c) -> p a c", a=2)[:, :, 0:2 * FIRST].rearrange("p a (k c) -> p a k c", k=2)
                step(dve.tensor_tensor(lg.rearrange("p (a k e) -> p a k e", a=2, e=E), v[:, :, :, 0:E],
                                       r("gateb").unsqueeze(1).unsqueeze(1).to_broadcast([128, 2, 2, E]), ALU.add))
                done(1)
                for t in range(TILES):
                    i = dve.max(m8[:, t * 8:t * 8 + 8], lg[:, t * E:(t + 1) * E])
                step(i)
                done(2)
                for t in range(TILES):
                    i = dve.max_index(ix8.bitcast(U32)[:, t * 8:t * 8 + 8], m8[:, t * 8:t * 8 + 8], lg[:, t * E:(t + 1) * E])
                step(i)
                m3 = m8.rearrange("p (t k) -> p t k", k=8)
                after(dve, ed_ready, n)
                dve.tensor_tensor(dd, m3[:, :, 1], m3[:, :, 0], ALU.subtract).then_inc(dd_ready, 1)
                done(3)
                step(dve.tensor_copy(ixf.rearrange("p (k t) -> p t k", k=2), ix8.bitcast(U32).rearrange("p (t k) -> p t k", k=8)[:, :, 0:2]))
                done(4)
                o4 = oh.rearrange("p (k t e) -> p k t e", k=2, e=E)
                i3 = r("iota16").unsqueeze(1).to_broadcast([128, TILES, E])
                for k in range(2):
                    i = dve.tensor_tensor(o4[:, k], i3, ixf[:, k * TILES:(k + 1) * TILES].unsqueeze(2).to_broadcast([128, TILES, E]), ALU.is_equal)
                step(i)
                done(5)
                after(dve, rank_ps, n - 1)
                dve.tensor_tensor(both[s % 2], oh[:, 0:TILES * E], oh[:, TILES * E:], ALU.add).then_inc(both_ready, 1)
                dve.wait_ge(both_ready, n + 1)
                step(dve.tensor_reduce(tsum, both[s % 2].rearrange("p (t e) -> p e t", e=E), AX, ALU.add))
                done(6)
                after(dve, rank_ps, n)
                after(dve, seen_ready, n)
                dve.tensor_tensor(seen[(s + 1) % 2], seen[s % 2], tsum, ALU.add).then_inc(seen_ready, 1)

            def weights_of(n, s):
                dve.wait_ge(ed_ready, n + 1)
                dve.tensor_scalar(ed, ed, 1.0, None, ALU.add).then_inc(ed_plus, 1)
                dve.wait_ge(ed_plus, n + 1)
                dve.reciprocal(cols(wts, n, 2 * TILES), ed).then_inc(wts_ready, 1)

            def slots_of(n, s):
                def done(k):
                    dve.wait_ge(rt2, n * 3 + k)

                dve.wait_ge(rank_ps, n + 1)
                dve.tensor_tensor(rb.rearrange("p (t e) -> p t e", e=E), bank(5)[:, 64:64 + TILES * E].rearrange("p (t e) -> p t e", e=E),
                                  r("ebase").unsqueeze(1).to_broadcast([128, TILES, E]), ALU.add).then_inc(rt2, 1)
                done(1)
                dve.tensor_tensor(ohr.rearrange("p (k c) -> p k c", k=2), oh.rearrange("p (k c) -> p k c", k=2),
                                  rb.unsqueeze(1).to_broadcast([128, 2, TILES * E]), ALU.mult).then_inc(rt2, 1)
                done(2)
                dve.tensor_reduce(slf, ohr.rearrange("p (kt e) -> p kt e", e=E), AX, ALU.add).then_inc(rt2, 1)
                done(3)
                dve.tensor_copy(sl32[s].bitcast(I32), slf).then_inc(slot_ready, 1)

            def swiglu_a(n, s):
                hs = bank(6, 2).rearrange("p (a c) -> p a c", a=2)[:, :, 0:2 * FIRST].rearrange("p a (k c) -> p a k c", k=2)
                gh, uh = (hs[:, :, :, E + u * IH:E + (u + 1) * IH] for u in range(2))
                gv, uv = (t.rearrange("p (a k h) -> p a k h", a=2, k=2) for t in (gc, uc[s % 2]))
                dve.wait_ge(hs_ps, n + 1)
                for a in range(2):
                    i = dve.tensor_scalar(gv[:, a], gh[:, a], clamp[:, 2 * E:2 * E + 1], nclamp[:, 2 * E:2 * E + 1], ALU.min, ALU.max)
                i.then_inc(gc_ready, 1)
                after(dve, tt_ps, n - 1)
                for a in range(2):
                    i = dve.tensor_scalar(uv[:, a], uh[:, a], clamp[:, 2 * E + 1:2 * E + 2], nclamp[:, 2 * E + 1:2 * E + 2], ALU.min, ALU.max)
                i.then_inc(uc_ready, 1)

            def swiglu_b(n, s):
                dve.wait_ge(eg_act, n + 1)
                dve.scalar_tensor_tensor(eg, eg, 1.0, gc, ALU.add, ALU.mult).then_inc(eg_dve, 1)
                dve.wait_ge(eg_dve, n + 1)
                dve.scalar_tensor_tensor(uc[s % 2], uc[s % 2], par[:, E, 2:3], eg, ALU.add, ALU.mult).then_inc(ts_ready, 1)

            def add_z(n, s):
                dve.wait_ge(z_ps, n + 1)
                dve.tensor_tensor(cols(wnT, n), bank(4), cols(wnT, n), ALU.add).then_inc(z_added, 1)

            staged(dve, CHUNKS, [(sum_exps, 2), (norm_ffn, 4), (router, 5), (add_scores, 1), (swiglu_a, 5), (q_expand, 0), (v_turn, 1), (add_h1, 3), (add_z, 6), (swiglu_b, 5), (weights_of, 5), (slots_of, 5), (turn_p, 2)], 4, 2)

            dve.wait_ge(counts_ps, 1)
            dve.tensor_tensor(cnt1[0:1, 0:E].bitcast(I32), bank(0)[0:1, 0:E], r("ebase")[0:1], ALU.add).then_inc(tail_at, 1)
            dve.memset(ones1, 1.0)
            for t in teT:
                dve.memset(t[96:97, :], 1.0)
            ci = cnt.bitcast(I32)
            dve.tensor_scalar(ci[0:E, 0:1], bank(0)[0:E, 32:33], 127.0, None, ALU.add).then_inc(prep, 1)
            dve.wait_ge(prep, 1)
            dve.tensor_scalar(ci[0:E, 1:2], ci[0:E, 0:1], 7, None, ALU.arith_shift_right).then_inc(prep, 1)
            dve.wait_ge(prep, 2)
            dve.tensor_copy(cnt[0:E, 2:3], ci[0:E, 1:2]).then_inc(prep, 1)
            dve.wait_ge(prep, 3)
            dve.wait_ge(prep_mm, 1)
            dve.tensor_copy(cnt[0:E, 3:4], bank(0)[0:E, 64:65]).then_inc(prep, 1)
            dve.wait_ge(prep, 4)
            dve.tensor_scalar(cmp[0:E], w("iota")[0:E], cnt[0:E, 3:4], None, ALU.is_ge).then_inc(prep, 1)
            dve.wait_ge(prep_mm, 2)
            ex, first, use, tmp = (rowf[0:1, k * ETILES:(k + 1) * ETILES] for k in range(4))
            dve.tensor_copy(ex, bank(0)[0:1, 128:128 + ETILES])
            dve.tensor_tensor(first, w("iota")[0:1], bank(1)[0:1, 0:ETILES], ALU.subtract).then_inc(prep, 1)
            dve.wait_ge(prep, 6)
            dve.tensor_scalar(use, ex, float(E), None, ALU.is_lt)
            dve.tensor_scalar(tmp, ex, float(REGION), -float(DUMMY), ALU.mult, ALU.add).then_inc(prep, 1)
            dve.wait_ge(prep, 7)
            dve.scalar_tensor_tensor(tmp, first, 128.0, tmp, ALU.mult, ALU.add).then_inc(prep, 1)
            dve.wait_ge(prep, 8)
            dve.tensor_tensor(tmp, tmp, use, ALU.mult)
            dve.scalar_tensor_tensor(rowe[0:1].bitcast(I32), ex, float(TW), use, ALU.mult, ALU.mult).then_inc(prep, 1)
            dve.wait_ge(prep, 9)
            dve.tensor_scalar(rowi[0:1].bitcast(I32), tmp, float(DUMMY), None, ALU.add).then_inc(map_ready, 1)
            dve.wait_ge(experts_in, 32)
            for k, v in enumerate((clamp[:, 0:2 * E:2], nclamp[:, 0:2 * E:2], clamp[:, 1:2 * E:2], nclamp[:, 1:2 * E:2],
                                   shift_p[:, 0:E], alpha[:, 0:E], alpha[:, 0:E], alpha[:, 0:E])):
                dve.tensor_copy(table3[:, :, TPAR + k], v)
            dve.tensor_tensor(table3[0:IH, :, TW2:TPAR], table3[0:IH, :, TW2:TPAR],
                              par[0:IH, 0:E, 1].unsqueeze(2).to_broadcast([IH, E, D]), ALU.mult).then_inc(table_ready, 1)

            def xet_copy(n, s):
                dve.wait_ge(xet_ps, n + 1)
                dve.tensor_copy(xeT[s % 2], bank(s % 2)[:, 0:128]).then_inc(xet_sb, 1)

            def clip_e(n, s):
                dve.wait_ge(he_ps, n + 1)
                if not isinstance(n, int) or n >= RING:
                    dve.wait_ge(ye_out[s], (n - s) * 2)
                dve.tensor_tensor(place[s].bitcast(I32), xe[s][:, D:XW], cols(w("place"), n, 1), ALU.max)
                h, p = bank(2 + s % 2), mine[s][:, TPAR:]
                dve.tensor_scalar(ge[s], h[:, 0:IH], p[:, 0:1], p[:, 1:2], ALU.min, ALU.max).then_inc(ge_ready, 1)
                dve.tensor_scalar(ue[s], h[:, IH:2 * IH], p[:, 2:3], p[:, 3:4], ALU.min, ALU.max).then_inc(ue_ready, 1)

            def gate_e(n, s):
                dve.wait_ge(ee_ready, n + 1)
                dve.tensor_tensor(ee[s], ge[s], ee[s], ALU.mult).then_inc(m_ready, 1)
                dve.wait_ge(m_ready, n + 1)
                after(dve, tet_ps, n - 1)
                dve.scalar_tensor_tensor(te[s % 2], ue[s], mine[s][:, TPAR + 4:TPAR + 5], ee[s], ALU.add, ALU.mult).then_inc(te_ready, 1)

            staged(dve, ETILES, [(clip_e, 2), (xet_copy, 0), (gate_e, 4)], RING)

            def combine(n, s):
                dve.wait_ge(g_in[s], (n - s) * 8 + 32)
                if not isinstance(n, int) or n >= 4:
                    dve.wait_ge(stored[s], (n - s) * 4)
                for t in range(TILES):
                    c = slice(t * D, (t + 1) * D)
                    i = dve.scalar_tensor_tensor(of[s][:, c], gk[1][s][:, c], weight_of(n, 1, t), cols(wnT, n * TILES + t, D),
                                                 ALU.mult, ALU.add)
                i.then_inc(f_half, 1)

            dve.wait_ge(wts_ready, CHUNKS)
            dve.wait_ge(z_added, CHUNKS)
            staged(dve, CHUNKS, [(combine, 0)])


def kernel(**inputs):
    import concourse.bacc as bacc
    from concourse.bass_utils import run_bass_kernel_spmd

    f = np.float32
    a = {k: np.asarray(v) for k, v in inputs.items()}
    p = "L0_attn_"
    perm = np.array([(2 * q + g) * DH + d for g in range(GROUPS) for q in range(QUADS) for d in range(DH)])
    wide = np.zeros((128, W_ALL), f)

    def put(key, v):
        v = np.asarray(v)
        wide[:v.shape[0], W_AT[key][0]:W_AT[key][1]] = v

    ck = a["L0_tok_kernel"]
    put("conv01", ck[0:2].reshape(2 * CIN, D))
    put("conv2", ck[2])
    wide[CIN:, W_AT["conv0"][0]:W_AT["conv0"][1]] = ck[0]
    put("conv12", ck[1:3].reshape(2 * CIN, D))
    qkv = a[p + "Wqkv"]
    put("wq", qkv[0:D][perm].T)
    put("wk", qkv[D:2 * D][perm].T)
    put("wv", qkv[2 * D:].T)
    put("wvp", qkv[2 * D:][perm].T)
    put("wo", a[p + "Wo"].T[perm])
    pos = np.arange(SEG - 1, -1, -1, dtype=f)
    inv = f(1.0) / (f(10000.0) ** (np.arange(0, D, 2, dtype=f) / f(D)))
    ang = (pos[:, None] * inv[None, :]).astype(f)
    put("post", np.concatenate([np.sin(ang), np.cos(ang)], axis=1).T)
    put("ident", np.eye(128))
    put("rwb", a[p + "r_w_bias"].reshape(D)[perm][:, None])
    put("rrb", a[p + "r_r_bias"].reshape(D)[perm][:, None])
    put("gamma", a[p + "ln_gamma"][:, None])
    put("beta", a[p + "ln_beta"][:, None])
    m = "L0_ffn_"

    def halves(t):
        return np.concatenate([t[..., 0::2], t[..., 1::2]], axis=-1)

    put("gate", a[m + "gate_w"])
    put("ws1", halves(a[m + "shared_w1"]))
    put("ws2", np.concatenate([a[m + "shared_w2"], a[m + "shared_b2"][None]]))
    put("iota", np.tile(np.arange(ETILES, dtype=f), (128, 1)))
    part = np.arange(128)
    put("qmask", (part[:, None] % 64 // DH == np.arange(QUADS)).astype(f))
    put("pmask", (part[:, None] // SEG == np.arange(QUADS)).astype(f))
    put("tri16", np.triu(np.ones((E, E), f)))
    put("place", np.arange(ETILES, dtype=f) * 128 + part[:, None])
    act = np.concatenate([a[m + "expert_act"], a[m + "shared_act"][None]])
    rows = np.concatenate([a["L0_tok_bias"], a["L0_tok_kernel_scale"], a[m + "gate_b"], act.reshape(-1),
                           np.arange(E, dtype=f), np.arange(E, dtype=f) * REGION])[None]
    b_wide = np.zeros((128, B_ALL), f)
    for g in range(GROUPS):
        twice = np.tile(perm[g * 64:(g + 1) * 64], 2)
        for key, v in (("wr", a[p + "Wr"][twice].T),):
            lo, hi = B_AT[f"{key}{g}"]
            b_wide[:, lo:hi] = v
    arrays = {
        "x": a["x"].reshape(SEG, WIDTH // 2, 2 * CIN),
        "weights": wide,
        "b_weights": b_wide,
        "rows": rows,
        "w1": halves(a[m + "expert_w1"]).transpose(1, 0, 2),
        "w2": np.concatenate([a[m + "expert_w2"], a[m + "expert_b2"][:, None, :],
                              np.zeros((E, 127 - IH, D), f)], axis=1).transpose(1, 0, 2),
        "b1": halves(np.concatenate([a[m + "expert_b1"], a[m + "shared_b1"][None]])).reshape(1, -1),
    }
    arrays = {k: np.ascontiguousarray(v, dtype=v.dtype) for k, v in arrays.items()}
    nc = bacc.Bacc("TRN2", target_bir_lowering=False, num_devices=1)
    args = [nc.dram_tensor(k, v.shape, mybir.dt.from_np(v.dtype), kind="ExternalInput").ap() for k, v in arrays.items()]
    out = nc.dram_tensor("out", (POSP, SEG, D), F32, kind="ExternalOutput").ap()
    build(nc, *args, out)
    got = run_bass_kernel_spmd(nc, [arrays], core_ids=[0]).results[0]["out"]
    return np.ascontiguousarray(got[:POS].transpose(1, 0, 2))
```
